# Optimizing a Trainium2 kernel written in Bass

```python
import numpy as np
import jax
import jax.numpy as jnp

def _softmax(x, axis=-1):
    return jax.nn.softmax(x, axis=axis)

def _gelu(x):
    return jax.nn.gelu(x, approximate=True)

def _silu(x):
    return jax.nn.silu(x)

def _sigmoid(x):
    return jax.nn.sigmoid(x)

def _layernorm(x, axis=-1, eps=1e-05):
    m = jnp.mean(x, axis=axis, keepdims=True)
    v = jnp.var(x, axis=axis, keepdims=True)
    return (x - m) / jnp.sqrt(v + eps)

def _scatter_add(tgt, idx, src, axis=0):
    return tgt.at[idx].add(src)

def _segment_sum(src, seg, n):
    return jax.ops.segment_sum(src, seg, n)
kernel_name = 'mk_perceiver_d1_seqx_r2_4b3488'

def setup_inputs(seed: int=0):
    np.random.seed(seed)
    _w = jnp.asarray

    def _rec_inputs():
        import jax
        import jax.numpy as jnp
        _rk = jax.random.key(seed)
        x = 7.22e-05 + 1 * jax.random.normal(jax.random.fold_in(_rk, 1), (32, 64, 512), jnp.float32)
        _lenS = 64 - jax.random.randint(jax.random.fold_in(_rk, 7), (32,), 0, max(1, 64 // 4) + 1, jnp.int32)
        _lenS2 = 1601 - jax.random.randint(jax.random.fold_in(_rk, 8), (32,), 0, max(1, 1601 // 4) + 1, jnp.int32)
        _ctx_1024P = jax.random.normal(jax.random.fold_in(_rk, 11), (32, 16, 512), jnp.float32)
        _ctx_1024c = jax.random.dirichlet(jax.random.fold_in(_rk, 511), 0.3 * jnp.ones((16,), jnp.float32), (32, 1601))
        _ctx_1024t = jnp.einsum('bsk,bkd->bsd', _ctx_1024c, _ctx_1024P)
        _ctx_1024t = _ctx_1024t * jax.lax.rsqrt(jnp.mean(jnp.square(_ctx_1024t)) + 1e-12) * 0.953939
        ctx_1024 = -0.000514642 + 1.00011 * (_ctx_1024t + 0.3 * jax.random.normal(jax.random.fold_in(_rk, 611), (32, 1601, 512), jnp.float32))
        return (x, ctx_1024)
    x, ctx_1024 = _rec_inputs()

    def _L0_xattn_setup():
        import jax, jax.numpy as jnp
        import numpy as np
        B, L_ENC, L_DEC, D = (16, 256, 128, 512)
        key = jax.random.key(seed)
        k1, k2, k3, k4, k5, k6 = jax.random.split(key, 6)
        encoder_hc = jax.random.normal(k1, (B, L_ENC, D), dtype=jnp.float32)
        decoder_hq = jax.random.normal(k2, (B, L_DEC, D), dtype=jnp.float32)
        w_sim = jax.random.normal(k3, (3 * D,), dtype=jnp.float32) * 0.02
        b_sim = jax.random.normal(k4, (1,), dtype=jnp.float32) * 0.02
        W_qv = jax.random.normal(k5, (4 * D, D), dtype=jnp.float32) * 0.02
        b_qv = jax.random.normal(k6, (D,), dtype=jnp.float32) * 0.02
        return {'encoder_hc': encoder_hc, 'decoder_hq': decoder_hq, 'w_sim': w_sim, 'b_sim': b_sim, 'W_qv': W_qv, 'b_qv': b_qv}
    _L0_xattn_all = _L0_xattn_setup()
    _L0_xattn_in = {k: v for k, v in _L0_xattn_all.items() if k in ('w_sim', 'b_sim', 'W_qv', 'b_qv')}
    del _L0_xattn_all

    def _L0_attn_setup():
        import jax, jax.numpy as jnp
        import numpy as np
        B, S, D = (4, 1024, 512)
        H = 16
        HS = D // H
        SCALE = HS ** 0.5
        key = jax.random.key(seed)
        ks = jax.random.split(key, 9)
        std = 1.0 / np.sqrt(D)

        def lin(kw, kb, fan_in, fan_out):
            w = jax.random.uniform(kw, (fan_in, fan_out), minval=-std, maxval=std, dtype=jnp.float32)
            b = jax.random.uniform(kb, (fan_out,), minval=-std, maxval=std, dtype=jnp.float32)
            return (w, b)
        Wq, bq = lin(ks[0], ks[1], D, D)
        Wk, bk = lin(ks[2], ks[3], D, D)
        Wv, bv = lin(ks[4], ks[5], D, D)
        Wm, bm = lin(ks[6], ks[7], D, D)
        x = jax.random.normal(ks[8], (B, S, D), dtype=jnp.float32)
        return {'x': x, 'Wq': Wq, 'bq': bq, 'Wk': Wk, 'bk': bk, 'Wv': Wv, 'bv': bv, 'Wm': Wm, 'bm': bm}
    _L0_attn_all = _L0_attn_setup()
    _L0_attn_in = {k: v for k, v in _L0_attn_all.items() if k in ('Wq', 'bq', 'Wk', 'bk', 'Wv', 'bv', 'Wm', 'bm')}
    del _L0_attn_all

    def _L0_ffn_setup():
        import jax, jax.numpy as jnp
        import numpy as np
        B, T, C = (2, 1024, 512)
        E, F = (8, 512)
        FS = 1024
        TOP_K = 2
        key = jax.random.key(seed)
        ks = jax.random.split(key, 6)
        s = lambda *d: 1.0 / np.sqrt(d[-1])
        return {'hidden_tensor': jax.random.normal(ks[0], (B, T, C), jnp.float32), 'w_router': jax.random.normal(ks[1], (E, C), jnp.float32) * s(C), 'w1_stack': jax.random.normal(ks[2], (E, F, C), jnp.float32) * s(C), 'w2_stack': jax.random.normal(ks[3], (E, C, F), jnp.float32) * s(F), 'ws1': jax.random.normal(ks[4], (FS, C), jnp.float32) * s(C), 'ws2': jax.random.normal(ks[5], (C, FS), jnp.float32) * s(FS)}
    _L0_ffn_all = _L0_ffn_setup()
    _L0_ffn_in = {k: v for k, v in _L0_ffn_all.items() if k in ('w_router', 'w1_stack', 'w2_stack', 'ws1', 'ws2')}
    del _L0_ffn_all
    return {'x': x, 'ctx_1024': ctx_1024, 'L0_xattn_w_sim': _L0_xattn_in['w_sim'], 'L0_xattn_b_sim': _L0_xattn_in['b_sim'], 'L0_xattn_W_qv': _L0_xattn_in['W_qv'], 'L0_xattn_b_qv': _L0_xattn_in['b_qv'], 'L0_attn_Wq': _L0_attn_in['Wq'], 'L0_attn_bq': _L0_attn_in['bq'], 'L0_attn_Wk': _L0_attn_in['Wk'], 'L0_attn_bk': _L0_attn_in['bk'], 'L0_attn_Wv': _L0_attn_in['Wv'], 'L0_attn_bv': _L0_attn_in['bv'], 'L0_attn_Wm': _L0_attn_in['Wm'], 'L0_attn_bm': _L0_attn_in['bm'], 'L0_ffn_w_router': _L0_ffn_in['w_router'], 'L0_ffn_w1_stack': _L0_ffn_in['w1_stack'], 'L0_ffn_w2_stack': _L0_ffn_in['w2_stack'], 'L0_ffn_ws1': _L0_ffn_in['ws1'], 'L0_ffn_ws2': _L0_ffn_in['ws2']}

def reference(x, ctx_1024, L0_xattn_w_sim, L0_xattn_b_sim, L0_xattn_W_qv, L0_xattn_b_qv, L0_attn_Wq, L0_attn_bq, L0_attn_Wk, L0_attn_bk, L0_attn_Wv, L0_attn_bv, L0_attn_Wm, L0_attn_bm, L0_ffn_w_router, L0_ffn_w1_stack, L0_ffn_w2_stack, L0_ffn_ws1, L0_ffn_ws2):
    import jax
    import jax.numpy as jnp

    def _L0_xattn_ref(encoder_hc, decoder_hq, w_sim, b_sim, W_qv, b_qv):
        import jax, jax.numpy as jnp
        import numpy as np
        B, L_ENC, L_DEC, D = (16, 256, 128, 512)
        d = encoder_hc.shape[-1]
        w1, w2, w3 = (w_sim[:d], w_sim[d:2 * d], w_sim[2 * d:])
        Sim = (encoder_hc @ w1)[:, :, None] + (decoder_hq @ w2)[:, None, :] + jnp.einsum('bid,bjd->bij', encoder_hc * w3, decoder_hq) + b_sim[0]
        A = jax.nn.softmax(Sim, axis=2)
        hq_hat = jnp.einsum('bij,bjd->bid', A, decoder_hq)
        Batt = jax.nn.softmax(jnp.max(Sim, axis=2), axis=1)
        hc_bar = jnp.einsum('bi,bid->bd', Batt, encoder_hc)[:, None, :]
        hc_hat = jnp.broadcast_to(hc_bar, encoder_hc.shape)
        feats = jnp.concatenate([encoder_hc, hq_hat, encoder_hc * hq_hat, encoder_hc * hc_hat], axis=-1)
        hcq = feats @ W_qv + b_qv
        return hcq

    def _L0_attn_ref(x, Wq, bq, Wk, bk, Wv, bv, Wm, bm):
        import jax, jax.numpy as jnp
        import numpy as np
        B, S, D = (4, 1024, 512)
        H = 16
        HS = D // H
        SCALE = HS ** 0.5
        bs, seq, _ = x.shape

        def heads(w, b):
            return (x @ w + b).reshape(bs, seq, H, HS).transpose(0, 2, 1, 3)
        q = heads(Wq, bq)
        k = heads(Wk, bk)
        v = heads(Wv, bv)
        scores = jnp.einsum('bhqd,bhkd->bhqk', q, k) / SCALE
        causal_mask = jnp.arange(seq)[None, :] > jnp.arange(seq)[:, None]
        scores = jnp.where(causal_mask, jnp.float32(-1000000000000.0), scores)
        probs = jax.nn.softmax(scores, axis=-1)
        attn = jnp.einsum('bhqk,bhkd->bhqd', probs, v)
        attn = attn.transpose(0, 2, 1, 3).reshape(bs, seq, H * HS)
        return attn @ Wm + bm

    def _L0_ffn_ref(hidden_tensor, w_router, w1_stack, w2_stack, ws1, ws2):
        import jax, jax.numpy as jnp
        import numpy as np
        B, T, C = (2, 1024, 512)
        E, F = (8, 512)
        FS = 1024
        TOP_K = 2
        Bb, Tt, Cc = hidden_tensor.shape
        x = hidden_tensor.reshape(-1, Cc)
        t = x.shape[0]
        logits = x @ w_router.T
        probs = jax.nn.softmax(logits, axis=-1)
        expert_weight, expert_idx = jax.lax.top_k(probs, TOP_K)
        expert_weight = expert_weight / jnp.sum(expert_weight, axis=-1, keepdims=True)
        flat_e = expert_idx.reshape(-1)
        order = jnp.argsort(flat_e, stable=True)
        sorted_e = flat_e[order]
        flat_tok = jnp.repeat(jnp.arange(t), TOP_K)
        sorted_tok = flat_tok[order]
        sorted_w = expert_weight.reshape(-1)[order]
        counts = jnp.bincount(sorted_e, length=E)
        offsets = jnp.concatenate([jnp.zeros((1,), counts.dtype), jnp.cumsum(counts)])
        local_pos = jnp.arange(t * TOP_K) - offsets[sorted_e]
        cap = t * TOP_K
        binned = jnp.zeros((E, cap, Cc), x.dtype).at[sorted_e, local_pos].set(x[sorted_tok])
        inter = jnp.einsum('ecd,efd->ecf', binned, w1_stack)
        inter = jnp.square(jax.nn.relu(inter))
        outb = jnp.einsum('ecf,edf->ecd', inter, w2_stack)
        flat_out = outb[sorted_e, local_pos] * sorted_w[:, None]
        moe_out = jnp.zeros((t, Cc), x.dtype).at[sorted_tok].add(flat_out)
        moe_out = moe_out.reshape(Bb, Tt, Cc)
        sh = jnp.square(jax.nn.relu(jnp.einsum('btc,fc->btf', hidden_tensor, ws1)))
        shared_out = jnp.einsum('btf,cf->btc', sh, ws2)
        return shared_out + moe_out
    x = x + _L0_xattn_ref(_layernorm(x, axis=-1), ctx_1024, L0_xattn_w_sim, L0_xattn_b_sim, L0_xattn_W_qv, L0_xattn_b_qv)
    x = x + _L0_attn_ref(_layernorm(x, axis=-1), L0_attn_Wq, L0_attn_bq, L0_attn_Wk, L0_attn_bk, L0_attn_Wv, L0_attn_bv, L0_attn_Wm, L0_attn_bm)
    x = x + _L0_ffn_ref(_layernorm(x, axis=-1), L0_ffn_w_router, L0_ffn_w1_stack, L0_ffn_w2_stack, L0_ffn_ws1, L0_ffn_ws2)
    return x

_drawn_inputs = setup_inputs


def setup_inputs(seed=0):
    import zlib

    import numpy as np

    out = dict(_drawn_inputs(seed))
    spreads = {}
    factors = {'L0_attn_bq': 6.986, 'L0_attn_bk': 8.0}
    for name, (base, spread) in spreads.items():
        noise = np.random.default_rng([zlib.crc32(name.encode()), seed]).standard_normal(out[name].shape)
        drawn = base * np.exp(spread * noise) if base else spread * noise
        out[name] = jnp.asarray(drawn.astype(out[name].dtype))
    for name, factor in factors.items():
        out[name] = (out[name] * factor).astype(out[name].dtype)
    return out
```

```python
from contextlib import ExitStack

import concourse.bass as bass
from concourse import mybir

F32 = mybir.dt.float32
I32 = mybir.dt.int32
ALU = mybir.AluOpType
ACT = mybir.ActivationFunctionType
AX = mybir.AxisListType.X

P = 128
B, S, D = 32, 64, 512
J = 1601
T = B * S // P
KD = D // P
JM = J // P
JT = J - JM * P
JC = JM + 1
JB = [(c * D, min(D, J - c * D)) for c in range(-(-J // D))]
NP = 5
H, HD = 16, 32
HG = P // HD
FS = 1024
KF = FS // P
E, F = 8, 512
GT = (2 * B * S) // P + E
EPS = 1e-5
SCALE = float(HD) ** 0.5
MASKED = -1.0e12
BIG = 3.0e38


def perceiver_layer(nc, x, ctx_n, ctx_t, w1, w23, b_sim, w_qv, b_qv, wq, wk, wv, wm, b_qk, bv, bm,
                    w_router, w1t, w2t, ws1t, ws2t, out):
    moe_in = nc.dram_tensor("moe_in", [GT * P, D], F32).ap()
    moe_out = nc.dram_tensor("moe_out", [GT * P, D], F32).ap()

    with ExitStack() as stack:
        def sb(name, shape, dt=F32):
            return stack.enter_context(nc.sbuf_tensor(name, shape, dt))

        def sem(name):
            return stack.enter_context(nc.semaphore(name))

        X = sb("residual", [P, T, D])
        ident = sb("ident", [P, P])
        ones = sb("ones", [P, P])
        same_batch = sb("same_batch", [P, P])
        earlier = sb("earlier", [P, P])
        causal = sb("causal", [P, S])
        causal_b = sb("causal_b", [P, S])
        row_a = sb("row_a", [P, D])
        row_b = sb("row_b", [P, D])
        w23c = sb("w23c", [P, 2, KD])
        bqkc = sb("bqkc", [P, 2, KD])
        bsim = sb("bsim", [P, 1])
        stats = sb("stats", [P, T, 6])
        mean = sb("mean", [P, T])
        dmean = sb("dmean", [P, T])
        var = sb("var", [P, T])
        rstd = sb("rstd", [P, T])
        nmr = sb("nmr", [P, T])
        small = sb("small", [P, 16])
        rinv = sb("rinv", [P, H])
        rmax = sb("rmax", [P, H])
        rsum = sb("rsum", [P, H])
        cdot, smax, nsmax, smx, erow, rs, bmax, nbmax, bsum, ecol, brec = (
            small[:, i:i + 1] for i in range(11))

        arena = sb("arena", [P, 42496])
        used = [0]

        def at(lo):
            used[0] = lo

        def carve(*dims):
            n = 1
            for d in dims:
                n *= d
            v = arena[:, used[0]:used[0] + n]
            used[0] += n
            if len(dims) == 2:
                v = v.rearrange("p (a b) -> p a b", b=dims[1])
            if len(dims) == 3:
                v = v.rearrange("p (a b c) -> p a b c", b=dims[1], c=dims[2])
            if len(dims) == 4:
                v = v.rearrange("p (a b c d) -> p a b c d", b=dims[1], c=dims[2], d=dims[3])
            return v

        at(0)
        ctxT = [carve(KD, J) for _ in range(2)]
        ctxN = [carve(JC, D) for _ in range(2)]
        w_qv_sb = carve(4 * KD, D)
        expS = carve(J)
        used[0] += -used[0] % 4
        ET = carve(JC, P)
        hc = carve(D)
        hc2 = carve(D)
        qT = carve(KD, P)
        hq = carve(D)
        F1, F2, F3, F4 = (carve(KD, P) for _ in range(4))
        diag = carve(P)
        bexp = carve(S)
        bmat = carve(P)
        end_a = used[0]
        at(0)
        wq_sb, wk_sb, wv_sb, wm_sb = (carve(KD, D) for _ in range(4))
        h1 = carve(D)
        h1T = carve(KD, P)
        qhT = carve(KD, P)
        khT = carve(KD, P)
        Kbd = carve(KD, 2, HG * S)
        Vbd = carve(2, H // 2, 2 * HD)
        sm = carve(H, S)
        prob = carve(H, S)
        PT = carve(H // 2, P)
        attn = carve(H, HD)
        attnT = carve(KD, P)
        w1_sb = carve(E, KD, F)
        ws1_sb = carve(KD, FS)
        ws2_sb = carve(KF, D)
        end_b = used[0]
        at(0)
        w2_lo = carve(E // 2, KD, D)
        h2 = [carve(D) for _ in range(2)]
        h2T = carve(KD, P)
        shT = carve(KF, P)
        wr_sb = carve(KD, P)
        lg = carve(T, E)
        pr = carve(T, E)
        pr2 = carve(T, E)
        eq = carve(T, E)
        cand = carve(T, E)
        oh0 = carve(T, E)
        oh1 = carve(T, E)
        msk = carve(T, E)
        tot = carve(T, E)
        inc = [carve(T, E) for _ in range(2)]
        slotm = carve(T, E)
        iota_m8 = carve(E)
        iota_k = carve(T)
        iota_g = carve(GT)
        cntcmp = carve(E, T)
        gcmp = carve(GT, E)
        v0, v1, e0, e1, wt0, wt1, s0f, s1f, vs = (carve(T) for _ in range(9))
        nt, st0, st1, cnt = (carve(E) for _ in range(4))
        eg_f = carve(GT)
        zero = carve(D)
        xg = [carve(D) for _ in range(2)]
        xgT = carve(KD, P)
        inter = zero
        interT = carve(KD, P)
        yg = [carve(D) for _ in range(2)]
        y0, y1 = xg, yg
        assert used[0] <= 8192 + 9216, used[0]
        assert max(end_a, end_b) <= 42496, (end_a, end_b)
        at(end_b - KD * FS - KF * D)
        w2_hi = carve(E // 2, KD, D)
        slot_i = [sb(f"slot_i{k}", [P, T], I32) for k in range(2)]
        eg_i = sb("eg_i", [P, GT], I32)
        idx = [[sb(f"idx{k}{i}", [P, 1], I32) for i in range(2)] for k in range(2)]

        ps = stack.enter_context(nc.psum_tensor("ps", [P, 8, D], F32))

        def bank(i):
            return ps[:, i, :]

        x_in = [sem(f"x_in{i}") for i in range(4)]
        const_in, wqv_in = sem("const_in"), sem("wqv_in")
        ctxT_in = [[sem(f"ctxT_in{h}{k}") for k in range(KD)] for h in range(2)]
        ctxN_in = [[sem(f"ctxN_in{h}{q}") for q in range(NP)] for h in range(2)]
        attnw_in = [sem(f"attnw_in{i}") for i in range(4)]
        rows_in = sem("rows_in")
        w1_in, ws_in, w2lo_in, w2hi_in, wr_in = (sem(n) for n in ("w1_in", "ws_in", "w2lo_in", "w2hi_in", "wr_in"))
        pool_step, consts_ready = sem("pool_step"), sem("consts_ready")
        pool_go = sem("pool_go")
        dve_step = sem("dve_step")
        act_step = sem("act_step")
        stats_ready = sem("stats_ready")
        var_ready, std_ready, ln_ready = sem("var_ready"), sem("std_ready"), sem("ln_ready")
        hc_ready, c_ready, hc2_ready, xb_ready = (sem(n) for n in ("hc_ready", "c_ready", "hc2_ready", "xb_ready"))
        hcT_done, F1_ready, qT_ready = (sem(n) for n in ("hcT_done", "F1_ready", "qT_ready"))
        sim_done, pv_done = sem("sim_done"), sem("pv_done")
        max_ready, nmax_ready, smx_ready, diag_ready = (sem(n) for n in ("max_ready", "nmax_ready", "smx_ready", "diag_ready"))
        exp_done, et_done, et_act, et_dve = (sem(n) for n in ("exp_done", "et_done", "et_act", "et_dve"))
        rs_ready, hq_ready, hqT_done, F2_ready, F34_ready = (
            sem(n) for n in ("rs_ready", "hq_ready", "hqT_done", "F2_ready", "F34_ready"))
        mxb_done, bmax_ready, nbmax_ready, bexp_ready, brec_ready, bmat_ready, hb_done = (
            sem(n) for n in ("mxb_done", "bmax_ready", "nbmax_ready", "bexp_ready", "brec_ready", "bmat_ready", "hb_done"))
        feats_done, x1_ready = sem("feats_done"), sem("x1_ready")
        kbd_zero, vbd_zero = sem("kbd_zero"), sem("vbd_zero")
        h1_ready, xb2_ready, h1T_done, h1T_ready = (sem(n) for n in ("h1_ready", "xb2_ready", "h1T_done", "h1T_ready"))
        q_done, k_done, v_done, q_ready, k_ready, kbd_ready, vbd_ready = (
            sem(n) for n in ("q_done", "k_done", "v_done", "q_ready", "k_ready", "kbd_ready", "vbd_ready"))
        s_done, smask_ready, smax_ready, ssub_ready, p_ready, ssum_ready, rinv_ready = (
            sem(n) for n in ("s_done", "smask_ready", "smax_ready", "ssub_ready", "p_ready", "ssum_ready", "rinv_ready"))
        pt_done, pt_ready, av_done, attn_norm, attn_ready, attnT_done, attnT_ready, out_done, x2_ready = (
            sem(n) for n in ("pt_done", "pt_ready", "av_done", "attn_norm", "attn_ready", "attnT_done", "attnT_ready",
                             "out_done", "x2_ready"))
        zero_ready, slots_zeroed = sem("zero_ready"), sem("slots_zeroed")
        r_h2_ready, r_h2T_done, r_h2T_ready, lg_done, lg_ready = (
            sem(n) for n in ("r_h2_ready", "r_h2T_done", "r_h2T_ready", "lg_done", "lg_ready"))
        rexp_in, rexp_ready, msk_ready, prefix_done, route_ready, eg_ready = (
            sem(n) for n in ("rexp_in", "rexp_ready", "msk_ready", "prefix_done", "route_ready", "eg_ready"))
        h2_ready, idx_ready, scat = sem("h2_ready"), sem("idx_ready"), [sem(f"scattered{i}") for i in range(2)]
        h2T_done, h2T_ready, sh_done, relu_ready, sh_ready, shared_done, x3_ready = (
            sem(n) for n in ("h2T_done", "h2T_ready", "sh_done", "relu_ready", "sh_ready", "shared_done", "x3_ready"))
        xg_in = [sem(f"xg_in{i}") for i in range(2)]
        xgT_done, xgT_ready, in_done, irelu_ready, inter_ready, iT_done, iT_ready, y_done, y_ready = (
            sem(n) for n in ("xgT_done", "xgT_ready", "in_done", "irelu_ready", "inter_ready", "iT_done", "iT_ready",
                             "y_done", "y_ready"))
        y_out = [sem(f"y_out{i}") for i in range(2)]
        gidx_ready, y01_in = sem("gidx_ready"), [sem(f"y01_in{i}") for i in range(2)]
        mix0_ready, mix_ready, out_sem = sem("mix0_ready"), sem("mix_ready"), sem("out_sem")

        x_v = x.rearrange("(t p) d -> p t d", p=P)
        out_v = out.rearrange("(t p) d -> p t d", p=P)

        block = stack.enter_context(nc.Block())

        @block.sync
        def _(sp):
            for i in range(4):
                n = T // 4
                sp.dma_start(X[:, n * i:n * (i + 1), :], x_v[:, n * i:n * (i + 1), :]).then_inc(x_in[i], 16)
            sp.dma_start(row_a[:, :], w1.partition_broadcast(P)).then_inc(const_in, 16)
            sp.dma_start(row_b[:, :], b_qv.partition_broadcast(P)).then_inc(const_in, 16)
            sp.dma_start(w23c[:, :, :], w23).then_inc(const_in, 16)
            sp.dma_start(bqkc[:, :, :], b_qk).then_inc(const_in, 16)
            sp.dma_start(bsim[:, :], b_sim.partition_broadcast(P)).then_inc(const_in, 16)

            def load_ctx(t, first):
                for k in range(KD):
                    if not first:
                        sp.wait_ge(sim_done, KD * t + (k + 1 - KD))
                    for h in range(2):
                        src = ctx_t[bass.ds(2 * t + h, 1), k].rearrange("o p n -> p (o n)")
                        sp.dma_start(ctxT[h][:, k, :], src).then_inc(ctxT_in[h][k], 16)
                for q in range(NP):
                    if not first:
                        sp.wait_ge(pv_done, NP * t + (q + 1 - NP))
                    for h in range(2):
                        one = ctx_n[bass.ds(2 * t + h, 1)].rearrange("o j d -> (o j) d")
                        if q < NP - 1:
                            n = JM // (NP - 1)
                            main = one[0:JM * P].rearrange("(p c) d -> p c d", c=JM)
                            sp.dma_start(ctxN[h][:, n * q:n * (q + 1), :],
                                         main[:, n * q:n * (q + 1), :]).then_inc(ctxN_in[h][q], 16)
                        else:
                            sp.dma_start(ctxN[h][0:JT, JM, :], one[JM * P:J]).then_inc(ctxN_in[h][q], 16)

            load_ctx(0, True)
            sp.dma_start(w_qv_sb, w_qv.rearrange("(k p) n -> p k n", p=P)).then_inc(wqv_in, 16)
            with sp.Fori(1, T) as t:
                load_ctx(t, False)
            sp.wait_ge(sim_done, KD * (T))
            for i, (dst, src) in enumerate(((wq_sb, wq), (wk_sb, wk), (wv_sb, wv), (wm_sb, wm))):
                sp.dma_start(dst, src.rearrange("(k p) n -> p k n", p=P)).then_inc(attnw_in[i], 16)
            sp.wait_ge(c_ready, T)
            sp.dma_start(row_a[:, :], bv.partition_broadcast(P)).then_inc(rows_in, 16)
            sp.wait_ge(xb_ready, T)
            sp.dma_start(row_b[:, :], bm.partition_broadcast(P)).then_inc(rows_in, 16)
            sp.wait_ge(feats_done, T)
            sp.dma_start(w1_sb, w1t.rearrange("e (k p) n -> p e k n", p=P)).then_inc(w1_in, 16)
            sp.dma_start(ws1_sb, ws1t.rearrange("(k p) n -> p k n", p=P)).then_inc(ws_in, 16)
            sp.dma_start(ws2_sb, ws2t.rearrange("(k p) n -> p k n", p=P)).then_inc(ws_in, 16)
            sp.wait_ge(out_done, T)
            sp.wait_ge(attnT_ready, T)
            sp.dma_start(wr_sb, w_router.rearrange("(k p) n -> p k n", p=P)).then_inc(wr_in, 16)
            sp.wait_ge(zero_ready, 1)
            for q in range(4):
                n = GT // 4
                dst = moe_in.rearrange("(g p) d -> p g d", p=P)[:, n * q:n * (q + 1), :]
                sp.dma_start(dst, zero.unsqueeze(1).to_broadcast([P, n, D])).then_inc(slots_zeroed, 16)
            w2v = w2t.rearrange("e (k p) n -> p e k n", p=P)
            sp.dma_start(w2_lo, w2v[:, 0:E // 2]).then_inc(w2lo_in, 16)
            sp.wait_ge(shared_done, T)
            sp.dma_start(w2_hi, w2v[:, E // 2:E]).then_inc(w2hi_in, 16)
            for i in range(2):
                sp.wait_ge(scat[i], 32 * (T // 2))

            def load_slots(g, i):
                sp.dma_start(xg[i], moe_in[bass.ds(g * P, P), :]).then_inc(xg_in[i], 16)

            def store_slots(g, i):
                sp.wait_ge(y_ready, g + 1)
                sp.dma_start(moe_out[bass.ds(g * P, P), :], yg[i]).then_inc(y_out[i], 16)

            load_slots(0, 0)
            load_slots(1, 1)
            with sp.Fori(0, GT // 2 - 1) as n:
                for i in range(2):
                    sp.wait_ge(xgT_done, 2 * n + i + 1)
                    load_slots(2 * n + i + 2, i)
                    store_slots(2 * n + i, i)
            for i in range(2):
                store_slots(GT - 2 + i, i)
            with sp.Fori(0, T) as t:
                sp.wait_ge(mix_ready, t + 1)
                sp.dma_start(out_v[:, bass.ds(t, 1), :], X[:, bass.ds(t, 1), :]).then_inc(out_sem, 16)
            sp.wait_ge(out_sem, 16 * T)

        @block.gpsimd
        def _(pool):
            nc.gpsimd.memset(ident[:, :], 0.0).then_inc(pool_step, 1)
            nc.gpsimd.memset(earlier[:, :], 1.0).then_inc(pool_step, 1)
            nc.gpsimd.memset(causal[:, :], BIG).then_inc(pool_step, 1)
            nc.gpsimd.memset(causal_b[:, :], BIG).then_inc(pool_step, 1)
            nc.gpsimd.memset(ones[:, :], 1.0).then_inc(consts_ready, 1)
            pool.wait_ge(pool_step, 4)
            nc.gpsimd.affine_select(out=ident[:, :], in_=ident[:, :], compare_op=ALU.not_equal, fill=1.0, base=0,
                                    pattern=[[-1, P]], channel_multiplier=1).then_inc(consts_ready, 1)
            nc.gpsimd.affine_select(out=earlier[:, :], in_=earlier[:, :], compare_op=ALU.is_gt, fill=0.0, base=0,
                                    pattern=[[1, P]], channel_multiplier=-1).then_inc(consts_ready, 1)
            nc.gpsimd.affine_select(out=causal[:, :], in_=causal[:, :], compare_op=ALU.is_ge, fill=MASKED, base=0,
                                    pattern=[[-1, S]], channel_multiplier=1).then_inc(consts_ready, 1)
            nc.gpsimd.affine_select(out=causal_b[:, :], in_=causal_b[:, :], compare_op=ALU.is_ge, fill=MASKED,
                                    base=-S, pattern=[[-1, S]], channel_multiplier=1).then_inc(consts_ready, 1)

            def copies(t, first):
                pool.wait_ge(hc_ready, t + 1)
                if not first:
                    pool.wait_ge(hb_done, t)
                xt = X[:, bass.ds(t, 1), :].rearrange("p o d -> p (o d)")
                nc.gpsimd.tensor_tensor(xt, xt, row_b[:, :], ALU.add).then_inc(xb_ready, 1)
                nc.gpsimd.tensor_copy(hc2, hc).then_inc(hc2_ready, 1)

            pool.wait_ge(const_in, 80)
            copies(0, True)
            with pool.Fori(1, T) as t:
                copies(t, False)
            pool.wait_ge(feats_done, T)
            pool.wait_ge(pv_done, NP * (T))
            nc.gpsimd.memset(Kbd, 0.0).then_inc(kbd_zero, 1)
            nc.gpsimd.memset(Vbd, 0.0).then_inc(vbd_zero, 1)
            pool.wait_ge(rows_in, 32)

            def add_bm(t):
                pool.wait_ge(h1_ready, t + 1)
                xt = X[:, bass.ds(t, 1), :].rearrange("p o d -> p (o d)")
                nc.gpsimd.tensor_tensor(xt, xt, row_b[:, :], ALU.add).then_inc(xb2_ready, 1)

            with pool.Fori(0, T) as t:
                add_bm(t)
            pool.wait_ge(out_done, T)
            pool.wait_ge(attnT_ready, T)
            nc.gpsimd.memset(zero, 0.0).then_inc(zero_ready, 1)
            nc.gpsimd.iota(iota_m8, pattern=[[1, E]], base=-E, channel_multiplier=0,
                           allow_small_or_imprecise_dtypes=True).then_inc(zero_ready, 1)
            nc.gpsimd.iota(iota_k, pattern=[[P, T]], base=0, channel_multiplier=0,
                           allow_small_or_imprecise_dtypes=True).then_inc(zero_ready, 1)
            nc.gpsimd.iota(iota_g, pattern=[[1, GT]], base=0, channel_multiplier=0,
                           allow_small_or_imprecise_dtypes=True).then_inc(zero_ready, 1)
            with pool.Fori(0, T // 2) as n:
                for i in range(2):
                    pool.wait_ge(h2_ready, 2 * n + i + 1)
                    pool.wait_ge(idx_ready, 4 * n + 2 * i + 2)
                    pool.wait_ge(slots_zeroed, 64)
                    pool.sem_inc(pool_go, 1)
                    for k in range(2):
                        nc.gpsimd.indirect_dma_start(
                            moe_in, bass.IndirectOffsetOnAxis(ap=idx[k][i][:, :], axis=0), h2[i], None
                        ).then_inc(scat[i], 16)
            for s in y_out:
                pool.wait_ge(s, 16 * (GT // 2))
            with pool.Fori(0, T // 2) as n:
                for i in range(2):
                    pool.wait_ge(gidx_ready, 4 * n + 2 * i + 2)
                    pool.sem_inc(pool_go, 1)
                    for k, dst in ((0, y0[i]), (1, y1[i])):
                        nc.gpsimd.indirect_dma_start(
                            dst, None, moe_out, bass.IndirectOffsetOnAxis(ap=idx[k][i][:, :], axis=0)
                        ).then_inc(y01_in[i], 16)

        @block.scalar
        def _(act):
            def copy(o, i):
                return nc.scalar.activation(o, i, ACT.Copy)

            def sqrt_of_var(s):
                act.wait_ge(var_ready, s + 1)
                nc.scalar.activation(var[:, :], var[:, :], ACT.Sqrt).then_inc(std_ready, 1)

            def exp_scores(t, first):
                act.wait_ge(nmax_ready, t + 1)
                if not first:
                    act.wait_ge(et_done, 4 * t)
                    act.wait_ge(rs_ready, t)
                nc.scalar.activation(expS, ps[:, 0:4, :].rearrange("p a b -> p (a b)")[:, 0:J], ACT.Exp,
                                     bias=nsmax, accum_out=erow).then_inc(exp_done, 1)

            def after_scores(t, first):
                if not first:
                    act.wait_ge(feats_done, t)
                act.wait_ge(hcT_done, t + 1)
                copy(F1.rearrange("p a b -> p (a b)"), bank(4)).then_inc(F1_ready, 1)
                act.wait_ge(nbmax_ready, t + 1)
                if not first:
                    act.wait_ge(bmat_ready, t)
                for h in range(2):
                    r = slice(S * h, S * (h + 1))
                    nc.scalar.activation(bexp[r, :],
                                         bank(6)[r, S * h:S * (h + 1)], ACT.Exp, bias=nbmax[r, :],
                                         accum_out=bsum[r, :]).then_inc(bexp_ready, 1)
                nc.scalar.activation(ecol, smx, ACT.Exp, bias=nbmax).then_inc(bexp_ready, 1)
                for g in (0, 2):
                    act.wait_ge(et_done, 4 * t + g + 1)
                    if not first and g == 0:
                        act.wait_ge(pv_done, NP * (t))
                    copy(ET[:, 4 * g:4 * g + 4, :].rearrange("p a b -> p (a b)"), bank(g)).then_inc(et_act, 1)
                act.wait_ge(hqT_done, t + 1)
                copy(F2.rearrange("p a b -> p (a b)"), bank(5)).then_inc(F2_ready, 1)

            sqrt_of_var(0)
            exp_scores(0, True)
            after_scores(0, True)
            with act.Fori(1, T) as t:
                exp_scores(t, False)
                after_scores(t, False)
            sqrt_of_var(1)

            def h1T_copy(t, first):
                act.wait_ge(h1T_done, t + 1)
                if not first:
                    act.wait_ge(v_done, t)
                copy(h1T.rearrange("p a b -> p (a b)"), bank(0)).then_inc(h1T_ready, 1)

            def attnT_copy(t):
                act.wait_ge(attnT_done, t + 1)
                copy(attnT.rearrange("p a b -> p (a b)"), bank(2)).then_inc(attnT_ready, 1)

            def keys(t, first):
                act.wait_ge(k_ready, t + 1)
                if not first:
                    act.wait_ge(s_done, t)
                for h in range(HG):
                    r = slice(HD * h, HD * (h + 1))
                    copy(Kbd[r, :, :, S * h:S * (h + 1)],
                         khT[r].rearrange("p m (b j) -> p m b j", b=2)).then_inc(kbd_ready, 1)

            def pt_copy(t, first):
                for g in range(2):
                    act.wait_ge(pt_done, 2 * t + g + 1)
                    if not first and g == 0:
                        act.wait_ge(av_done, t)
                    copy(PT[:, 4 * g:4 * g + 4, :].rearrange("p a b -> p (a b)"), bank(6 + g)).then_inc(pt_ready, 1)

            def exp_probs(t, first):
                act.wait_ge(ssub_ready, t + 1)
                if not first:
                    act.wait_ge(pt_done, 2 * t)
                    act.wait_ge(ssum_ready, t)
                nc.scalar.activation(prob.rearrange("p a b -> p (a b)"), sm.rearrange("p a b -> p (a b)"),
                                     ACT.Exp).then_inc(p_ready, 1)

            def stage_b(t, now, last, last2, first=False, second=False):
                if last2:
                    attnT_copy(t - 2)
                if now:
                    h1T_copy(t, first)
                    keys(t, first)
                if last:
                    pt_copy(t - 1, second)
                if now:
                    exp_probs(t, first)

            act.wait_ge(kbd_zero, 1)
            stage_b(0, True, False, False, first=True)
            stage_b(1, True, True, False, second=True)
            with act.Fori(2, T) as t:
                stage_b(t, True, True, True)
            stage_b(T, False, True, True)
            stage_b(T + 1, False, False, True)
            sqrt_of_var(2)

            act.wait_ge(ln_ready, 3)

            def router(t, first):
                act.wait_ge(r_h2T_done, t + 1)
                if not first:
                    act.wait_ge(lg_done, t)
                copy(h2T.rearrange("p a b -> p (a b)"), bank(0)).then_inc(r_h2T_ready, 1)

            router(0, True)
            with act.Fori(1, T) as t:
                router(t, False)
            act.wait_ge(rexp_in, 1)
            nc.scalar.activation(pr.rearrange("p a b -> p (a b)"), pr2.rearrange("p a b -> p (a b)"),
                                 ACT.Exp).then_inc(rexp_ready, 1)

            def shared(t, first):
                act.wait_ge(h2T_done, t + 1)
                if not first:
                    act.wait_ge(sh_done, 2 * t)
                copy(h2T.rearrange("p a b -> p (a b)"), bank(0)).then_inc(h2T_ready, 1)
                for g in range(2):
                    act.wait_ge(sh_done, 2 * t + g + 1)
                    if not first and g == 0:
                        act.wait_ge(shared_done, t)
                    nc.scalar.activation(shT[:, 4 * g:4 * g + 4, :].rearrange("p a b -> p (a b)"), bank(1 + g),
                                         ACT.Relu).then_inc(relu_ready, 1)

            shared(0, True)
            with act.Fori(1, T) as t:
                shared(t, False)

            def experts(g, now, last, first=False):
                if now:
                    act.wait_ge(xgT_done, g + 1)
                    if not first:
                        act.wait_ge(in_done, g)
                    copy(xgT.rearrange("p a b -> p (a b)"), bank(0)).then_inc(xgT_ready, 1)
                if last:
                    act.wait_ge(iT_done, g)
                    copy(interT.rearrange("p a b -> p (a b)"), bank(1)).then_inc(iT_ready, 1)
                if now:
                    act.wait_ge(in_done, g + 1)
                    nc.scalar.activation(inter, bank(2), ACT.Relu).then_inc(irelu_ready, 1)

            experts(0, True, False, True)
            with act.Fori(1, GT) as g:
                experts(g, True, True)
            experts(GT, False, True)

        @block.vector
        def _(dve):
            v = nc.vector
            chain = [0]

            def step(ins):
                chain[0] += 1
                ins.then_inc(dve_step, 1)
                dve.wait_ge(dve_step, chain[0])

            def finish_norm(s):
                dve.wait_ge(stats_ready, T * (s + 1))
                step(v.tensor_tensor(mean[:, :], stats[:, :, 1], stats[:, :, 4], ALU.add))
                step(v.tensor_scalar(mean[:, :], mean[:, :], 0.5, None, ALU.mult))
                step(v.tensor_tensor(dmean[:, :], stats[:, :, 1], stats[:, :, 4], ALU.subtract))
                step(v.tensor_tensor(dmean[:, :], dmean[:, :], dmean[:, :], ALU.mult))
                step(v.tensor_tensor(var[:, :], stats[:, :, 2], stats[:, :, 5], ALU.add))
                step(v.scalar_tensor_tensor(var[:, :], dmean[:, :], D / 4.0, var[:, :], ALU.mult, ALU.add))
                v.tensor_scalar(var[:, :], var[:, :], 1.0 / D, EPS, ALU.mult, ALU.add).then_inc(var_ready, 1)
                dve.wait_ge(std_ready, s + 1)
                step(v.reciprocal(rstd[:, :], var[:, :]))
                v.scalar_tensor_tensor(nmr[:, :], mean[:, :], -1.0, rstd[:, :], ALU.mult, ALU.mult
                                       ).then_inc(ln_ready, 1)
                dve.wait_ge(ln_ready, s + 1)

            def x_tile(t):
                return X[:, bass.ds(t, 1), :].rearrange("p o d -> p (o d)")

            def normed(o, t):
                return v.tensor_scalar(o, x_tile(t), rstd[:, bass.ds(t, 1)], nmr[:, bass.ds(t, 1)], ALU.mult, ALU.add)

            def row_stats(t):
                return v.bn_stats(stats[:, bass.ds(t, 1), :].rearrange("p o s -> p (o s)"), x_tile(t))

            for i in range(4):
                dve.wait_ge(x_in[i], 16)
            with dve.Fori(0, T) as t:
                row_stats(t).then_inc(stats_ready, 1)
            finish_norm(0)
            dve.wait_ge(const_in, 80)
            dve.wait_ge(consts_ready, 5)

            step(v.memset(same_batch[:, :], 0.0))
            for h in range(2):
                r = slice(S * h, S * (h + 1))
                step(v.memset(same_batch[r, r], 1.0))
            step(v.tensor_copy(causal[S:P, :], causal_b[S:P, :]))

            def norm_a(t, first):
                if not first:
                    dve.wait_ge(hcT_done, t)
                    dve.wait_ge(hc2_ready, t)
                normed(hc, t).then_inc(hc_ready, 1)
                if not first:
                    dve.wait_ge(et_done, 4 * t)
                dve.wait_ge(hc_ready, t + 1)
                v.scalar_tensor_tensor(expS[:, 0:D], hc, 1.0, row_a[:, :], ALU.mult, ALU.mult,
                                       accum_out=cdot).then_inc(c_ready, 1)

            def queries(t, first):
                dve.wait_ge(hcT_done, t + 1)
                if not first:
                    dve.wait_ge(sim_done, KD * (t))
                for k in range(KD):
                    v.tensor_scalar(qT[:, k, :], bank(4)[:, P * k:P * (k + 1)], w23c[:, 1, k:k + 1],
                                    w23c[:, 0, k:k + 1], ALU.mult, ALU.add).then_inc(qT_ready, 1)

            def maxima(t, first):
                dve.wait_ge(sim_done, KD * (t + 1))
                if not first:
                    dve.wait_ge(exp_done, t)
                    dve.wait_ge(bexp_ready, 3 * t)
                    dve.wait_ge(mxb_done, t)
                v.reduce_max(smax, ps[:, 0:4, :].rearrange("p a b -> p (a b)")[:, 0:J], AX).then_inc(max_ready, 1)
                dve.wait_ge(max_ready, t + 1)
                v.tensor_scalar(nsmax, smax, -1.0, None, ALU.mult).then_inc(nmax_ready, 1)
                dve.wait_ge(c_ready, t + 1)
                v.scalar_tensor_tensor(smx, smax, cdot, bsim[:, :], ALU.add, ALU.add).then_inc(smx_ready, 1)
                dve.wait_ge(smx_ready, t + 1)
                v.tensor_scalar(diag, ident[:, :], smx, None, ALU.mult).then_inc(diag_ready, 1)

            def batch_weights(t, first):
                dve.wait_ge(mxb_done, t + 1)
                if not first:
                    dve.wait_ge(bexp_ready, 3 * t)
                for h in range(2):
                    r = slice(S * h, S * (h + 1))
                    v.reduce_max(bmax[r, :], bank(6)[r, S * h:S * (h + 1)], AX).then_inc(bmax_ready, 1)
                dve.wait_ge(bmax_ready, 2 * (t + 1))
                v.tensor_scalar(nbmax, bmax, -1.0, None, ALU.mult).then_inc(nbmax_ready, 1)
                dve.wait_ge(bexp_ready, 3 * (t + 1))
                if not first:
                    dve.wait_ge(hb_done, t)
                v.reciprocal(brec, bsum).then_inc(brec_ready, 1)
                dve.wait_ge(brec_ready, t + 1)
                v.tensor_scalar(bmat, same_batch[:, :], ecol, brec, ALU.mult, ALU.mult).then_inc(bmat_ready, 1)

            def exp_copies(t, first):
                for g in (1, 3):
                    dve.wait_ge(et_done, 4 * t + g + 1)
                    if not first and g == 1:
                        dve.wait_ge(pv_done, NP * (t))
                    if g == 1:
                        v.tensor_copy(ET[:, 4:8, :].rearrange("p a b -> p (a b)"), bank(1)).then_inc(et_dve, 1)
                    else:
                        v.tensor_copy(ET[0:JT, JM, :], bank(3)[0:JT, 0:P]).then_inc(et_dve, 1)

            def attended(t, first):
                dve.wait_ge(exp_done, t + 1)
                v.reciprocal(rs, erow).then_inc(rs_ready, 1)
                dve.wait_ge(pv_done, NP * (t + 1))
                dve.wait_ge(rs_ready, t + 1)
                if not first:
                    dve.wait_ge(hqT_done, t)
                v.tensor_scalar(hq, bank(7), rs, None, ALU.mult).then_inc(hq_ready, 1)

            def features(t, first):
                dve.wait_ge(F1_ready, t + 1)
                if not first:
                    dve.wait_ge(feats_done, t)
                dve.wait_ge(hb_done, t + 1)
                v.tensor_tensor(F4.rearrange("p a b -> p (a b)"), F1.rearrange("p a b -> p (a b)"), bank(6),
                                ALU.mult).then_inc(F34_ready, 1)
                dve.wait_ge(F2_ready, t + 1)
                v.tensor_tensor(F3.rearrange("p a b -> p (a b)"), F1.rearrange("p a b -> p (a b)"),
                                F2.rearrange("p a b -> p (a b)"), ALU.mult).then_inc(F34_ready, 1)

            def residual_a(t):
                dve.wait_ge(feats_done, t + 1)
                dve.wait_ge(xb_ready, t + 1)
                v.tensor_tensor(x_tile(t), x_tile(t), bank(5), ALU.add).then_inc(x1_ready, 1)
                dve.wait_ge(x1_ready, t + 1)
                row_stats(t).then_inc(stats_ready, 1)

            norm_a(0, True)
            queries(0, True)
            maxima(0, True)

            def stage_a(t, first):
                batch_weights(t - 1, first)
                exp_copies(t - 1, first)
                norm_a(t, False)
                attended(t - 1, first)
                queries(t, False)
                features(t - 1, first)
                maxima(t, False)
                residual_a(t - 1)

            stage_a(1, True)
            with dve.Fori(2, T) as t:
                stage_a(t, False)
            batch_weights(T - 1, False)
            exp_copies(T - 1, False)
            attended(T - 1, False)
            features(T - 1, False)
            residual_a(T - 1)
            finish_norm(1)

            dve.wait_ge(rows_in, 32)
            dve.wait_ge(vbd_zero, 1)

            def norm_b(t, first=False):
                if not first:
                    dve.wait_ge(h1T_done, t)
                normed(h1, t).then_inc(h1_ready, 1)

            def projections(t, first):
                dve.wait_ge(q_done, t + 1)
                if not first:
                    dve.wait_ge(s_done, t)
                v.tensor_tensor(qhT, bank(1).rearrange("p (m n) -> p m n", m=KD),
                                bqkc[:, 0, :].unsqueeze(2).to_broadcast([P, KD, P]), ALU.add).then_inc(q_ready, 1)
                dve.wait_ge(k_done, t + 1)
                if not first:
                    dve.wait_ge(kbd_ready, HG * t)
                v.tensor_tensor(khT, bank(2).rearrange("p (m n) -> p m n", m=KD),
                                bqkc[:, 1, :].unsqueeze(2).to_broadcast([P, KD, P]), ALU.add).then_inc(k_ready, 1)

            def values(t, first):
                dve.wait_ge(v_done, t + 1)
                if not first:
                    dve.wait_ge(av_done, t)
                for b in range(2):
                    rb = slice(S * b, S * (b + 1))
                    for e in range(2):
                        src = bank(3)[rb].rearrange("p (g e d) -> p g e d", e=2, d=HD)[:, :, e, :]
                        bias = row_a[rb].rearrange("p (g e d) -> p g e d", e=2, d=HD)[:, :, e, :]
                        v.tensor_tensor(Vbd[S * e:S * (e + 1), b, :, HD * e:HD * (e + 1)], src, bias,
                                        ALU.add).then_inc(vbd_ready, 1)

            def masked_scores(t, first):
                dve.wait_ge(s_done, t + 1)
                if not first:
                    dve.wait_ge(p_ready, t)
                v.scalar_tensor_tensor(sm, ps[:, 4:6, :].rearrange("p a (h j) -> p (a h) j", j=S), 1.0 / SCALE,
                                       causal[:, :].unsqueeze(1).to_broadcast([P, H, S]), ALU.mult, ALU.min
                                       ).then_inc(smask_ready, 1)
                dve.wait_ge(smask_ready, t + 1)
                v.tensor_reduce(rmax[:, :], sm, AX, ALU.max).then_inc(smax_ready, 1)
                dve.wait_ge(smax_ready, t + 1)
                v.tensor_tensor(sm, sm, rmax[:, :].unsqueeze(2).to_broadcast([P, H, S]), ALU.subtract
                                ).then_inc(ssub_ready, 1)

            def prob_sums(t):
                dve.wait_ge(p_ready, t + 1)
                v.tensor_reduce(rsum[:, :], prob, AX, ALU.add).then_inc(ssum_ready, 1)
                dve.wait_ge(ssum_ready, t + 1)
                v.reciprocal(rinv[:, :], rsum[:, :]).then_inc(rinv_ready, 1)

            def attended_b(t, first):
                dve.wait_ge(av_done, t + 1)
                dve.wait_ge(rinv_ready, t + 1)
                if not first:
                    dve.wait_ge(attnT_done, t)
                v.tensor_tensor(attn, bank(6).rearrange("p (h d) -> p h d", d=HD),
                                rinv[:, :].unsqueeze(2).to_broadcast([P, H, HD]), ALU.mult).then_inc(attn_ready, 1)

            def residual_b(t):
                dve.wait_ge(out_done, t + 1)
                dve.wait_ge(xb2_ready, t + 1)
                v.tensor_tensor(x_tile(t), x_tile(t), bank(7), ALU.add).then_inc(x2_ready, 1)
                dve.wait_ge(x2_ready, t + 1)
                row_stats(t).then_inc(stats_ready, 1)

            def stage_b(t, now, last, last2, first=False, second=False, more=True):
                if now:
                    projections(t, first)
                if last2:
                    residual_b(t - 2)
                if now:
                    values(t, first)
                    if more:
                        norm_b(t + 1)
                    masked_scores(t, first)
                if last:
                    attended_b(t - 1, second)
                if now:
                    prob_sums(t)

            norm_b(0, True)
            stage_b(0, True, False, False, first=True)
            stage_b(1, True, True, False, second=True)
            with dve.Fori(2, T - 1) as t:
                stage_b(t, True, True, True)
            stage_b(T - 1, True, True, True, more=False)
            stage_b(T, False, True, True)
            stage_b(T + 1, False, False, True)
            finish_norm(2)

            dve.wait_ge(zero_ready, 4)

            def router(t, first):
                if not first:
                    dve.wait_ge(r_h2T_done, t)
                normed(h2[0], t).then_inc(r_h2_ready, 1)
                dve.wait_ge(lg_done, t + 1)
                v.tensor_copy(lg[:, bass.ds(t, 1), :].rearrange("p o e -> p (o e)"), bank(3)[:, 0:E]
                              ).then_inc(lg_ready, 1)

            router(0, True)
            with dve.Fori(1, T) as t:
                router(t, False)
            dve.wait_ge(lg_ready, T)

            def over_e(a):
                return a.unsqueeze(2).to_broadcast([P, T, E])

            def over_t(a):
                return a.unsqueeze(1).to_broadcast([P, T, E])

            step(v.tensor_reduce(v0, lg, AX, ALU.max))
            v.tensor_tensor(pr2, lg, over_e(v0), ALU.subtract).then_inc(rexp_in, 1)
            dve.wait_ge(rexp_ready, 1)
            step(v.tensor_reduce(vs, pr, AX, ALU.add))
            step(v.reciprocal(vs, vs))
            step(v.tensor_tensor(pr, pr, over_e(vs), ALU.mult))
            for probs, val, arg, onehot in ((pr, v0, e0, oh0), (pr2, v1, e1, oh1)):
                if probs is pr2:
                    step(v.scalar_tensor_tensor(pr2, oh0, -2.0, pr, ALU.mult, ALU.add))
                step(v.tensor_reduce(val, probs, AX, ALU.max))
                step(v.tensor_tensor(eq, probs, over_e(val), ALU.is_equal))
                step(v.tensor_tensor(cand, eq, over_t(iota_m8), ALU.mult))
                step(v.tensor_reduce(arg, cand, AX, ALU.min))
                step(v.tensor_tensor(onehot, over_t(iota_m8), over_e(arg), ALU.is_equal))
            step(v.tensor_tensor(vs, v0, v1, ALU.add))
            step(v.reciprocal(vs, vs))
            step(v.tensor_tensor(wt0, v0, vs, ALU.mult))
            step(v.tensor_tensor(wt1, v1, vs, ALU.mult))
            v.tensor_tensor(msk, oh0, oh1, ALU.add).then_inc(msk_ready, 1)
            dve.wait_ge(prefix_done, 1)
            step(v.tensor_copy(tot.rearrange("p a b -> p (a b)"), bank(5)[:, 0:T * E]))
            src, d = tot, 1
            k = 0
            while d < T:
                dst = inc[k % 2]
                step(v.tensor_copy(dst[:, 0:d, :], src[:, 0:d, :]))
                step(v.tensor_tensor(dst[:, d:T, :], src[:, d:T, :], src[:, 0:T - d, :], ALU.add))
                src, d, k = dst, 2 * d, k + 1
            step(v.tensor_copy(cnt, src[:, T - 1, :]))
            step(v.tensor_tensor(cntcmp, cnt.unsqueeze(2).to_broadcast([P, E, T]),
                                 iota_k.unsqueeze(1).to_broadcast([P, E, T]), ALU.is_gt))
            step(v.tensor_reduce(nt, cntcmp, AX, ALU.add))
            a, b, d = nt, st0, 1
            while d < E:
                step(v.tensor_copy(b[:, 0:d], a[:, 0:d]))
                step(v.tensor_tensor(b[:, d:E], a[:, d:E], a[:, 0:E - d], ALU.add))
                a, b, d = b, (st1 if b is st0 else st0), 2 * d
            ends, first_tile = a, b
            step(v.tensor_tensor(first_tile, ends, nt, ALU.subtract))
            step(v.tensor_tensor(slotm, src, tot, ALU.subtract))
            step(v.tensor_tensor(slotm, slotm, bank(4)[:, 0:T * E].rearrange("p (t e) -> p t e", e=E), ALU.add))
            step(v.scalar_tensor_tensor(slotm, over_t(first_tile), float(P), slotm, ALU.mult, ALU.add))
            for onehot, sf, si in ((oh0, s0f, slot_i[0]), (oh1, s1f, slot_i[1])):
                step(v.tensor_tensor(cand, slotm, onehot, ALU.mult))
                step(v.tensor_reduce(sf, cand, AX, ALU.add))
                step(v.tensor_copy(si[:, :], sf))
            step(v.tensor_tensor(gcmp, ends.unsqueeze(1).to_broadcast([P, GT, E]),
                                 iota_g.unsqueeze(2).to_broadcast([P, GT, E]), ALU.is_le))
            step(v.tensor_reduce(eg_f, gcmp, AX, ALU.add))
            step(v.tensor_scalar(eg_f, eg_f, float(E - 1), None, ALU.min))
            v.tensor_copy(eg_i[:, :], eg_f).then_inc(eg_ready, 1)

            def norm_c(n, i, first):
                t = 2 * n + i
                if not first:
                    dve.wait_ge(scat[i], 32 * n)
                    dve.wait_ge(h2T_done, t - 1)
                normed(h2[i], t).then_inc(h2_ready, 1)
                for k in range(2):
                    v.tensor_copy(idx[k][i][:, :], slot_i[k][:, bass.ds(t, 1)]).then_inc(idx_ready, 1)

            def squares(t):
                for g in range(2):
                    dve.wait_ge(relu_ready, 2 * t + g + 1)
                    part = shT[:, 4 * g:4 * g + 4, :].rearrange("p a b -> p (a b)")
                    v.tensor_tensor(part, part, part, ALU.mult).then_inc(sh_ready, 1)

            def residual_c(t):
                dve.wait_ge(shared_done, t + 1)
                v.tensor_tensor(x_tile(t), x_tile(t), bank(3), ALU.add).then_inc(x3_ready, 1)

            norm_c(0, 0, True)
            norm_c(0, 1, True)
            with dve.Fori(0, T // 2 - 1) as n:
                for i in range(2):
                    squares(2 * n + i)
                    residual_c(2 * n + i)
                    norm_c(n + 1, i, False)
            for i in range(2):
                squares(T - 2 + i)
                residual_c(T - 2 + i)

            def experts(g, i, now, last):
                if now:
                    dve.wait_ge(irelu_ready, g + 1)
                    v.tensor_tensor(inter, inter, inter, ALU.mult).then_inc(inter_ready, 1)
                if last:
                    dve.wait_ge(y_done, g)
                    v.tensor_copy(yg[1 - i], bank(3)).then_inc(y_ready, 1)

            def store_of(g, i, n):
                dve.wait_ge(y_out[1 - i], n)

            experts(0, 0, True, False)
            experts(1, 1, True, True)
            experts(2, 0, True, True)
            with dve.Fori(1, GT // 2 - 1) as n:
                dve.wait_ge(y_out[0], 16 * n)
                experts(2 * n + 1, 1, True, True)
                dve.wait_ge(y_out[1], 16 * n)
                experts(2 * n + 2, 0, True, True)
            dve.wait_ge(y_out[0], 16 * (GT // 2 - 1))
            experts(GT - 1, 1, True, True)
            dve.wait_ge(y_out[1], 16 * (GT // 2 - 1))
            experts(GT, 0, False, True)

            def gather_index(n, i):
                t = 2 * n + i
                for k in range(2):
                    v.tensor_copy(idx[k][i][:, :], slot_i[k][:, bass.ds(t, 1)]).then_inc(gidx_ready, 1)

            def mix(n, i):
                t = 2 * n + i
                dve.wait_ge(y01_in[i], 32 * (n + 1))
                dve.wait_ge(x3_ready, T)
                v.scalar_tensor_tensor(x_tile(t), y0[i], wt0[:, bass.ds(t, 1)], x_tile(t), ALU.mult, ALU.add
                                       ).then_inc(mix0_ready, 1)
                dve.wait_ge(mix0_ready, t + 1)
                v.scalar_tensor_tensor(x_tile(t), y1[i], wt1[:, bass.ds(t, 1)], x_tile(t), ALU.mult, ALU.add
                                       ).then_inc(mix_ready, 1)

            dve.wait_ge(scat[0], 32 * (T // 2))
            dve.wait_ge(scat[1], 32 * (T // 2))
            gather_index(0, 0)
            gather_index(0, 1)
            with dve.Fori(0, T // 2 - 1) as n:
                for i in range(2):
                    mix(n, i)
                    gather_index(n + 1, i)
            for i in range(2):
                mix(T // 2 - 1, i)

        @block.tensor
        def _(pe):
            mm = nc.tensor.matmul

            def transposes(dst, src):
                for k in range(KD):
                    last = nc.tensor.transpose(dst[:, P * k:P * (k + 1)], src[:, P * k:P * (k + 1)], ident[:, :])
                return last

            def rows(dst, lhsT, rhs):
                n = lhsT.shape[1]
                for k in range(n):
                    last = mm(dst, lhsT[:, k, :], rhs[:, k, :], start=(k == 0), stop=(k == n - 1))
                return last

            def normed_T(t, first):
                pe.wait_ge(hc_ready, t + 1)
                if not first:
                    pe.wait_ge(F1_ready, t)
                transposes(bank(4), hc).then_inc(hcT_done, 1)

            def batch_means(t):
                pe.wait_ge(bmat_ready, t + 1)
                pe.wait_ge(hc2_ready, t + 1)
                for k in range(KD):
                    last = mm(bank(6)[:, P * k:P * (k + 1)], hc2[:, P * k:P * (k + 1)], bmat, start=True, stop=True)
                last.then_inc(hb_done, 1)

            def attended_T(t, first):
                pe.wait_ge(hq_ready, t + 1)
                if not first:
                    pe.wait_ge(x1_ready, t)
                transposes(bank(5), hq).then_inc(hqT_done, 1)

            def similarities(t, first):
                pe.wait_ge(qT_ready, KD * (t + 1))
                if not first:
                    pe.wait_ge(et_act, 2 * t)
                    pe.wait_ge(et_dve, 2 * t)
                for k in range(KD):
                    for h in range(2):
                        pe.wait_ge(ctxT_in[h][k], 16 * (t + 1))
                    for n, (lo, w) in enumerate(JB):
                        for h in range(2):
                            last = mm(bank(n)[S * h:S * (h + 1), 0:w], qT[:, k, S * h:S * (h + 1)],
                                      ctxT[h][:, k, lo:lo + w], start=(k == 0), stop=(k == KD - 1))
                    last.then_inc(sim_done, 1)

            def features(t):
                pe.wait_ge(F1_ready, t + 1)
                pe.wait_ge(F2_ready, t + 1)
                pe.wait_ge(F34_ready, 2 * (t + 1))
                for f, block_T in enumerate((F1, F2, F3, F4)):
                    for k in range(KD):
                        last = mm(bank(5), block_T[:, k, :], w_qv_sb[:, KD * f + k, :],
                                  start=(f + k == 0), stop=(f == 3 and k == KD - 1))
                last.then_inc(feats_done, 1)

            def spread_max(t):
                pe.wait_ge(diag_ready, t + 1)
                mm(bank(6)[:, 0:P], ones[:, :], diag, start=True, stop=True).then_inc(mxb_done, 1)

            def exp_T(t):
                pe.wait_ge(exp_done, t + 1)
                for c in range(JC):
                    w = P if c < JM else JT
                    last = nc.tensor.transpose(bank(c // 4)[0:w, P * (c % 4):P * (c % 4 + 1)],
                                               expS[:, P * c:P * c + w], ident[:, :])
                    if c % 4 == 3 or c == JC - 1:
                        last.then_inc(et_done, 1)

            def attend(t, first):
                if not first:
                    pe.wait_ge(hq_ready, t)
                for c in range(JC):
                    w = P if c < JM else JT
                    if c == 0:
                        pe.wait_ge(et_act, 2 * t + 1)
                    if c == 4:
                        pe.wait_ge(et_dve, 2 * t + 1)
                    if c == 8:
                        pe.wait_ge(et_act, 2 * t + 2)
                    if c == 12:
                        pe.wait_ge(et_dve, 2 * t + 2)
                    if c % 3 == 0:
                        for h in range(2):
                            pe.wait_ge(ctxN_in[h][c // 3], 16 * (t + 1))
                    for h in range(2):
                        last = mm(bank(7)[S * h:S * (h + 1), :], ET[0:w, c, S * h:S * (h + 1)], ctxN[h][0:w, c, :],
                                  start=(c == 0), stop=(c == JC - 1))
                    if c % 3 == 2 or c == JC - 1:
                        last.then_inc(pv_done, 1)

            pe.wait_ge(consts_ready, 5)

            def stage_a(t, now, last, first=False, second=False):
                if now:
                    normed_T(t, first)
                if last:
                    batch_means(t - 1)
                    attended_T(t - 1, second)
                if now:
                    similarities(t, first)
                if last:
                    features(t - 1)
                if now:
                    spread_max(t)
                    exp_T(t)
                    attend(t, first)

            stage_a(0, True, False, first=True)
            pe.wait_ge(wqv_in, 16)
            stage_a(1, True, True, second=True)
            with pe.Fori(2, T) as t:
                stage_a(t, True, True)
            stage_a(T, False, True)

            def stage_b(t, now, last, last2, first=False, second=False, third=False):
                if last2:
                    pe.wait_ge(attn_ready, t - 1)
                    pe.wait_ge(k_ready, t if now else T)
                    transposes(bank(2), attn.rearrange("p h d -> p (h d)")).then_inc(attnT_done, 1)
                if now:
                    pe.wait_ge(h1_ready, t + 1)
                    if not first:
                        pe.wait_ge(h1T_ready, t)
                    transposes(bank(0), h1).then_inc(h1T_done, 1)
                    pe.wait_ge(h1T_ready, t + 1)
                    if not first:
                        pe.wait_ge(q_ready, t)
                    for m in range(KD):
                        for k in range(KD):
                            mq = mm(bank(1)[:, P * m:P * (m + 1)], wq_sb[:, k, P * m:P * (m + 1)], h1T[:, k, :],
                                    start=(k == 0), stop=(k == KD - 1))
                    mq.then_inc(q_done, 1)
                if last2:
                    pe.wait_ge(attnT_ready, t - 1)
                    pe.wait_ge(pt_ready, 2 * (t - 1))
                    rows(bank(7), attnT, wm_sb).then_inc(out_done, 1)
                if now:
                    if not first:
                        pe.wait_ge(k_ready, t)
                    for m in range(KD):
                        for k in range(KD):
                            mk = mm(bank(2)[:, P * m:P * (m + 1)], wk_sb[:, k, P * m:P * (m + 1)], h1T[:, k, :],
                                    start=(k == 0), stop=(k == KD - 1))
                    mk.then_inc(k_done, 1)
                    if not first:
                        pe.wait_ge(vbd_ready, 4 * t)
                    rows(bank(3), h1T, wv_sb).then_inc(v_done, 1)
                if last:
                    pe.wait_ge(p_ready, t)
                    if last2:
                        pe.wait_ge(attn_ready, t - 1)
                        pe.wait_ge(x2_ready, t - 1)
                    for g in range(H // 2):
                        mt = nc.tensor.transpose(bank(6 + g // 4)[:, P * (g % 4):P * (g % 4 + 1)],
                                                 prob[:, 2 * g:2 * g + 2, :].rearrange("p a b -> p (a b)"), ident[:, :])
                        if g % 4 == 3:
                            mt.then_inc(pt_done, 1)
                if now:
                    pe.wait_ge(q_ready, t + 1)
                    pe.wait_ge(kbd_ready, HG * (t + 1))
                    if not first:
                        pe.wait_ge(smask_ready, t)
                    for m in range(KD):
                        for b in range(2):
                            ms = mm(bank(4 + m // 2)[S * b:S * (b + 1), HG * S * (m % 2):HG * S * (m % 2 + 1)],
                                    qhT[:, m, S * b:S * (b + 1)], Kbd[:, m, b, :], start=True, stop=True)
                    ms.then_inc(s_done, 1)
                if last:
                    pe.wait_ge(pt_ready, 2 * t)
                    for g in range(H // 2):
                        for b in range(2):
                            ma = mm(bank(6)[S * b:S * (b + 1), 2 * HD * g:2 * HD * (g + 1)], PT[:, g, S * b:S * (b + 1)],
                                    Vbd[:, b, g, :], start=True, stop=True)
                    ma.then_inc(av_done, 1)

            pe.wait_ge(ln_ready, 2)
            for s in attnw_in:
                pe.wait_ge(s, 16)
            stage_b(0, True, False, False, first=True)
            pe.wait_ge(vbd_ready, 4)
            stage_b(1, True, True, False)
            with pe.Fori(2, T) as t:
                stage_b(t, True, True, True)
            stage_b(T, False, True, True)
            stage_b(T + 1, False, False, True)

            pe.wait_ge(ln_ready, 3)
            pe.wait_ge(wr_in, 16)

            def router(t, first):
                pe.wait_ge(r_h2_ready, t + 1)
                if not first:
                    pe.wait_ge(r_h2T_ready, t)
                transposes(bank(0), h2[0]).then_inc(r_h2T_done, 1)
                pe.wait_ge(r_h2T_ready, t + 1)
                if not first:
                    pe.wait_ge(lg_ready, t)
                for k in range(KD):
                    last = mm(bank(3)[:, 0:P], h2T[:, k, :], wr_sb[:, k, :], start=(k == 0), stop=(k == KD - 1))
                last.then_inc(lg_done, 1)

            router(0, True)
            with pe.Fori(1, T) as t:
                router(t, False)
            pe.wait_ge(msk_ready, 1)
            flat = msk.rearrange("p a b -> p (a b)")
            mm(bank(4)[:, 0:T * E], earlier[:, :], flat, start=True, stop=True)
            mm(bank(5)[:, 0:T * E], ones[:, :], flat, start=True, stop=True).then_inc(prefix_done, 1)

            pe.wait_ge(ws_in, 32)

            def shared(t, i, now, last, first=False, second=False):
                if now:
                    pe.wait_ge(h2_ready, t + 1)
                    if not first:
                        pe.wait_ge(h2T_ready, t)
                    transposes(bank(0), h2[i]).then_inc(h2T_done, 1)
                if last:
                    pe.wait_ge(sh_ready, 2 * t)
                    if not second:
                        pe.wait_ge(x3_ready, t - 1)
                    rows(bank(3), shT, ws2_sb).then_inc(shared_done, 1)
                if now:
                    pe.wait_ge(h2T_ready, t + 1)
                    for g in range(2):
                        for m in range(4 * g, 4 * g + 4):
                            for k in range(KD):
                                ms = mm(bank(1 + g)[:, P * (m % 4):P * (m % 4 + 1)], ws1_sb[:, k, P * m:P * (m + 1)],
                                        h2T[:, k, :], start=(k == 0), stop=(k == KD - 1))
                        ms.then_inc(sh_done, 1)

            shared(0, 0, True, False, first=True)
            shared(1, 1, True, True, second=True)
            with pe.Fori(1, T // 2) as n:
                for i in range(2):
                    shared(2 * n + i, i, True, True)
            shared(T, 0, False, True)

            pe.wait_ge(eg_ready, 1)
            pe.wait_ge(w1_in, 16)

            def expert(g):
                return pe.value_load(eg_i[0:1, bass.ds(g, 1)], min_val=0, max_val=E - 1)

            def experts(g, i, now, last, first=False, second=False):
                if now:
                    pe.wait_ge(xg_in[i], 16 * (g // 2 + 1) if isinstance(g, int) else g * 8 + (16 - 8 * i))
                    if not first:
                        pe.wait_ge(xgT_ready, g)
                    transposes(bank(0), xg[i]).then_inc(xgT_done, 1)
                if last:
                    pe.wait_ge(inter_ready, g)
                    if not second:
                        pe.wait_ge(iT_ready, g - 1)
                    transposes(bank(1), inter).then_inc(iT_done, 1)
                if now:
                    e = expert(g)
                    pe.wait_ge(xgT_ready, g + 1)
                    if not first:
                        pe.wait_ge(irelu_ready, g)
                    for k in range(KD):
                        m1 = mm(bank(2), xgT[:, k, :], w1_sb[:, bass.ds(e, 1), k, :].rearrange("p o f -> p (o f)"),
                                start=(k == 0), stop=(k == KD - 1))
                    m1.then_inc(in_done, 1)
                if last:
                    e = expert(g - 1)
                    pe.wait_ge(iT_ready, g)
                    if not second:
                        pe.wait_ge(y_ready, g - 1)
                    for k in range(KD):
                        m2 = mm(bank(3), interT[:, k, :], w2_of(e, k), start=(k == 0), stop=(k == KD - 1))
                    m2.then_inc(y_done, 1)

            pe.wait_ge(w2lo_in, 16)
            pe.wait_ge(w2hi_in, 16)

            lo_word = 0
            hi_word = end_b - KD * FS - KF * D

            def w2_of(e, k):
                at_e = e * (KD * D) + (e >= E // 2) * (hi_word - lo_word - (E // 2) * KD * D) + k * D
                return arena[:, bass.ds(at_e, D)]

            experts(0, 0, True, False, first=True)
            experts(1, 1, True, True, second=True)
            with pe.Fori(1, GT // 2) as n:
                for i in range(2):
                    experts(2 * n + i, i, True, True)
            experts(GT, 0, False, True)


_OUT = "out"


def kernel(x, ctx_1024, L0_xattn_w_sim, L0_xattn_b_sim, L0_xattn_W_qv, L0_xattn_b_qv, L0_attn_Wq, L0_attn_bq,
           L0_attn_Wk, L0_attn_bk, L0_attn_Wv, L0_attn_bv, L0_attn_Wm, L0_attn_bm, L0_ffn_w_router,
           L0_ffn_w1_stack, L0_ffn_w2_stack, L0_ffn_ws1, L0_ffn_ws2):
    import numpy as np
    from concourse import bacc
    from concourse.bass_utils import run_bass_kernel_spmd

    def cols(v):
        return np.asarray(v).reshape(KD, P).T

    ctx = np.asarray(ctx_1024)
    main = ctx[:, :JM * P].reshape(B, P, JM, KD, P).transpose(0, 3, 4, 2, 1).reshape(B, KD, P, JM * P)
    tail = ctx[:, JM * P:].reshape(B, JT, KD, P).transpose(0, 2, 3, 1)
    w_sim = np.asarray(L0_xattn_w_sim)
    w_r = np.zeros((D, P), np.float32)
    w_r[:, :E] = np.asarray(L0_ffn_w_router).T
    ins = {
        "x": np.asarray(x).reshape(B * S, D),
        "ctx_n": ctx,
        "ctx_t": np.concatenate([main, tail], axis=-1),
        "w1": w_sim[0:D],
        "w23": np.stack([cols(w_sim[D:2 * D]), cols(w_sim[2 * D:])], axis=1),
        "b_sim": np.asarray(L0_xattn_b_sim),
        "w_qv": np.asarray(L0_xattn_W_qv),
        "b_qv": np.asarray(L0_xattn_b_qv),
        "wq": np.asarray(L0_attn_Wq), "wk": np.asarray(L0_attn_Wk),
        "wv": np.asarray(L0_attn_Wv), "wm": np.asarray(L0_attn_Wm),
        "b_qk": np.stack([cols(L0_attn_bq), cols(L0_attn_bk)], axis=1),
        "bv": np.asarray(L0_attn_bv), "bm": np.asarray(L0_attn_bm),
        "w_router": w_r,
        "w1t": np.asarray(L0_ffn_w1_stack).transpose(0, 2, 1),
        "w2t": np.asarray(L0_ffn_w2_stack).transpose(0, 2, 1),
        "ws1t": np.asarray(L0_ffn_ws1).T,
        "ws2t": np.asarray(L0_ffn_ws2).T,
    }
    ins = {n: np.ascontiguousarray(a) for n, a in ins.items()}
    nc = bacc.Bacc("TRN2", target_bir_lowering=False, num_devices=1)
    aps = [nc.dram_tensor(n, a.shape, mybir.dt.from_np(a.dtype), kind="ExternalInput").ap() for n, a in ins.items()]
    out = nc.dram_tensor(_OUT, (B * S, D), F32, kind="ExternalOutput").ap()
    perceiver_layer(nc, *aps, out)
    r = run_bass_kernel_spmd(nc, [ins], core_ids=[0])
    return r.results[0][_OUT].reshape(B, S, D)
```

```python
from contextlib import ExitStack

import concourse.bass as bass
from concourse import mybir

F32 = mybir.dt.float32
I32 = mybir.dt.int32
ALU = mybir.AluOpType
ACT = mybir.ActivationFunctionType
AX = mybir.AxisListType.X

P = 128
B, S, D = 32, 64, 512
J = 1601
T = B * S // P
KD = D // P
JM = J // P
JT = J - JM * P
JC = JM + 1
JB = [(c * D, min(D, J - c * D)) for c in range(-(-J // D))]
NP = 5
H, HD = 16, 32
HG = P // HD
FS = 1024
KF = FS // P
E, F = 8, 512
GT = (2 * B * S) // P + E
TX = 2
TA = 3 * T // 4
TH = T // 2
EPS = 1e-5
SCALE = float(HD) ** 0.5
MASKED = -1.0e12
BIG = 3.0e38


def perceiver_layer(nc, x, ctx_n, ctx_t, w1, w23, b_sim, w_qv, b_qv, wq, wk, wv, wm, b_qk, bv, bm,
                    w_router, w1t, w2t, ws1t, ws2t, out):
    moe_in = nc.dram_tensor("moe_in", [GT * P, D], F32).ap()
    moe_out = nc.dram_tensor("moe_out", [GT * P, D], F32).ap()
    x3_away = nc.dram_tensor("x3_away", [TH * P, D], F32).ap()

    with ExitStack() as stack:
        def sb(name, shape, dt=F32):
            return stack.enter_context(nc.sbuf_tensor(name, shape, dt))

        def sem(name):
            return stack.enter_context(nc.semaphore(name))

        ident = sb("ident", [P, P])
        ones = sb("ones", [P, P])
        same_batch = sb("same_batch", [P, P])
        earlier = sb("earlier", [P, P])
        causal = sb("causal", [P, S])
        causal_b = sb("causal_b", [P, S])
        row_a = sb("row_a", [P, D])
        row_b = sb("row_b", [P, D])
        w23c = sb("w23c", [P, 2, KD])
        bqkc = sb("bqkc", [P, 2, KD])
        bsim = sb("bsim", [P, 1])
        stats = sb("stats", [P, T, 6])
        mean = sb("mean", [P, T])
        dmean = sb("dmean", [P, T])
        var = sb("var", [P, T])
        rstd = sb("rstd", [P, T])
        nmr = sb("nmr", [P, T])
        small = sb("small", [P, 16])
        rinv = sb("rinv", [P, H])
        rmax = sb("rmax", [P, H])
        rsum = sb("rsum", [P, H])
        wt0 = sb("wt0", [P, T])
        wt1 = sb("wt1", [P, T])
        cdot, smax, nsmax, smx, erow, rs, bmax, nbmax, bsum, ecol, brec, cnow = (
            small[:, i:i + 1] for i in range(12))

        ARENA = 42496
        arena = sb("arena", [P, ARENA + T * D])
        X = arena[:, ARENA:].rearrange("p (t d) -> p t d", d=D)
        used = [0]

        def at(lo):
            used[0] = lo

        def carve(*dims):
            n = 1
            for d in dims:
                n *= d
            v = arena[:, used[0]:used[0] + n]
            used[0] += n
            if len(dims) == 2:
                v = v.rearrange("p (a b) -> p a b", b=dims[1])
            if len(dims) == 3:
                v = v.rearrange("p (a b c) -> p a b c", b=dims[1], c=dims[2])
            if len(dims) == 4:
                v = v.rearrange("p (a b c d) -> p a b c d", b=dims[1], c=dims[2], d=dims[3])
            return v

        at(0)
        ctxT = [carve(KD, J) for _ in range(2)]
        ctxN = [carve(JC, D) for _ in range(2)]
        w_qv_sb = carve(4 * KD, D)
        expS = carve(J)
        used[0] += -used[0] % 4
        ET = carve(JC, P)
        hc = carve(D)
        hc2 = carve(D)
        qT = carve(KD, P)
        hq = carve(D)
        F1, F2, F3, F4 = (carve(KD, P) for _ in range(4))
        diag = carve(P)
        bexp = carve(S)
        bmat = carve(P)
        end_a = used[0]
        at(0)
        wq_sb, wk_sb, wv_sb, wm_sb = (carve(KD, D) for _ in range(4))
        h1 = carve(D)
        h1T = carve(KD, P)
        qhT = carve(KD, P)
        khT = carve(KD, P)
        Kbd = carve(KD, 2, HG * S)
        Vbd = carve(2, H // 2, 2 * HD)
        sm = carve(H, S)
        prob = carve(H, S)
        PT = carve(H // 2, P)
        attn = carve(H, HD)
        attnT = carve(KD, P)
        w1_sb = carve(E, KD, F)
        ws1_sb = carve(KD, FS)
        ws2_sb = carve(KF, D)
        zero = carve(D)
        end_b = used[0]
        at(0)
        w2_low = carve(6, KD, D)
        w2_high = arena[:, ARENA:ARENA + TH * D].rearrange("p (e k d) -> p e k d", k=KD, d=D)
        assert TH * D == 2 * KD * D
        at(4 * KD * D)
        wr_sb = carve(KD, P)
        pr, pr2, eq, cand, oh0, oh1, msk, tot, inc0, inc1, slotm = (carve(T, E) for _ in range(11))
        inc = [inc0, inc1]
        iota_m8 = carve(E)
        iota_k = carve(T)
        iota_g = carve(GT)
        cntcmp = carve(E, T)
        gcmp = carve(GT, E)
        v0, v1, e0, e1, s0f, s1f, vs = (carve(T) for _ in range(7))
        nt, st0, st1, cnt = (carve(E) for _ in range(4))
        eg_f = carve(GT)
        assert used[0] <= 6 * KD * D, used[0]
        at(6 * KD * D)
        h2 = carve(D)
        h2T = carve(KD, P)
        shT = carve(KF, P)
        hs = [carve(D) for _ in range(2)]
        xg = [carve(D) for _ in range(2)]
        xgT = carve(KD, P)
        interT = carve(KD, P)
        assert used[0] <= 8192 + 9216, used[0]
        inter = row_a[:, :]
        h2Ts = [h2T, interT]
        yg = hs
        y01 = [[w1_sb[:, i, 2 * k, :] for i in range(4)] for k in range(2)]
        assert max(end_a, end_b) <= ARENA, (end_a, end_b)
        slot_i = [sb(f"slot_i{k}", [P, T], I32) for k in range(2)]
        eg_i = sb("eg_i", [P, GT], I32)
        idx = [[sb(f"idx{k}{i}", [P, 1], I32) for i in range(4)] for k in range(2)]

        ps = stack.enter_context(nc.psum_tensor("ps", [P, 8, D], F32))

        def bank(i):
            return ps[:, i, :]

        x_in = [sem(f"x_in{i}") for i in range(2)]
        const_in, wqv_in = sem("const_in"), sem("wqv_in")
        ctxT_in = [[sem(f"ctxT_in{h}{k}") for k in range(KD)] for h in range(2)]
        ctxN_in = [[sem(f"ctxN_in{h}{q}") for q in range(NP)] for h in range(2)]
        attnw_in = [sem(f"attnw_in{i}") for i in range(4)]
        rows_in = sem("rows_in")
        w1_in, ws_in, w2_in, wr_in = (sem(n) for n in ("w1_in", "ws_in", "w2_in", "wr_in"))
        pool_step, consts_ready = sem("pool_step"), sem("consts_ready")
        pool_go = sem("pool_go")
        dve_step = sem("dve_step")
        act_step = sem("act_step")
        stats_ready = sem("stats_ready")
        var_ready, std_ready, ln_ready = sem("var_ready"), sem("std_ready"), sem("ln_ready")
        hc_ready, c_ready, cnow_ready, hc2_ready, xb_ready = (
            sem(n) for n in ("hc_ready", "c_ready", "cnow_ready", "hc2_ready", "xb_ready"))
        hcT_done, F1_ready, qT_ready = (sem(n) for n in ("hcT_done", "F1_ready", "qT_ready"))
        sim_done, pv_done = sem("sim_done"), sem("pv_done")
        max_ready, nmax_ready, smx_ready, diag_ready = (sem(n) for n in ("max_ready", "nmax_ready", "smx_ready", "diag_ready"))
        exp_done, et_done, et_act, et_dve = (sem(n) for n in ("exp_done", "et_done", "et_act", "et_dve"))
        rs_ready, hq_ready, hqT_done, F2_ready, F34_ready = (
            sem(n) for n in ("rs_ready", "hq_ready", "hqT_done", "F2_ready", "F34_ready"))
        mxb_done, bmax_ready, nbmax_ready, bexp_ready, brec_ready, bmat_ready, hb_done = (
            sem(n) for n in ("mxb_done", "bmax_ready", "nbmax_ready", "bexp_ready", "brec_ready", "bmat_ready", "hb_done"))
        feats_done, x1_ready = sem("feats_done"), sem("x1_ready")
        kbd_zero, vbd_zero = sem("kbd_zero"), sem("vbd_zero")
        h1_ready, xb2_ready, h1T_done, h1T_ready = (sem(n) for n in ("h1_ready", "xb2_ready", "h1T_done", "h1T_ready"))
        q_done, k_done, v_done, q_ready, k_ready, kbd_ready, vbd_ready = (
            sem(n) for n in ("q_done", "k_done", "v_done", "q_ready", "k_ready", "kbd_ready", "vbd_ready"))
        s_done, smask_ready, smax_ready, ssub_ready, p_ready, ssum_ready, rinv_ready = (
            sem(n) for n in ("s_done", "smask_ready", "smax_ready", "ssub_ready", "p_ready", "ssum_ready", "rinv_ready"))
        pt_done, pt_ready, av_done, attn_norm, attn_ready, attnT_done, attnT_ready, out_done, x2_ready = (
            sem(n) for n in ("pt_done", "pt_ready", "av_done", "attn_norm", "attn_ready", "attnT_done", "attnT_ready",
                             "out_done", "x2_ready"))
        zero_ready, slots_zeroed, iota_ready = sem("zero_ready"), sem("slots_zeroed"), sem("iota_ready")
        r_h2_ready, r_h2T_done, r_h2T_ready, lg_done = (
            sem(n) for n in ("r_h2_ready", "r_h2T_done", "r_h2T_ready", "lg_done"))
        rexp_in, rexp_ready, msk_ready, prefix_done, eg_ready = (
            sem(n) for n in ("rexp_in", "rexp_ready", "msk_ready", "prefix_done", "eg_ready"))
        hs_ready, idx_ready, scat = sem("hs_ready"), sem("idx_ready"), [sem(f"scattered{i}") for i in range(2)]
        h2_ready, h2T_done, h2T_ready, sh_done, relu_ready, sh_ready, shared_done, x3_ready = (
            sem(n) for n in ("h2_ready", "h2T_done", "h2T_ready", "sh_done", "relu_ready", "sh_ready", "shared_done", "x3_ready"))
        x3_out, x3_back = sem("x3_out"), sem("x3_back")
        xg_in = [sem(f"xg_in{i}") for i in range(2)]
        xgT_done, xgT_ready, in_done, irelu_ready, inter_ready, iT_done, iT_ready, y_done, y_ready = (
            sem(n) for n in ("xgT_done", "xgT_ready", "in_done", "irelu_ready", "inter_ready", "iT_done", "iT_ready",
                             "y_done", "y_ready"))
        y_out = [sem(f"y_out{i}") for i in range(2)]
        gidx_ready, y01_in = sem("gidx_ready"), [sem(f"y01_in{i}") for i in range(4)]
        mix0_ready, mix_ready, out_sem = sem("mix0_ready"), sem("mix_ready"), sem("out_sem")

        x_v = x.rearrange("(t p) d -> p t d", p=P)
        out_v = out.rearrange("(t p) d -> p t d", p=P)

        block = stack.enter_context(nc.Block())

        @block.sync
        def _(sp):
            sp.dma_start(X[:, 0:TX, :], x_v[:, 0:TX, :]).then_inc(x_in[0], 16)
            sp.dma_start(row_a[:, :], w1.partition_broadcast(P)).then_inc(const_in, 16)
            sp.dma_start(row_b[:, :], b_qv.partition_broadcast(P)).then_inc(const_in, 16)
            sp.dma_start(w23c[:, :, :], w23).then_inc(const_in, 16)
            sp.dma_start(bqkc[:, :, :], b_qk).then_inc(const_in, 16)
            sp.dma_start(bsim[:, :], b_sim.partition_broadcast(P)).then_inc(const_in, 16)

            def load_ctx(t, first):
                for k in range(KD):
                    if not first:
                        sp.wait_ge(sim_done, KD * t + (k + 1 - KD))
                    for h in range(2):
                        src = ctx_t[bass.ds(2 * t + h, 1), k].rearrange("o p n -> p (o n)")
                        sp.dma_start(ctxT[h][:, k, :], src).then_inc(ctxT_in[h][k], 16)
                for q in range(NP):
                    if not first:
                        sp.wait_ge(pv_done, NP * t + (q + 1 - NP))
                    for h in range(2):
                        one = ctx_n[bass.ds(2 * t + h, 1)].rearrange("o j d -> (o j) d")
                        if q < NP - 1:
                            n = JM // (NP - 1)
                            main = one[0:JM * P].rearrange("(p c) d -> p c d", c=JM)
                            sp.dma_start(ctxN[h][:, n * q:n * (q + 1), :],
                                         main[:, n * q:n * (q + 1), :]).then_inc(ctxN_in[h][q], 16)
                        else:
                            sp.dma_start(ctxN[h][0:JT, JM, :], one[JM * P:J]).then_inc(ctxN_in[h][q], 16)

            load_ctx(0, True)
            sp.dma_start(X[:, TX:T, :], x_v[:, TX:T, :]).then_inc(x_in[1], 16)
            sp.dma_start(w_qv_sb, w_qv.rearrange("(k p) n -> p k n", p=P)).then_inc(wqv_in, 16)
            with sp.Fori(1, T) as t:
                load_ctx(t, False)
            sp.wait_ge(sim_done, KD * (T))
            for i, (dst, src) in enumerate(((wq_sb, wq), (wk_sb, wk), (wv_sb, wv), (wm_sb, wm))):
                sp.dma_start(dst, src.rearrange("(k p) n -> p k n", p=P)).then_inc(attnw_in[i], 16)
            sp.wait_ge(c_ready, T)
            sp.dma_start(row_a[:, :], bv.partition_broadcast(P)).then_inc(rows_in, 16)
            sp.wait_ge(xb_ready, T)
            sp.dma_start(row_b[:, :], bm.partition_broadcast(P)).then_inc(rows_in, 16)
            sp.wait_ge(feats_done, T)
            sp.dma_start(w1_sb, w1t.rearrange("e (k p) n -> p e k n", p=P)).then_inc(w1_in, 16)
            sp.dma_start(ws1_sb, ws1t.rearrange("(k p) n -> p k n", p=P)).then_inc(ws_in, 16)
            sp.dma_start(ws2_sb, ws2t.rearrange("(k p) n -> p k n", p=P)).then_inc(ws_in, 16)
            sp.wait_ge(zero_ready, 1)
            for q in range(4):
                n = GT // 4
                dst = moe_in.rearrange("(g p) d -> p g d", p=P)[:, n * q:n * (q + 1), :]
                sp.dma_start(dst, zero.unsqueeze(1).to_broadcast([P, n, D])).then_inc(slots_zeroed, 16)
            sp.wait_ge(out_done, T)
            sp.wait_ge(attnT_ready, T)
            sp.dma_start(wr_sb, w_router.rearrange("(k p) n -> p k n", p=P)).then_inc(wr_in, 16)
            w2v = w2t.rearrange("e (k p) n -> p e k n", p=P)
            sp.dma_start(w2_low[:, 0:4], w2v[:, 0:4]).then_inc(w2_in, 16)
            sp.wait_ge(eg_ready, 1)
            sp.dma_start(w2_low[:, 4:6], w2v[:, 4:6]).then_inc(w2_in, 16)
            sp.wait_ge(x3_ready, TH)
            sp.dma_start(x3_away.rearrange("(t p) d -> p t d", p=P), X[:, 0:TH, :]).then_inc(x3_out, 16)
            sp.wait_ge(x3_out, 16)
            sp.dma_start(w2_high, w2v[:, 6:8]).then_inc(w2_in, 16)
            for i in range(2):
                sp.wait_ge(scat[i], 32 * (T // 2))

            def load_slots(g, i):
                sp.dma_start(xg[i], moe_in[bass.ds(g * P, P), :]).then_inc(xg_in[i], 16)

            def store_slots(g, i):
                sp.wait_ge(y_ready, g + 1)
                sp.dma_start(moe_out[bass.ds(g * P, P), :], yg[i]).then_inc(y_out[i], 16)

            load_slots(0, 0)
            load_slots(1, 1)
            def slots(g, i, first=False):
                sp.wait_ge(xgT_done, g + 1)
                load_slots(g + 2, i)
                if not first:
                    store_slots(g - 1, 1 - i)

            slots(0, 0, first=True)
            slots(1, 1)
            with sp.Fori(1, GT // 2 - 1) as n:
                for i in range(2):
                    slots(2 * n + i, i)
            store_slots(GT - 3, 1)
            for i in range(2):
                store_slots(GT - 2 + i, i)
            sp.dma_start(X[:, 0:TH, :], x3_away.rearrange("(t p) d -> p t d", p=P)).then_inc(x3_back, 16)
            with sp.Fori(0, T) as t:
                sp.wait_ge(mix_ready, t + 1)
                sp.dma_start(out_v[:, bass.ds(t, 1), :], X[:, bass.ds(t, 1), :]).then_inc(out_sem, 16)
            sp.wait_ge(out_sem, 16 * T)

        @block.gpsimd
        def _(pool):
            nc.gpsimd.memset(ident[:, :], 0.0).then_inc(pool_step, 1)
            nc.gpsimd.memset(earlier[:, :], 1.0).then_inc(pool_step, 1)
            nc.gpsimd.memset(causal[:, :], BIG).then_inc(pool_step, 1)
            nc.gpsimd.memset(causal_b[:, :], BIG).then_inc(pool_step, 1)
            nc.gpsimd.memset(ones[:, :], 1.0).then_inc(consts_ready, 1)
            pool.wait_ge(pool_step, 4)
            nc.gpsimd.affine_select(out=ident[:, :], in_=ident[:, :], compare_op=ALU.not_equal, fill=1.0, base=0,
                                    pattern=[[-1, P]], channel_multiplier=1).then_inc(consts_ready, 1)
            nc.gpsimd.affine_select(out=earlier[:, :], in_=earlier[:, :], compare_op=ALU.is_gt, fill=0.0, base=0,
                                    pattern=[[1, P]], channel_multiplier=-1).then_inc(consts_ready, 1)
            nc.gpsimd.affine_select(out=causal[:, :], in_=causal[:, :], compare_op=ALU.is_ge, fill=MASKED, base=0,
                                    pattern=[[-1, S]], channel_multiplier=1).then_inc(consts_ready, 1)
            nc.gpsimd.affine_select(out=causal_b[:, :], in_=causal_b[:, :], compare_op=ALU.is_ge, fill=MASKED,
                                    base=-S, pattern=[[-1, S]], channel_multiplier=1).then_inc(consts_ready, 1)

            def copies(t, first):
                pool.wait_ge(hc_ready, t + 1)
                if not first:
                    pool.wait_ge(hb_done, t)
                xt = X[:, bass.ds(t, 1), :].rearrange("p o d -> p (o d)")
                nc.gpsimd.tensor_tensor(xt, xt, row_b[:, :], ALU.add).then_inc(xb_ready, 1)
                nc.gpsimd.tensor_copy(hc2, hc).then_inc(hc2_ready, 1)

            pool.wait_ge(const_in, 80)
            copies(0, True)
            with pool.Fori(1, T) as t:
                copies(t, False)
            pool.wait_ge(feats_done, T)
            pool.wait_ge(pv_done, NP * (T))
            nc.gpsimd.memset(Kbd, 0.0).then_inc(kbd_zero, 1)
            nc.gpsimd.memset(Vbd, 0.0).then_inc(vbd_zero, 1)
            nc.gpsimd.memset(zero, 0.0).then_inc(zero_ready, 1)
            pool.wait_ge(rows_in, 32)

            def add_bm(t):
                pool.wait_ge(h1_ready, t + 1)
                xt = X[:, bass.ds(t, 1), :].rearrange("p o d -> p (o d)")
                nc.gpsimd.tensor_tensor(xt, xt, row_b[:, :], ALU.add).then_inc(xb2_ready, 1)

            with pool.Fori(0, T) as t:
                add_bm(t)
            pool.wait_ge(out_done, T)
            pool.wait_ge(attnT_ready, T)
            nc.gpsimd.iota(iota_m8, pattern=[[1, E]], base=-E, channel_multiplier=0,
                           allow_small_or_imprecise_dtypes=True).then_inc(iota_ready, 1)
            nc.gpsimd.iota(iota_k, pattern=[[P, T]], base=0, channel_multiplier=0,
                           allow_small_or_imprecise_dtypes=True).then_inc(iota_ready, 1)
            nc.gpsimd.iota(iota_g, pattern=[[1, GT]], base=0, channel_multiplier=0,
                           allow_small_or_imprecise_dtypes=True).then_inc(iota_ready, 1)
            with pool.Fori(0, T // 2) as n:
                for i in range(2):
                    pool.wait_ge(hs_ready, 2 * n + i + 1)
                    pool.wait_ge(idx_ready, 4 * n + 2 * i + 2)
                    pool.wait_ge(slots_zeroed, 64)
                    pool.sem_inc(pool_go, 1)
                    for k in range(2):
                        nc.gpsimd.indirect_dma_start(
                            moe_in, bass.IndirectOffsetOnAxis(ap=idx[k][i][:, :], axis=0), hs[i], None
                        ).then_inc(scat[i], 16)
            for s in y_out:
                pool.wait_ge(s, 16 * (GT // 2))

            def gather(n, i, first):
                if not first:
                    pool.wait_ge(mix_ready, 4 * (n - 1) + i + 1)
                    pool.sem_inc(pool_go, 1)
                for k in range(2):
                    nc.gpsimd.tensor_copy(idx[k][i][:, :], slot_i[k][:, bass.ds(4 * n + i, 1)]).then_inc(gidx_ready, 1)
                pool.wait_ge(gidx_ready, 8 * n + 2 * i + 2)
                pool.sem_inc(pool_go, 1)
                for k in range(2):
                    nc.gpsimd.indirect_dma_start(
                        y01[k][i], None, moe_out, bass.IndirectOffsetOnAxis(ap=idx[k][i][:, :], axis=0)
                    ).then_inc(y01_in[i], 16)

            for i in range(4):
                gather(0, i, True)
            with pool.Fori(1, T // 4) as n:
                for i in range(4):
                    gather(n, i, False)

        @block.scalar
        def _(act):
            def copy(o, i):
                return nc.scalar.activation(o, i, ACT.Copy)

            def sqrt_of_var(s, lo=0, hi=T):
                act.wait_ge(var_ready, s + 1)
                nc.scalar.activation(var[:, lo:hi], var[:, lo:hi], ACT.Sqrt).then_inc(std_ready, 1)

            def exp_scores(t, first):
                act.wait_ge(nmax_ready, t + 1)
                if not first:
                    act.wait_ge(et_done, 4 * t)
                    act.wait_ge(rs_ready, t)
                nc.scalar.activation(expS, ps[:, 0:4, :].rearrange("p a b -> p (a b)")[:, 0:J], ACT.Exp,
                                     bias=nsmax, accum_out=erow).then_inc(exp_done, 1)

            def after_scores(t, first, tail=True):
                if not first:
                    act.wait_ge(feats_done, t)
                act.wait_ge(hcT_done, t + 1)
                copy(F1.rearrange("p a b -> p (a b)"), bank(4)).then_inc(F1_ready, 1)
                for g in (0, 2):
                    act.wait_ge(et_done, 4 * t + g + 1)
                    if not first and g == 0:
                        act.wait_ge(pv_done, NP * (t))
                    copy(ET[:, 4 * g:4 * g + 4, :].rearrange("p a b -> p (a b)"), bank(g)).then_inc(et_act, 1)
                act.wait_ge(nbmax_ready, t + 1)
                if not first:
                    act.wait_ge(bmat_ready, t)
                for h in range(2):
                    r = slice(S * h, S * (h + 1))
                    nc.scalar.activation(bexp[r, :],
                                         bank(6)[r, S * h:S * (h + 1)], ACT.Exp, bias=nbmax[r, :],
                                         accum_out=bsum[r, :]).then_inc(bexp_ready, 1)
                nc.scalar.activation(ecol, smx, ACT.Exp, bias=nbmax).then_inc(bexp_ready, 1)
                if tail:
                    attended_copy(t)

            def attended_copy(t):
                act.wait_ge(hqT_done, t + 1)
                copy(F2.rearrange("p a b -> p (a b)"), bank(5)).then_inc(F2_ready, 1)

            sqrt_of_var(0, 0, TX)
            exp_scores(0, True)
            after_scores(0, True, tail=False)
            sqrt_of_var(1, TX, T)
            attended_copy(0)
            exp_scores(1, False)
            after_scores(1, False)
            with act.Fori(2, T) as t:
                exp_scores(t, False)
                after_scores(t, False)
            sqrt_of_var(2)

            def h1T_copy(t, first):
                act.wait_ge(h1T_done, t + 1)
                if not first:
                    act.wait_ge(v_done, t)
                copy(h1T.rearrange("p a b -> p (a b)"), bank(0)).then_inc(h1T_ready, 1)

            def attnT_copy(t):
                act.wait_ge(attnT_done, t + 1)
                copy(attnT.rearrange("p a b -> p (a b)"), bank(2)).then_inc(attnT_ready, 1)

            def keys(t, first):
                act.wait_ge(k_ready, t + 1)
                if not first:
                    act.wait_ge(s_done, t)
                for h in range(HG):
                    r = slice(HD * h, HD * (h + 1))
                    copy(Kbd[r, :, :, S * h:S * (h + 1)],
                         khT[r].rearrange("p m (b j) -> p m b j", b=2)).then_inc(kbd_ready, 1)

            def pt_copy(t, first):
                for g in range(2):
                    act.wait_ge(pt_done, 2 * t + g + 1)
                    if not first and g == 0:
                        act.wait_ge(av_done, t)
                    copy(PT[:, 4 * g:4 * g + 4, :].rearrange("p a b -> p (a b)"), bank(6 + g)).then_inc(pt_ready, 1)

            def exp_probs(t, first):
                act.wait_ge(ssub_ready, t + 1)
                if not first:
                    act.wait_ge(pt_done, 2 * t)
                    act.wait_ge(ssum_ready, t)
                nc.scalar.activation(prob.rearrange("p a b -> p (a b)"), sm.rearrange("p a b -> p (a b)"),
                                     ACT.Exp).then_inc(p_ready, 1)

            def stage_b(t, now, last, last2, second=False, more=True):
                if last2:
                    attnT_copy(t - 2)
                if last:
                    exp_probs(t - 1, second)
                    pt_copy(t - 1, second)
                if now:
                    keys(t, not last)
                    if more:
                        h1T_copy(t + 1, False)

            act.wait_ge(kbd_zero, 1)
            h1T_copy(0, True)
            stage_b(0, True, False, False)
            stage_b(1, True, True, False, second=True)
            with act.Fori(2, T - 1) as t:
                stage_b(t, True, True, True)
            stage_b(T - 1, True, True, True, more=False)
            stage_b(T, False, True, True)
            stage_b(T + 1, False, False, True)
            sqrt_of_var(3)

            act.wait_ge(ln_ready, 4)

            def router(t, i, first):
                act.wait_ge(r_h2T_done, t + 1)
                if not first:
                    act.wait_ge(lg_done, t - 1)
                copy(h2Ts[i].rearrange("p a b -> p (a b)"), bank(i)).then_inc(r_h2T_ready, 1)

            for i in range(2):
                router(i, i, True)
            with act.Fori(1, T // 2) as n:
                for i in range(2):
                    router(2 * n + i, i, False)
            act.wait_ge(rexp_in, 1)
            nc.scalar.activation(pr.rearrange("p a b -> p (a b)"), pr2.rearrange("p a b -> p (a b)"),
                                 ACT.Exp).then_inc(rexp_ready, 1)

            def tokens_T(t, i, first=False):
                act.wait_ge(h2T_done, t + 1)
                if not first:
                    act.wait_ge(sh_done, 2 * (t - 1))
                copy(h2Ts[i].rearrange("p a b -> p (a b)"), bank(0)).then_inc(h2T_ready, 1)

            def shared(t, i, first=False, more=True):
                for g in range(2):
                    act.wait_ge(sh_done, 2 * t + g + 1)
                    if not first and g == 0:
                        act.wait_ge(shared_done, t)
                    nc.scalar.activation(shT[:, 4 * g:4 * g + 4, :].rearrange("p a b -> p (a b)"), bank(1 + g),
                                         ACT.Relu).then_inc(relu_ready, 1)
                    if g == 0 and more:
                        tokens_T(t + 1, 1 - i, first)

            act.wait_ge(lg_done, T)
            tokens_T(0, 0, True)
            shared(0, 0, first=True)
            shared(1, 1)
            with act.Fori(1, TA // 2) as n:
                for i in range(2):
                    shared(2 * n + i, i)

            def experts(g, now, last, more):
                if last:
                    act.wait_ge(iT_done, g)
                    copy(interT.rearrange("p a b -> p (a b)"), bank(5)).then_inc(iT_ready, 1)
                if now:
                    act.wait_ge(in_done, g + 1)
                    nc.scalar.activation(inter, bank(6), ACT.Relu).then_inc(irelu_ready, 1)
                if more:
                    act.wait_ge(xgT_done, g + 2)
                    copy(xgT.rearrange("p a b -> p (a b)"), bank(4)).then_inc(xgT_ready, 1)

            experts(-1, False, False, True)
            experts(0, True, False, True)
            with act.Fori(1, GT - 1) as g:
                experts(g, True, True, True)
            experts(GT - 1, True, True, False)
            experts(GT, False, True, False)

            for t in range(TA, T):
                shared(t, t % 2, more=t < T - 1)

        @block.vector
        def _(dve):
            v = nc.vector
            chain = [0]

            def step(ins):
                chain[0] += 1
                ins.then_inc(dve_step, 1)
                dve.wait_ge(dve_step, chain[0])

            def finish_norm(s, count, lo=0, hi=T):
                r = slice(lo, hi)
                dve.wait_ge(stats_ready, count)
                step(v.tensor_tensor(mean[:, r], stats[:, r, 1], stats[:, r, 4], ALU.add))
                step(v.tensor_scalar(mean[:, r], mean[:, r], 0.5, None, ALU.mult))
                step(v.tensor_tensor(dmean[:, r], stats[:, r, 1], stats[:, r, 4], ALU.subtract))
                step(v.tensor_tensor(dmean[:, r], dmean[:, r], dmean[:, r], ALU.mult))
                step(v.tensor_tensor(var[:, r], stats[:, r, 2], stats[:, r, 5], ALU.add))
                step(v.scalar_tensor_tensor(var[:, r], dmean[:, r], D / 4.0, var[:, r], ALU.mult, ALU.add))
                v.tensor_scalar(var[:, r], var[:, r], 1.0 / D, EPS, ALU.mult, ALU.add).then_inc(var_ready, 1)
                dve.wait_ge(std_ready, s + 1)
                step(v.reciprocal(rstd[:, r], var[:, r]))
                v.scalar_tensor_tensor(nmr[:, r], mean[:, r], -1.0, rstd[:, r], ALU.mult, ALU.mult
                                       ).then_inc(ln_ready, 1)
                dve.wait_ge(ln_ready, s + 1)

            def x_tile(t):
                return X[:, bass.ds(t, 1), :].rearrange("p o d -> p (o d)")

            def normed(o, t):
                return v.tensor_scalar(o, x_tile(t), rstd[:, bass.ds(t, 1)], nmr[:, bass.ds(t, 1)], ALU.mult, ALU.add)

            def row_stats(t):
                return v.bn_stats(stats[:, bass.ds(t, 1), :].rearrange("p o s -> p (o s)"), x_tile(t))

            dve.wait_ge(x_in[0], 16)
            for t in range(TX):
                row_stats(t).then_inc(stats_ready, 1)
            finish_norm(0, TX, 0, TX)
            dve.wait_ge(const_in, 80)
            dve.wait_ge(consts_ready, 5)

            step(v.memset(same_batch[:, :], 0.0))
            for h in range(2):
                r = slice(S * h, S * (h + 1))
                step(v.memset(same_batch[r, r], 1.0))
            step(v.tensor_copy(causal[S:P, :], causal_b[S:P, :]))

            def norm_a(t, first, second=False):
                if not first:
                    dve.wait_ge(hcT_done, t)
                    dve.wait_ge(hc2_ready, t)
                normed(hc, t).then_inc(hc_ready, 1)
                if not first and not second:
                    dve.wait_ge(et_done, 4 * (t - 1))
                dve.wait_ge(hc_ready, t + 1)
                v.scalar_tensor_tensor(expS[:, 0:D], hc, 1.0, row_a[:, :], ALU.mult, ALU.mult,
                                       accum_out=cdot).then_inc(c_ready, 1)

            def keep_c(t):
                dve.wait_ge(c_ready, t + 1)
                v.tensor_copy(cnow, cdot).then_inc(cnow_ready, 1)
                dve.wait_ge(cnow_ready, t + 1)

            def queries(t, first):
                dve.wait_ge(hcT_done, t + 1)
                if not first:
                    dve.wait_ge(sim_done, KD * (t))
                for k in range(KD):
                    v.tensor_scalar(qT[:, k, :], bank(4)[:, P * k:P * (k + 1)], w23c[:, 1, k:k + 1],
                                    w23c[:, 0, k:k + 1], ALU.mult, ALU.add).then_inc(qT_ready, 1)

            def maxima(t, first):
                dve.wait_ge(sim_done, KD * (t + 1))
                if not first:
                    dve.wait_ge(exp_done, t)
                    dve.wait_ge(bexp_ready, 3 * t)
                    dve.wait_ge(mxb_done, t)
                v.reduce_max(smax, ps[:, 0:4, :].rearrange("p a b -> p (a b)")[:, 0:J], AX).then_inc(max_ready, 1)
                dve.wait_ge(max_ready, t + 1)
                v.tensor_scalar(nsmax, smax, -1.0, None, ALU.mult).then_inc(nmax_ready, 1)
                v.scalar_tensor_tensor(smx, smax, cnow, bsim[:, :], ALU.add, ALU.add).then_inc(smx_ready, 1)
                dve.wait_ge(smx_ready, t + 1)
                v.tensor_scalar(diag, ident[:, :], smx, None, ALU.mult).then_inc(diag_ready, 1)

            def batch_weights(t, first):
                dve.wait_ge(mxb_done, t + 1)
                if not first:
                    dve.wait_ge(bexp_ready, 3 * t)
                for h in range(2):
                    r = slice(S * h, S * (h + 1))
                    v.reduce_max(bmax[r, :], bank(6)[r, S * h:S * (h + 1)], AX).then_inc(bmax_ready, 1)
                dve.wait_ge(bmax_ready, 2 * (t + 1))
                v.tensor_scalar(nbmax, bmax, -1.0, None, ALU.mult).then_inc(nbmax_ready, 1)
                dve.wait_ge(bexp_ready, 3 * (t + 1))
                if not first:
                    dve.wait_ge(hb_done, t)
                v.reciprocal(brec, bsum).then_inc(brec_ready, 1)
                dve.wait_ge(brec_ready, t + 1)
                v.tensor_scalar(bmat, same_batch[:, :], ecol, brec, ALU.mult, ALU.mult).then_inc(bmat_ready, 1)

            def exp_copies(t, first):
                for g in (1, 3):
                    dve.wait_ge(et_done, 4 * t + g + 1)
                    if not first and g == 1:
                        dve.wait_ge(pv_done, NP * (t))
                    if g == 1:
                        v.tensor_copy(ET[:, 4:8, :].rearrange("p a b -> p (a b)"), bank(1)).then_inc(et_dve, 1)
                    else:
                        v.tensor_copy(ET[0:JT, JM, :], bank(3)[0:JT, 0:P]).then_inc(et_dve, 1)

            def attended(t, first):
                dve.wait_ge(exp_done, t + 1)
                v.reciprocal(rs, erow).then_inc(rs_ready, 1)
                dve.wait_ge(pv_done, NP * (t + 1))
                dve.wait_ge(rs_ready, t + 1)
                if not first:
                    dve.wait_ge(hqT_done, t)
                v.tensor_scalar(hq, bank(7), rs, None, ALU.mult).then_inc(hq_ready, 1)

            def features(t, first):
                dve.wait_ge(F1_ready, t + 1)
                if not first:
                    dve.wait_ge(feats_done, t)
                dve.wait_ge(hb_done, t + 1)
                v.tensor_tensor(F4.rearrange("p a b -> p (a b)"), F1.rearrange("p a b -> p (a b)"), bank(6),
                                ALU.mult).then_inc(F34_ready, 1)
                dve.wait_ge(F2_ready, t + 1)
                v.tensor_tensor(F3.rearrange("p a b -> p (a b)"), F1.rearrange("p a b -> p (a b)"),
                                F2.rearrange("p a b -> p (a b)"), ALU.mult).then_inc(F34_ready, 1)

            def residual_a(t):
                dve.wait_ge(feats_done, t + 1)
                dve.wait_ge(xb_ready, t + 1)
                v.tensor_tensor(x_tile(t), x_tile(t), bank(5), ALU.add).then_inc(x1_ready, 1)
                dve.wait_ge(x1_ready, t + 1)
                row_stats(t).then_inc(stats_ready, 1)

            def stage_a(t, first=False, more=True, after=False):
                if not first:
                    attended(t - 1, after)
                    features(t - 1, after)
                keep_c(t)
                if more:
                    norm_a(t + 1, False, first)
                maxima(t, first)
                if not first:
                    residual_a(t - 1)
                exp_copies(t, first)
                if more:
                    queries(t + 1, False)
                batch_weights(t, first)

            norm_a(0, True)
            queries(0, True)
            stage_a(0, first=True)
            dve.wait_ge(x_in[1], 16)
            with dve.Fori(TX, T) as t:
                row_stats(t).then_inc(stats_ready, 1)
            finish_norm(1, T, TX, T)
            stage_a(1, after=True)
            with dve.Fori(2, T - 1) as t:
                stage_a(t)
            stage_a(T - 1, more=False)
            attended(T - 1, False)
            features(T - 1, False)
            residual_a(T - 1)
            finish_norm(2, 2 * T)

            dve.wait_ge(rows_in, 32)
            dve.wait_ge(vbd_zero, 1)

            def norm_b(t, first=False):
                if not first:
                    dve.wait_ge(h1T_done, t)
                normed(h1, t).then_inc(h1_ready, 1)

            def queries_b(t, first):
                dve.wait_ge(q_done, t + 1)
                if not first:
                    dve.wait_ge(s_done, t)
                v.tensor_tensor(qhT, bank(1).rearrange("p (m n) -> p m n", m=KD),
                                bqkc[:, 0, :].unsqueeze(2).to_broadcast([P, KD, P]), ALU.add).then_inc(q_ready, 1)

            def keys_b(t, first):
                dve.wait_ge(k_done, t + 1)
                if not first:
                    dve.wait_ge(kbd_ready, HG * t)
                v.tensor_tensor(khT, bank(2).rearrange("p (m n) -> p m n", m=KD),
                                bqkc[:, 1, :].unsqueeze(2).to_broadcast([P, KD, P]), ALU.add).then_inc(k_ready, 1)

            def values(t, first):
                dve.wait_ge(v_done, t + 1)
                if not first:
                    dve.wait_ge(av_done, t)
                for b in range(2):
                    rb = slice(S * b, S * (b + 1))
                    for e in range(2):
                        src = bank(3)[rb].rearrange("p (g e d) -> p g e d", e=2, d=HD)[:, :, e, :]
                        bias = row_a[rb].rearrange("p (g e d) -> p g e d", e=2, d=HD)[:, :, e, :]
                        v.tensor_tensor(Vbd[S * e:S * (e + 1), b, :, HD * e:HD * (e + 1)], src, bias,
                                        ALU.add).then_inc(vbd_ready, 1)

            def masked_scores(t, first):
                dve.wait_ge(s_done, t + 1)
                if not first:
                    dve.wait_ge(p_ready, t)
                v.scalar_tensor_tensor(sm, ps[:, 4:6, :].rearrange("p a (h j) -> p (a h) j", j=S), 1.0 / SCALE,
                                       causal[:, :].unsqueeze(1).to_broadcast([P, H, S]), ALU.mult, ALU.min
                                       ).then_inc(smask_ready, 1)
                dve.wait_ge(smask_ready, t + 1)
                v.tensor_reduce(rmax[:, :], sm, AX, ALU.max).then_inc(smax_ready, 1)
                dve.wait_ge(smax_ready, t + 1)
                v.tensor_tensor(sm, sm, rmax[:, :].unsqueeze(2).to_broadcast([P, H, S]), ALU.subtract
                                ).then_inc(ssub_ready, 1)

            def prob_sums(t):
                dve.wait_ge(p_ready, t + 1)
                v.tensor_reduce(rsum[:, :], prob, AX, ALU.add).then_inc(ssum_ready, 1)
                dve.wait_ge(ssum_ready, t + 1)
                v.reciprocal(rinv[:, :], rsum[:, :]).then_inc(rinv_ready, 1)

            def attended_b(t, first):
                dve.wait_ge(av_done, t + 1)
                dve.wait_ge(rinv_ready, t + 1)
                if not first:
                    dve.wait_ge(attnT_done, t)
                v.tensor_tensor(attn, bank(6).rearrange("p (h d) -> p h d", d=HD),
                                rinv[:, :].unsqueeze(2).to_broadcast([P, H, HD]), ALU.mult).then_inc(attn_ready, 1)

            def residual_b(t):
                dve.wait_ge(out_done, t + 1)
                dve.wait_ge(xb2_ready, t + 1)
                v.tensor_tensor(x_tile(t), x_tile(t), bank(7), ALU.add).then_inc(x2_ready, 1)
                dve.wait_ge(x2_ready, t + 1)
                row_stats(t).then_inc(stats_ready, 1)

            def stage_b(t, now, last, last2, first=False, second=False, more=True):
                if now:
                    queries_b(t, first)
                    if more:
                        norm_b(t + 1)
                if last2:
                    residual_b(t - 2)
                if now:
                    keys_b(t, first)
                if last:
                    prob_sums(t - 1)
                    attended_b(t - 1, second)
                if now:
                    values(t, first)
                    masked_scores(t, first)

            norm_b(0, True)
            stage_b(0, True, False, False, first=True)
            stage_b(1, True, True, False, second=True)
            with dve.Fori(2, T - 1) as t:
                stage_b(t, True, True, True)
            stage_b(T - 1, True, True, True, more=False)
            stage_b(T, False, True, True)
            stage_b(T + 1, False, False, True)
            finish_norm(3, 3 * T)

            def router(t, i, first):
                if not first:
                    dve.wait_ge(r_h2T_done, t - 1)
                normed(hs[i], t).then_inc(r_h2_ready, 1)

            def norm_c(t, first=False):
                if not first:
                    dve.wait_ge(h2T_done, t)
                normed(h2, t).then_inc(h2_ready, 1)

            def squares(t):
                for g in range(2):
                    dve.wait_ge(relu_ready, 2 * t + g + 1)
                    part = shT[:, 4 * g:4 * g + 4, :].rearrange("p a b -> p (a b)")
                    v.tensor_tensor(part, part, part, ALU.mult).then_inc(sh_ready, 1)

            def residual_c(t):
                dve.wait_ge(shared_done, t + 1)
                v.tensor_tensor(x_tile(t), x_tile(t), bank(3), ALU.add).then_inc(x3_ready, 1)

            for i in range(2):
                router(i, i, True)
            with dve.Fori(1, T // 2) as n:
                for i in range(2):
                    router(2 * n + i, i, False)
            norm_c(0, True)
            dve.wait_ge(iota_ready, 3)
            dve.wait_ge(lg_done, T)
            lg = ps[:, 4:8, :].rearrange("p a b -> p (a b)").rearrange("p (t e) -> p t e", e=P)[:, :, 0:E]

            def over_e(a):
                return a.unsqueeze(2).to_broadcast([P, T, E])

            def over_t(a):
                return a.unsqueeze(1).to_broadcast([P, T, E])

            step(v.tensor_reduce(v0, lg, AX, ALU.max))
            v.tensor_tensor(pr2, lg, over_e(v0), ALU.subtract).then_inc(rexp_in, 1)
            norm_c(1)
            dve.wait_ge(rexp_ready, 1)
            step(v.tensor_reduce(vs, pr, AX, ALU.add))
            step(v.reciprocal(vs, vs))
            step(v.tensor_tensor(pr, pr, over_e(vs), ALU.mult))
            for probs, val, arg, onehot in ((pr, v0, e0, oh0), (pr2, v1, e1, oh1)):
                if probs is pr2:
                    step(v.scalar_tensor_tensor(pr2, oh0, -2.0, pr, ALU.mult, ALU.add))
                step(v.tensor_reduce(val, probs, AX, ALU.max))
                step(v.tensor_tensor(eq, probs, over_e(val), ALU.is_equal))
                step(v.tensor_tensor(cand, eq, over_t(iota_m8), ALU.mult))
                step(v.tensor_reduce(arg, cand, AX, ALU.min))
                step(v.tensor_tensor(onehot, over_t(iota_m8), over_e(arg), ALU.is_equal))
            step(v.tensor_tensor(vs, v0, v1, ALU.add))
            step(v.reciprocal(vs, vs))
            step(v.tensor_tensor(wt0[:, :], v0, vs, ALU.mult))
            step(v.tensor_tensor(wt1[:, :], v1, vs, ALU.mult))
            v.tensor_tensor(msk, oh0, oh1, ALU.add).then_inc(msk_ready, 1)
            for i in range(2):
                normed(hs[i], i).then_inc(hs_ready, 1)
            squares(0)
            norm_c(2)
            residual_c(0)
            squares(1)
            dve.wait_ge(prefix_done, 1)
            step(v.tensor_copy(tot.rearrange("p a b -> p (a b)"), bank(5)[:, 0:T * E]))
            src, d = tot, 1
            k = 0
            while d < T:
                dst = inc[k % 2]
                step(v.tensor_copy(dst[:, 0:d, :], src[:, 0:d, :]))
                step(v.tensor_tensor(dst[:, d:T, :], src[:, d:T, :], src[:, 0:T - d, :], ALU.add))
                src, d, k = dst, 2 * d, k + 1
            step(v.tensor_copy(cnt, src[:, T - 1, :]))
            step(v.tensor_tensor(cntcmp, cnt.unsqueeze(2).to_broadcast([P, E, T]),
                                 iota_k.unsqueeze(1).to_broadcast([P, E, T]), ALU.is_gt))
            step(v.tensor_reduce(nt, cntcmp, AX, ALU.add))
            a, b, d = nt, st0, 1
            while d < E:
                step(v.tensor_copy(b[:, 0:d], a[:, 0:d]))
                step(v.tensor_tensor(b[:, d:E], a[:, d:E], a[:, 0:E - d], ALU.add))
                a, b, d = b, (st1 if b is st0 else st0), 2 * d
            ends, first_tile = a, b
            step(v.tensor_tensor(first_tile, ends, nt, ALU.subtract))
            step(v.tensor_tensor(slotm, src, tot, ALU.subtract))
            step(v.tensor_tensor(slotm, slotm, bank(4)[:, 0:T * E].rearrange("p (t e) -> p t e", e=E), ALU.add))
            step(v.scalar_tensor_tensor(slotm, over_t(first_tile), float(P), slotm, ALU.mult, ALU.add))
            for onehot, sf, si in ((oh0, s0f, slot_i[0]), (oh1, s1f, slot_i[1])):
                step(v.tensor_tensor(cand, slotm, onehot, ALU.mult))
                step(v.tensor_reduce(sf, cand, AX, ALU.add))
                step(v.tensor_copy(si[:, :], sf))
            step(v.tensor_tensor(gcmp, ends.unsqueeze(1).to_broadcast([P, GT, E]),
                                 iota_g.unsqueeze(2).to_broadcast([P, GT, E]), ALU.is_le))
            step(v.tensor_reduce(eg_f, gcmp, AX, ALU.add))
            step(v.tensor_scalar(eg_f, eg_f, float(E - 1), None, ALU.min))
            v.tensor_copy(eg_i[:, :], eg_f).then_inc(eg_ready, 1)

            def scattered_norm(n, first):
                for i in range(2):
                    t = 2 * n + i
                    if not first:
                        dve.wait_ge(scat[i], 32 * n)
                        normed(hs[i], t).then_inc(hs_ready, 1)
                    for k in range(2):
                        v.tensor_copy(idx[k][i][:, :], slot_i[k][:, bass.ds(t, 1)]).then_inc(idx_ready, 1)

            def shared(t):
                norm_c(t + 1)
                residual_c(t - 1)
                squares(t)

            scattered_norm(0, True)
            shared(2)
            with dve.Fori(3, 2 + T // 2) as t:
                scattered_norm(t - 2, False)
                shared(t)
            with dve.Fori(2 + T // 2, TA) as t:
                shared(t)
            residual_c(TA - 1)

            def experts(g, i, now, last):
                if now:
                    dve.wait_ge(irelu_ready, g + 1)
                    v.tensor_tensor(inter, inter, inter, ALU.mult).then_inc(inter_ready, 1)
                if last:
                    dve.wait_ge(y_done, g)
                    v.tensor_copy(yg[1 - i], bank(7)).then_inc(y_ready, 1)

            for s in scat:
                dve.wait_ge(s, 32 * (T // 2))
            experts(0, 0, True, False)
            experts(1, 1, True, True)
            experts(2, 0, True, True)
            with dve.Fori(1, GT // 2 - 1) as n:
                dve.wait_ge(y_out[0], 16 * n)
                experts(2 * n + 1, 1, True, True)
                dve.wait_ge(y_out[1], 16 * n)
                experts(2 * n + 2, 0, True, True)
            dve.wait_ge(y_out[0], 16 * (GT // 2 - 1))
            experts(GT - 1, 1, True, True)
            dve.wait_ge(y_out[1], 16 * (GT // 2 - 1))
            experts(GT, 0, False, True)

            def mix(t, n, i):
                dve.wait_ge(y01_in[i], 32 * (n + 1))
                for k, weight, mixed in ((0, wt0, mix0_ready), (1, wt1, mix_ready)):
                    v.scalar_tensor_tensor(x_tile(t), y01[k][i], weight[:, bass.ds(t, 1)], x_tile(t), ALU.mult, ALU.add
                                           ).then_inc(mixed, 1)
                    if k == 0:
                        dve.wait_ge(mix0_ready, t + 1)

            def last_shared(q, first=False, more=True):
                t = TA + q
                if more:
                    norm_c(t + 1)
                if first:
                    dve.wait_ge(x3_back, 16)
                else:
                    mix(4 * q - 2, q - 1, 2)
                    residual_c(t - 1)
                    mix(4 * q - 1, q - 1, 3)
                squares(t)
                for i in range(2):
                    mix(4 * q + i, q, i)

            last_shared(0, first=True)
            with dve.Fori(1, T - TA - 1) as q:
                last_shared(q)
            last_shared(T - TA - 1, more=False)
            residual_c(T - 1)
            for i in range(2):
                dve.wait_ge(x3_ready, T)
                mix(T - 2 + i, T // 4 - 1, 2 + i)

        @block.tensor
        def _(pe):
            mm = nc.tensor.matmul

            def transposes(dst, src):
                for k in range(KD):
                    last = nc.tensor.transpose(dst[:, P * k:P * (k + 1)], src[:, P * k:P * (k + 1)], ident[:, :])
                return last

            def rows(dst, lhsT, rhs):
                n = lhsT.shape[1]
                for k in range(n):
                    last = mm(dst, lhsT[:, k, :], rhs[:, k, :], start=(k == 0), stop=(k == n - 1))
                return last

            def normed_T(t, first):
                pe.wait_ge(hc_ready, t + 1)
                if not first:
                    pe.wait_ge(F1_ready, t)
                transposes(bank(4), hc).then_inc(hcT_done, 1)

            def batch_means(t):
                pe.wait_ge(bmat_ready, t + 1)
                pe.wait_ge(hc2_ready, t + 1)
                for k in range(KD):
                    last = mm(bank(6)[:, P * k:P * (k + 1)], hc2[:, P * k:P * (k + 1)], bmat, start=True, stop=True)
                last.then_inc(hb_done, 1)

            def attended_T(t, first):
                pe.wait_ge(hq_ready, t + 1)
                if not first:
                    pe.wait_ge(x1_ready, t)
                transposes(bank(5), hq).then_inc(hqT_done, 1)

            def similarities(t, first):
                pe.wait_ge(qT_ready, KD * (t + 1))
                if not first:
                    pe.wait_ge(et_act, 2 * t)
                    pe.wait_ge(et_dve, 2 * t)
                for k in range(KD):
                    for h in range(2):
                        pe.wait_ge(ctxT_in[h][k], 16 * (t + 1))
                    for n, (lo, w) in enumerate(JB):
                        for h in range(2):
                            last = mm(bank(n)[S * h:S * (h + 1), 0:w], qT[:, k, S * h:S * (h + 1)],
                                      ctxT[h][:, k, lo:lo + w], start=(k == 0), stop=(k == KD - 1))
                    last.then_inc(sim_done, 1)

            def features(t):
                pe.wait_ge(F1_ready, t + 1)
                pe.wait_ge(F2_ready, t + 1)
                pe.wait_ge(F34_ready, 2 * (t + 1))
                for f, block_T in enumerate((F1, F2, F3, F4)):
                    for k in range(KD):
                        last = mm(bank(5), block_T[:, k, :], w_qv_sb[:, KD * f + k, :],
                                  start=(f + k == 0), stop=(f == 3 and k == KD - 1))
                last.then_inc(feats_done, 1)

            def spread_max(t):
                pe.wait_ge(diag_ready, t + 1)
                mm(bank(6)[:, 0:P], ones[:, :], diag, start=True, stop=True).then_inc(mxb_done, 1)

            def exp_T(t):
                pe.wait_ge(exp_done, t + 1)
                for c in range(JC):
                    w = P if c < JM else JT
                    last = nc.tensor.transpose(bank(c // 4)[0:w, P * (c % 4):P * (c % 4 + 1)],
                                               expS[:, P * c:P * c + w], ident[:, :])
                    if c % 4 == 3 or c == JC - 1:
                        last.then_inc(et_done, 1)

            def attend(t, first):
                if not first:
                    pe.wait_ge(hq_ready, t)
                for c in range(JC):
                    w = P if c < JM else JT
                    if c == 0:
                        pe.wait_ge(et_act, 2 * t + 1)
                    if c == 4:
                        pe.wait_ge(et_dve, 2 * t + 1)
                    if c == 8:
                        pe.wait_ge(et_act, 2 * t + 2)
                    if c == 12:
                        pe.wait_ge(et_dve, 2 * t + 2)
                    if c % 3 == 0:
                        for h in range(2):
                            pe.wait_ge(ctxN_in[h][c // 3], 16 * (t + 1))
                    for h in range(2):
                        last = mm(bank(7)[S * h:S * (h + 1), :], ET[0:w, c, S * h:S * (h + 1)], ctxN[h][0:w, c, :],
                                  start=(c == 0), stop=(c == JC - 1))
                    if c % 3 == 2 or c == JC - 1:
                        last.then_inc(pv_done, 1)

            pe.wait_ge(consts_ready, 5)

            def stage_a(t, now, last, first=False, second=False, more=True):
                if last:
                    batch_means(t - 1)
                    attended_T(t - 1, second)
                if now:
                    similarities(t, first)
                if last:
                    features(t - 1)
                if now:
                    spread_max(t)
                    exp_T(t)
                    if more:
                        normed_T(t + 1, False)
                    attend(t, first)

            normed_T(0, True)
            stage_a(0, True, False, first=True)
            pe.wait_ge(wqv_in, 16)
            stage_a(1, True, True, second=True)
            with pe.Fori(2, T - 1) as t:
                stage_a(t, True, True)
            stage_a(T - 1, True, True, more=False)
            stage_a(T, False, True)

            def normed_T_b(t, first):
                pe.wait_ge(h1_ready, t + 1)
                if not first:
                    pe.wait_ge(h1T_ready, t)
                transposes(bank(0), h1).then_inc(h1T_done, 1)

            def stage_b(t, now, last, last2, first=False, more=True):
                if now:
                    pe.wait_ge(h1T_ready, t + 1)
                    if not first:
                        pe.wait_ge(q_ready, t)
                    for m in range(KD):
                        for k in range(KD):
                            mq = mm(bank(1)[:, P * m:P * (m + 1)], wq_sb[:, k, P * m:P * (m + 1)], h1T[:, k, :],
                                    start=(k == 0), stop=(k == KD - 1))
                    mq.then_inc(q_done, 1)
                if last2:
                    pe.wait_ge(attnT_ready, t - 1)
                    pe.wait_ge(pt_ready, 2 * (t - 1))
                    rows(bank(7), attnT, wm_sb).then_inc(out_done, 1)
                if now:
                    if not first:
                        pe.wait_ge(k_ready, t)
                    for m in range(KD):
                        for k in range(KD):
                            mk = mm(bank(2)[:, P * m:P * (m + 1)], wk_sb[:, k, P * m:P * (m + 1)], h1T[:, k, :],
                                    start=(k == 0), stop=(k == KD - 1))
                    mk.then_inc(k_done, 1)
                if last:
                    pe.wait_ge(p_ready, t)
                    if last2:
                        pe.wait_ge(attn_ready, t - 1)
                        pe.wait_ge(x2_ready, t - 1)
                    for g in range(H // 2):
                        mt = nc.tensor.transpose(bank(6 + g // 4)[:, P * (g % 4):P * (g % 4 + 1)],
                                                 prob[:, 2 * g:2 * g + 2, :].rearrange("p a b -> p (a b)"), ident[:, :])
                        if g % 4 == 3:
                            mt.then_inc(pt_done, 1)
                if now:
                    if not first:
                        pe.wait_ge(vbd_ready, 4 * t)
                    rows(bank(3), h1T, wv_sb).then_inc(v_done, 1)
                    if more:
                        normed_T_b(t + 1, False)
                if last:
                    pe.wait_ge(pt_ready, 2 * t)
                    pe.wait_ge(vbd_ready, 4 * t)
                    for g in range(H // 2):
                        for b in range(2):
                            ma = mm(bank(6)[S * b:S * (b + 1), 2 * HD * g:2 * HD * (g + 1)], PT[:, g, S * b:S * (b + 1)],
                                    Vbd[:, b, g, :], start=True, stop=True)
                    ma.then_inc(av_done, 1)
                if now:
                    pe.wait_ge(q_ready, t + 1)
                    pe.wait_ge(kbd_ready, HG * (t + 1))
                    if not first:
                        pe.wait_ge(smask_ready, t)
                    for m in range(KD):
                        for b in range(2):
                            ms = mm(bank(4 + m // 2)[S * b:S * (b + 1), HG * S * (m % 2):HG * S * (m % 2 + 1)],
                                    qhT[:, m, S * b:S * (b + 1)], Kbd[:, m, b, :], start=True, stop=True)
                    ms.then_inc(s_done, 1)
                if last:
                    pe.wait_ge(attn_ready, t)
                    pe.wait_ge(k_ready, t + 1 if now else T)
                    transposes(bank(2), attn.rearrange("p h d -> p (h d)")).then_inc(attnT_done, 1)

            pe.wait_ge(ln_ready, 3)
            for s in attnw_in:
                pe.wait_ge(s, 16)
            normed_T_b(0, True)
            stage_b(0, True, False, False, first=True)
            stage_b(1, True, True, False)
            with pe.Fori(2, T - 1) as t:
                stage_b(t, True, True, True)
            stage_b(T - 1, True, True, True, more=False)
            stage_b(T, False, True, True)
            stage_b(T + 1, False, False, True)

            pe.wait_ge(ln_ready, 4)
            pe.wait_ge(wr_in, 16)

            logits = ps.rearrange("p a b -> p (a b)")

            def router_T(t, i, first):
                pe.wait_ge(r_h2_ready, t + 1)
                if not first:
                    pe.wait_ge(r_h2T_ready, t - 1)
                transposes(bank(i), hs[i]).then_inc(r_h2T_done, 1)

            def router(t, i):
                pe.wait_ge(r_h2T_ready, t + 1)
                for k in range(KD):
                    last = mm(logits[:, bass.ds(4 * D + t * P, P)], h2Ts[i][:, k, :], wr_sb[:, k, :],
                              start=(k == 0), stop=(k == KD - 1))
                last.then_inc(lg_done, 1)

            router_T(0, 0, True)
            router_T(1, 1, True)
            router(0, 0)
            with pe.Fori(1, T // 2) as n:
                for i in range(2):
                    router_T(2 * n + i, i, False)
                    router(2 * n + i - 1, 1 - i)
            router(T - 1, 1)

            pe.wait_ge(ws_in, 32)

            def tokens_T_c(t, first=False):
                pe.wait_ge(h2_ready, t + 1)
                if not first:
                    pe.wait_ge(h2T_ready, t)
                transposes(bank(0), h2).then_inc(h2T_done, 1)

            def shared_first(t, i, g, first):
                if not first:
                    pe.wait_ge(sh_ready, 2 * t - 1 + g)
                for m in range(4 * g, 4 * g + 4):
                    for k in range(KD):
                        ms = mm(bank(1 + g)[:, P * (m % 4):P * (m % 4 + 1)], ws1_sb[:, k, P * m:P * (m + 1)],
                                h2Ts[i][:, k, :], start=(k == 0), stop=(k == KD - 1))
                ms.then_inc(sh_done, 1)

            def shared_second(t, first=False):
                pe.wait_ge(sh_ready, 2 * (t + 1))
                if not first:
                    pe.wait_ge(x3_ready, t)
                rows(bank(3), shT, ws2_sb).then_inc(shared_done, 1)

            def shared(t, i, last=True, first=False, second=False, more=True):
                pe.wait_ge(h2T_ready, t + 1)
                shared_first(t, i, 0, first)
                if last:
                    shared_second(t - 1, second)
                if more:
                    tokens_T_c(t + 1)
                shared_first(t, i, 1, first)

            tokens_T_c(0, first=True)
            shared(0, 0, last=False, first=True)
            shared(1, 1, second=True)
            pe.wait_ge(msk_ready, 1)
            flat = msk.rearrange("p a b -> p (a b)")
            mm(bank(4)[:, 0:T * E], earlier[:, :], flat, start=True, stop=True)
            mm(bank(5)[:, 0:T * E], ones[:, :], flat, start=True, stop=True).then_inc(prefix_done, 1)

            with pe.Fori(1, TA // 2) as n:
                for i in range(2):
                    shared(2 * n + i, i)
            shared_second(TA - 1)

            pe.wait_ge(eg_ready, 1)
            pe.wait_ge(w1_in, 16)

            def expert(g):
                return pe.value_load(eg_i[0:1, bass.ds(g, 1)], min_val=0, max_val=E - 1)

            def tokens_T(g, i, n, first=False):
                pe.wait_ge(xg_in[i], 16 * (n + 1))
                if not first:
                    pe.wait_ge(xgT_ready, g)
                transposes(bank(4), xg[i]).then_inc(xgT_done, 1)

            def experts(g, now, last, following=None, second=False):
                if last:
                    pe.wait_ge(inter_ready, g)
                    if not second:
                        pe.wait_ge(iT_ready, g - 1)
                    transposes(bank(5), inter).then_inc(iT_done, 1)
                if now:
                    e = expert(g)
                    pe.wait_ge(xgT_ready, g + 1)
                    for k in range(KD):
                        m1 = mm(bank(6), xgT[:, k, :], w1_sb[:, bass.ds(e, 1), k, :].rearrange("p o f -> p (o f)"),
                                start=(k == 0), stop=(k == KD - 1))
                    m1.then_inc(in_done, 1)
                if following is not None:
                    tokens_T(*following)
                if last:
                    e = expert(g - 1)
                    pe.wait_ge(iT_ready, g)
                    if not second:
                        pe.wait_ge(y_ready, g - 1)
                    for k in range(KD):
                        m2 = mm(bank(7), interT[:, k, :], w2_of(e, k), start=(k == 0), stop=(k == KD - 1))
                    m2.then_inc(y_done, 1)

            pe.wait_ge(w2_in, 48)

            def w2_of(e, k):
                at_e = e * (KD * D) + (e >= 6) * (ARENA - 6 * KD * D) + k * D
                return arena[:, bass.ds(at_e, D)]

            tokens_T(0, 0, 0, first=True)
            experts(0, True, False, following=(1, 1, 0))
            experts(1, True, True, following=(2, 0, 1), second=True)
            with pe.Fori(1, GT // 2 - 1) as n:
                experts(2 * n, True, True, following=(2 * n + 1, 1, n))
                experts(2 * n + 1, True, True, following=(2 * n + 2, 0, n + 1))
            experts(GT - 2, True, True, following=(GT - 1, 1, GT // 2 - 1))
            experts(GT - 1, True, True)
            experts(GT, False, True)

            shared(TA, 0, last=False)
            for t in range(TA + 1, T):
                shared(t, t % 2, more=t < T - 1)
            shared_second(T - 1)


_OUT = "out"


def kernel(x, ctx_1024, L0_xattn_w_sim, L0_xattn_b_sim, L0_xattn_W_qv, L0_xattn_b_qv, L0_attn_Wq, L0_attn_bq,
           L0_attn_Wk, L0_attn_bk, L0_attn_Wv, L0_attn_bv, L0_attn_Wm, L0_attn_bm, L0_ffn_w_router,
           L0_ffn_w1_stack, L0_ffn_w2_stack, L0_ffn_ws1, L0_ffn_ws2):
    import numpy as np
    from concourse import bacc
    from concourse.bass_utils import run_bass_kernel_spmd

    def cols(v):
        return np.asarray(v).reshape(KD, P).T

    ctx = np.asarray(ctx_1024)
    main = ctx[:, :JM * P].reshape(B, P, JM, KD, P).transpose(0, 3, 4, 2, 1).reshape(B, KD, P, JM * P)
    tail = ctx[:, JM * P:].reshape(B, JT, KD, P).transpose(0, 2, 3, 1)
    w_sim = np.asarray(L0_xattn_w_sim)
    w_r = np.zeros((D, P), np.float32)
    w_r[:, :E] = np.asarray(L0_ffn_w_router).T
    ins = {
        "x": np.asarray(x).reshape(B * S, D),
        "ctx_n": ctx,
        "ctx_t": np.concatenate([main, tail], axis=-1),
        "w1": w_sim[0:D],
        "w23": np.stack([cols(w_sim[D:2 * D]), cols(w_sim[2 * D:])], axis=1),
        "b_sim": np.asarray(L0_xattn_b_sim),
        "w_qv": np.asarray(L0_xattn_W_qv),
        "b_qv": np.asarray(L0_xattn_b_qv),
        "wq": np.asarray(L0_attn_Wq), "wk": np.asarray(L0_attn_Wk),
        "wv": np.asarray(L0_attn_Wv), "wm": np.asarray(L0_attn_Wm),
        "b_qk": np.stack([cols(L0_attn_bq), cols(L0_attn_bk)], axis=1),
        "bv": np.asarray(L0_attn_bv), "bm": np.asarray(L0_attn_bm),
        "w_router": w_r,
        "w1t": np.asarray(L0_ffn_w1_stack).transpose(0, 2, 1),
        "w2t": np.asarray(L0_ffn_w2_stack).transpose(0, 2, 1),
        "ws1t": np.asarray(L0_ffn_ws1).T,
        "ws2t": np.asarray(L0_ffn_ws2).T,
    }
    ins = {n: np.ascontiguousarray(a) for n, a in ins.items()}
    nc = bacc.Bacc("TRN2", target_bir_lowering=False, num_devices=1)
    aps = [nc.dram_tensor(n, a.shape, mybir.dt.from_np(a.dtype), kind="ExternalInput").ap() for n, a in ins.items()]
    out = nc.dram_tensor(_OUT, (B * S, D), F32, kind="ExternalOutput").ap()
    perceiver_layer(nc, *aps, out)
    r = run_bass_kernel_spmd(nc, [ins], core_ids=[0])
    return r.results[0][_OUT].reshape(B, S, D)
```

```python
from contextlib import ExitStack

import concourse.bass as bass
from concourse import mybir

F32 = mybir.dt.float32
I32 = mybir.dt.int32
U32 = mybir.dt.uint32
F32R = mybir.dt.float32r
ALU = mybir.AluOpType
ACT = mybir.ActivationFunctionType
AX = mybir.AxisListType.X

P = 128
B, S, D = 32, 64, 512
J = 1601
T = B * S // P
KD = D // P
Q = 32
NQ = P // Q
JM = J // P
JT = J - JM * P
JC = JM + 1
JB = [(c * D, min(D, J - c * D)) for c in range(-(-J // D))]
NP = 5
H, HD = 16, 32
HG = P // HD
FS = 1024
KF = FS // P
E, F = 8, 512
GT = (2 * B * S) // P + E - 1
GP = GT // 2
TR = T - 4
TX = 7
TY = (TX + T) // 2
TA = 3 * T // 4
TH = T // 2
EPS = 1e-5
SCALE = float(HD) ** 0.5
MASKED = -1.0e12
BIG = 3.0e38


def perceiver_layer(nc, x, ctx_n, ctx_t, w1, w23, b_sim, w_qv, b_qv, wq, wk, wv, wm, b_qk, bv, bm,
                    w_router, w1t, w2t, ws1t, ws2t, out):
    moe_in = nc.dram_tensor("moe_in", [GT * P, D], F32).ap()
    moe_out = nc.dram_tensor("moe_out", [GT * P, D], F32).ap()
    x3_away = nc.dram_tensor("x3_away", [TH * P, D], F32).ap()

    with ExitStack() as stack:
        def sb(name, shape, dt=F32):
            return stack.enter_context(nc.sbuf_tensor(name, shape, dt))

        def sem(name):
            return stack.enter_context(nc.semaphore(name))

        ident = sb("ident", [P, P])
        ones = sb("ones", [P, P])
        same_batch = sb("same_batch", [P, P])
        earlier = sb("earlier", [P, P])
        causal = sb("causal", [P, S])
        causal_b = sb("causal_b", [P, S])
        row_a = sb("row_a", [P, D])
        row_b = sb("row_b", [P, D])
        w23c = sb("w23c", [P, 2, KD])
        bqkc = sb("bqkc", [P, 2, KD])
        bsim = sb("bsim", [P, 1])
        lg = sb("lg", [P, T, E])
        stats = sb("stats", [P, T, 6])
        mean = sb("mean", [P, T])
        dmean = sb("dmean", [P, T])
        var = sb("var", [P, T])
        rstd = sb("rstd", [P, T])
        nmr = sb("nmr", [P, T])
        small = sb("small", [P, 12])
        hbar = sb("hbar", [P, KD, 2])
        rinv = sb("rinv", [P, H])
        rmax = sb("rmax", [P, H])
        rsum = sb("rsum", [P, H])
        wt0 = sb("wt0", [P, T])
        wt1 = sb("wt1", [P, T])
        cdot, smax, nsmax, smx, erow, rs, bmax, nbmax, bsum, ecol, brec, cnow = (
            small[:, i:i + 1] for i in range(12))

        slot_i = [sb(f"slot_i{k}", [P, T], I32) for k in range(2)]
        eg_i = sb("eg_i", [P, GT], I32)
        idx = [[sb(f"idx{k}{i}", [P, 1], I32) for i in range(4)] for k in range(2)]

        ARENA = 42528
        SPLIT = 21 * KD * P * 2
        with nc.sbuf_tensor("arena", [P, ARENA + T * D], F32) as arena:
            pass
        with nc.sbuf_tensor("raw_weights", [P, 4, KD, D], F32) as raw_weights:
            pass
        WS = 8192 + 9216 + E * KD * F
        split = sb("split", [P, SPLIT], F32R)
        sb("arena_before_ws", [P, WS - SPLIT])
        with nc.sbuf_tensor("raw_ws2", [P, KF, D], F32) as raw_ws2:
            pass
        split_ws2 = sb("split_ws2", [P, 2, KF, D], F32R)
        sb("arena_rest", [P, ARENA + T * D - WS - 2 * KF * D])
        X = arena[:, ARENA:].rearrange("p (t d) -> p t d", d=D)
        used = [0]

        def at(lo):
            used[0] = lo

        def carve(*dims):
            n = 1
            for d in dims:
                n *= d
            v = arena[:, used[0]:used[0] + n]
            used[0] += n
            if len(dims) == 2:
                v = v.rearrange("p (a b) -> p a b", b=dims[1])
            if len(dims) == 3:
                v = v.rearrange("p (a b c) -> p a b c", b=dims[1], c=dims[2])
            if len(dims) == 4:
                v = v.rearrange("p (a b c d) -> p a b c d", b=dims[1], c=dims[2], d=dims[3])
            return v

        def as_split(v):
            n = v.shape[1] * v.shape[2]
            return split[:, used[0] - n:used[0]].rearrange("p (a b) -> p a b", b=v.shape[2])

        at(0)
        ctxT = [carve(KD, J) for _ in range(2)]
        ctxN = [carve(JC, D) for _ in range(2)]
        w_qv_sb = carve(4 * KD, D)
        expS = carve(J)
        used[0] += -used[0] % 4
        ET = carve(JC, P)
        hc = carve(D)
        hc2 = carve(D)
        qT = carve(KD, P)
        hq = carve(D)
        F1, F2, F3 = (carve(KD, P) for _ in range(3))
        Wc = carve(2, D)
        diag = carve(P)
        bexp = carve(S)
        bmat = carve(P)
        end_a = used[0]
        at(0)
        w_raw = [raw_weights[:, i] for i in range(4)]
        w_lo = [as_split(carve(KD, D)) for _ in range(4)]
        h1 = [carve(D) for _ in range(2)]
        w_hi = [as_split(carve(KD, D)) for _ in range(4)]
        h1T = [as_split(carve(KD, 2 * P)) for _ in range(2)]
        attnT = [[as_split(carve(KD, P)) for _ in range(2)] for _ in range(2)]
        assert used[0] == SPLIT, used[0]
        Kbd = [carve(KD, 2, HG * S) for _ in range(2)]
        assert used[0] <= 2 * KD * J + 2 * JC * D, used[0]
        Vbd = [carve(2, H // 2, 2 * HD) for _ in range(2)]
        qhT = carve(KD, 2 * P)
        khT = carve(KD, 2 * P)
        sm = carve(H, S)
        prob = carve(H, S)
        PT = carve(H // 2, P)
        attn = carve(H, HD)
        assert used[0] <= 8192 + 9216 + E * KD * F, used[0]
        at(8192 + 9216)
        w1_sb = carve(E, KD, F)
        assert used[0] == WS
        ws1_sb = carve(KD, FS)
        ws2_sb = carve(KF, D)
        ws2_p = split_ws2[:, 1], split_ws2[:, 0]
        zero = carve(D)
        end_b = used[0]
        at(0)
        raw_ws1 = raw_weights[:, 0:2].rearrange("p a k d -> p (a k d)").rearrange("p (k n) -> p k n", n=FS)
        ws1_lo = as_split(carve(KD, FS))
        at(4 * KD * D + 2 * D)
        ws1_hi = as_split(carve(KD, FS))
        ws1_p = ws1_hi, ws1_lo
        shT_p = [as_split(carve(KF, 2 * P)) for _ in range(2)]
        h2T_p = [as_split(carve(KD, 2 * P)) for _ in range(2)]
        relu = [row_a[:, :], row_b[:, :]]
        wr_sb = zero.rearrange("p (k n) -> p k n", n=P)
        at(0)
        w2_low = carve(6, KD, D)
        w2_high = arena[:, ARENA:ARENA + TH * D].rearrange("p (e k d) -> p e k d", k=KD, d=D)
        assert TH * D == 2 * KD * D
        at(2 * KD * D)
        hs = [carve(D) for _ in range(2)]
        h2Tr = [carve(KD, P) for _ in range(2)]
        assert used[0] == 3 * KD * D, used[0]
        pr, pr2, eq, cand, oh0, oh1, msk, tot, inc0, inc1 = (carve(T, E) for _ in range(10))
        inc = [inc0, inc1]
        slotm = eq
        cntcmp = pr2.rearrange("p t e -> p (t e)").rearrange("p (e t) -> p e t", t=T)
        iota_m8 = carve(E)
        iota_k = carve(T)
        iota_g = carve(GT)
        gcmp = carve(GT, E)
        v0, v1, e0, e1, s0f, s1f, vs = (carve(T) for _ in range(7))
        nt, st0, st1, cnt = (carve(E) for _ in range(4))
        eg_f = carve(GT)
        assert used[0] <= 4 * KD * D, used[0]
        at(4 * KD * D)
        h2 = [carve(D) for _ in range(2)]
        at(6 * KD * D)
        xg = [carve(D) for _ in range(2)]
        xgT = wr_sb
        interT = carve(KD, P)
        yg = [carve(D) for _ in range(2)]
        assert used[0] <= 8192 + 9216, used[0]
        inter = row_a[:, :]
        h2_l = row_b[:, :]
        h2T_l = [xgT, interT]
        shT_l = [arena[:, lo:lo + KF * P].rearrange("p (k n) -> p k n", n=P)
                 for lo in (6 * KD * D, 6 * KD * D + 3 * D)]
        assert KF * P == 2 * D
        y01 = [[w1_sb[:, i, 2 * k, :] for i in range(4)] for k in range(2)]
        assert max(end_a, end_b) <= ARENA, (end_a, end_b)

        ps = stack.enter_context(nc.psum_tensor("ps", [P, 8, D], F32))

        def bank(i):
            return ps[:, i, :]

        late_bank = bank(6), bank(1)
        last_bank = bank(7), bank(2)

        def group_bank(p, g):
            return bank(5 if isinstance(p, int) and p == 0 and g == 2 else 1 + g)

        def logits(g):
            return bank(3 + 2 * (g % 2))

        x_in = [sem(f"x_in{i}") for i in range(2)]
        const_in, wqv_in = sem("const_in"), sem("wqv_in")
        ctxT_in = [sem(f"ctxT_in{k}") for k in range(KD)]
        ctxN_in = [sem(f"ctxN_in{q}") for q in range(NP)]
        attnw_in = sem("attnw_in")
        rows_in = sem("rows_in")
        w1_in, w2_in, wr_in = (sem(n) for n in ("w1_in", "w2_in", "wr_in"))
        pool_step, consts_ready = sem("pool_step"), sem("consts_ready")
        pool_go = sem("pool_go")
        dve_step = sem("dve_step")
        stats_ready = sem("stats_ready")
        var_ready, std_ready, ln_ready = sem("var_ready"), sem("std_ready"), sem("ln_ready")
        hc_ready, c_ready, cnow_ready, hc2_ready, xb_ready = (
            sem(n) for n in ("hc_ready", "c_ready", "cnow_ready", "hc2_ready", "xb_ready"))
        hcT_done, F1_ready, qT_ready = (sem(n) for n in ("hcT_done", "F1_ready", "qT_ready"))
        sim_done, pv_done = sem("sim_done"), sem("pv_done")
        max_ready, nmax_ready, smx_ready, diag_ready = (sem(n) for n in ("max_ready", "nmax_ready", "smx_ready", "diag_ready"))
        exp_done, et_done, et_act, et_dve = (sem(n) for n in ("exp_done", "et_done", "et_act", "et_dve"))
        rs_ready, hq_ready, hqT_done, F2_ready, F3_ready, hbar_ready, wc_ready, wc_used = (
            sem(n) for n in ("rs_ready", "hq_ready", "hqT_done", "F2_ready", "F3_ready", "hbar_ready", "wc_ready",
                             "wc_used"))
        mxb_done, bmax_ready, nbmax_ready, bexp_ready, brec_ready, bmat_ready, hb_done = (
            sem(n) for n in ("mxb_done", "bmax_ready", "nbmax_ready", "bexp_ready", "brec_ready", "bmat_ready", "hb_done"))
        feats_done, x1_ready = sem("feats_done"), sem("x1_ready")
        kbd_zero, vbd_zero = sem("kbd_zero"), sem("vbd_zero")
        w_hi_ready, w_lo_ready = sem("w_hi_ready"), sem("w_lo_ready")
        h1_ready, xb2_ready, h1T_done, h1hi_ready, h1lo_ready = (
            sem(n) for n in ("h1_ready", "xb2_ready", "h1T_done", "h1hi_ready", "h1lo_ready"))
        q_done, k_done, v_done, q_ready, k_ready, kbd_ready, vbd_ready = (
            sem(n) for n in ("q_done", "k_done", "v_done", "q_ready", "k_ready", "kbd_ready", "vbd_ready"))
        s_done, smask_ready, smax_ready, ssub_ready, p_ready, ssum_ready, rinv_ready = (
            sem(n) for n in ("s_done", "smask_ready", "smax_ready", "ssub_ready", "p_ready", "ssum_ready", "rinv_ready"))
        pt_done, pt_ready, av_done, attn_ready, attnT_done, ahi_ready, alo_ready, out_done, x2_ready = (
            sem(n) for n in ("pt_done", "pt_ready", "av_done", "attn_ready", "attnT_done", "ahi_ready",
                             "alo_ready", "out_done", "x2_ready"))
        zero_ready, slots_zeroed, iota_ready = sem("zero_ready"), sem("slots_zeroed"), sem("iota_ready")
        r_h2_ready, r_h2T_done, r_h2T_ready, lg_done = (
            sem(n) for n in ("r_h2_ready", "r_h2T_done", "r_h2T_ready", "lg_done"))
        lg_read = sem("lg_read")
        rexp_in, rexp_ready, msk_ready, prefix_done, prefix_read, eg_ready = (
            sem(n) for n in ("rexp_in", "rexp_ready", "msk_ready", "prefix_done", "prefix_read", "eg_ready"))
        hs_ready, idx_ready, scat = sem("hs_ready"), sem("idx_ready"), [sem(f"scattered{i}") for i in range(2)]
        ws1_split, ws2_split, wsl_in = sem("ws1_split"), sem("ws2_split"), sem("wsl_in")
        ws1_in, ws2_in = sem("ws1_in"), sem("ws2_in")
        h2_ready, h2T_done, h2hi_ready, h2lo_ready, sh_done, relu_ready, sq_ready, shhi_ready, shlo_ready = (
            sem(n) for n in ("h2_ready", "h2T_done", "h2hi_ready", "h2lo_ready", "sh_done", "relu_ready", "sq_ready",
                             "shhi_ready", "shlo_ready"))
        lT_done, lT_ready, lsh_done, lrelu_ready, lsh_ready = (
            sem(n) for n in ("lT_done", "lT_ready", "lsh_done", "lrelu_ready", "lsh_ready"))
        shared_done, x3_ready = sem("shared_done"), sem("x3_ready")
        x3_out, x3_back = [sem(f"x3_out{i}") for i in range(2)], sem("x3_back")
        xg_in = [sem(f"xg_in{i}") for i in range(2)]
        xgT_ready, in_done, irelu_ready, inter_ready, iT_done, iT_ready, y_done, y_ready = (
            sem(n) for n in ("xgT_ready", "in_done", "irelu_ready", "inter_ready", "iT_done", "iT_ready",
                             "y_done", "y_ready"))
        y_out = [sem(f"y_out{i}") for i in range(2)]
        gidx_ready, y01_in = sem("gidx_ready"), [sem(f"y01_in{i}") for i in range(4)]
        mix0_ready, mix_ready, out_sem = sem("mix0_ready"), sem("mix_ready"), sem("out_sem")

        x_v = x.rearrange("(t p) d -> p t d", p=P)
        out_v = out.rearrange("(t p) d -> p t d", p=P)

        block = stack.enter_context(nc.Block())

        @block.sync
        def _(sp):
            sp.dma_start(X[:, 0:1, :], x_v[:, 0:1, :]).then_inc(x_in[0], 16)
            sp.dma_start(w23c[:, :, :], w23).then_inc(const_in, 16)
            sp.dma_start(bsim[:, :], b_sim.partition_broadcast(P)).then_inc(const_in, 16)
            sp.dma_start(row_a[:, :], w1.partition_broadcast(P)).then_inc(const_in, 16)

            def load_ctx_T(t, first):
                for k in range(KD):
                    if not first:
                        sp.wait_ge(sim_done, KD * t + (k + 1 - KD))
                    for h in range(2):
                        src = ctx_t[bass.ds(2 * t + h, 1), k].rearrange("o p n -> p (o n)")
                        sp.dma_start(ctxT[h][:, k, :], src).then_inc(ctxT_in[k], 16)

            def load_ctx_N(t, first):
                for q in range(NP):
                    if not first:
                        sp.wait_ge(pv_done, NP * t + (q + 1 - NP))
                    for h in range(2):
                        one = ctx_n[bass.ds(2 * t + h, 1)].rearrange("o j d -> (o j) d")
                        if q < NP - 1:
                            n = JM // (NP - 1)
                            main = one[0:JM * P].rearrange("(p c) d -> p c d", c=JM)
                            sp.dma_start(ctxN[h][:, n * q:n * (q + 1), :],
                                         main[:, n * q:n * (q + 1), :]).then_inc(ctxN_in[q], 16)
                        else:
                            sp.dma_start(ctxN[h][0:JT, JM, :], one[JM * P:J]).then_inc(ctxN_in[q], 16)

            load_ctx_T(0, True)
            sp.dma_start(X[:, 1:TX, :], x_v[:, 1:TX, :]).then_inc(rows_in, 16)
            sp.dma_start(row_b[:, :], b_qv.partition_broadcast(P)).then_inc(rows_in, 16)
            sp.dma_start(bqkc[:, :, :], b_qk).then_inc(rows_in, 16)
            load_ctx_N(0, True)
            sp.dma_start(w_qv_sb, w_qv.rearrange("(k p) n -> p k n", p=P)).then_inc(wqv_in, 16)
            for t in range(1, TX - 1):
                load_ctx_T(t, False)
                if t == TX - 3:
                    sp.dma_start(X[:, TX:TY, :], x_v[:, TX:TY, :]).then_inc(x_in[0], 16)
                if t == TX - 2:
                    sp.dma_start(X[:, TY:T, :], x_v[:, TY:T, :]).then_inc(x_in[1], 16)
                load_ctx_N(t, False)
            with sp.Fori(TX - 1, T) as t:
                load_ctx_T(t, False)
                load_ctx_N(t, False)
            sp.wait_ge(sim_done, KD * (T))
            for dst, src in zip(w_raw, (wq, wk, wv, wm)):
                sp.dma_start(dst, src.rearrange("(k p) n -> p k n", p=P)).then_inc(attnw_in, 16)
            sp.wait_ge(c_ready, T)
            sp.dma_start(row_a[:, :], bv.partition_broadcast(P)).then_inc(rows_in, 16)
            sp.wait_ge(xb_ready, T)
            sp.dma_start(row_b[:, :], bm.partition_broadcast(P)).then_inc(rows_in, 16)
            sp.wait_ge(feats_done, T)
            sp.dma_start(raw_ws2[:, :, :], ws2t.rearrange("(k p) n -> p k n", p=P)).then_inc(ws2_in, 16)
            sp.wait_ge(zero_ready, 1)
            for q in range(3):
                n = GT // 3
                dst = moe_in.rearrange("(g p) d -> p g d", p=P)[:, n * q:n * (q + 1), :]
                sp.dma_start(dst, zero.unsqueeze(1).to_broadcast([P, n, D])).then_inc(slots_zeroed, 16)
            sp.wait_ge(slots_zeroed, 48)
            sp.dma_start(wr_sb[:, :, :], w_router.rearrange("(k p) n -> p k n", p=P)).then_inc(wr_in, 16)
            sp.wait_ge(k_done, T)
            sp.dma_start(raw_ws1, ws1t.rearrange("(k p) n -> p k n", p=P)).then_inc(ws1_in, 16)
            sp.wait_ge(out_done, T)
            w1v = w1t.rearrange("e (k p) n -> p e k n", p=P)
            w2v = w2t.rearrange("e (k p) n -> p e k n", p=P)
            sp.dma_start(w1_sb[:, 1:E], w1v[:, 1:E]).then_inc(w1_in, 16)
            away = x3_away.rearrange("(t p) d -> p t d", p=P)
            for i in range(2):
                r = slice(TH // 2 * i, TH // 2 * (i + 1))
                sp.wait_ge(x3_ready, TH // 2 * (i + 1))
                sp.dma_start(away[:, r, :], X[:, r, :]).then_inc(x3_out[i], 16)
                sp.wait_ge(x3_out[i], 16)
                sp.dma_start(w2_high[:, i:i + 1], w2v[:, 6 + i:7 + i]).then_inc(w2_in, 16)
                if i == 0:
                    sp.wait_ge(eg_ready, 1)
                    sp.dma_start(w2_low[:, 3:4], w2v[:, 3:4]).then_inc(w2_in, 16)
            sp.wait_ge(sh_done, 4 * (TA // 2))
            sp.dma_start(w1_sb[:, 0:1], w1v[:, 0:1]).then_inc(w1_in, 16)
            for i in range(2):
                sp.wait_ge(scat[i], 32 * (T // 2))

            def load_slots(g, i):
                for b in range(NQ):
                    sp.dma_start(xg[i][Q * b:Q * (b + 1), :].rearrange("q (a n) -> q a n", a=NQ),
                                 moe_in[bass.ds(g * P, P), P * b:P * (b + 1)].rearrange("(a q) n -> q a n", a=NQ)
                                 ).then_inc(xg_in[i], 16)

            def store_slots(g, i):
                sp.wait_ge(y_ready, g + 1)
                sp.dma_start(moe_out[bass.ds(g * P, P), :], yg[i]).then_inc(y_out[i], 16)

            load_slots(0, 0)
            load_slots(1, 1)
            sp.dma_start(w2_low[:, 0:2], w2v[:, 0:2]).then_inc(w2_in, 16)
            sp.dma_start(w2_low[:, 4:6], w2v[:, 4:6]).then_inc(w2_in, 16)
            sp.dma_start(w2_low[:, 2:3], w2v[:, 2:3]).then_inc(w2_in, 16)

            def slots(g, i, first=False):
                sp.wait_ge(xgT_ready, g + 1)
                load_slots(g + 2, i)
                if not first:
                    store_slots(g - 1, 1 - i)

            slots(0, 0, first=True)
            slots(1, 1)
            sp.wait_ge(shared_done, TA)
            for lo, hi, dst, src in ((1, 1 + KD, ws1_sb, ws1t), (1 + KD, 1 + KD + KF, ws2_sb, ws2t)):
                with sp.Fori(lo, hi) as n:
                    for i in range(2):
                        slots(2 * n + i, i)
                    k = bass.ds(n - lo, 1)
                    sp.dma_start(dst[:, k, :], src.rearrange("(k p) n -> p k n", p=P)[:, k, :]).then_inc(wsl_in, 16)
            with sp.Fori(1 + KD + KF, GP - 1) as n:
                for i in range(2):
                    slots(2 * n + i, i)
            slots(GT - 3, 0)
            for g in range(GT - 3, GT):
                store_slots(g, g % 2)
            sp.dma_start(X[:, 0:TH, :], x3_away.rearrange("(t p) d -> p t d", p=P)).then_inc(x3_back, 16)
            with sp.Fori(0, T - 2) as t:
                sp.wait_ge(mix_ready, t + 1)
                sp.dma_start(out_v[:, bass.ds(t, 1), :], X[:, bass.ds(t, 1), :]).then_inc(out_sem, 16)
            for t in (T - 2, T - 1):
                sp.wait_ge(mix_ready, t + 1)
                sp.wait_ge(x3_ready, t + 1)
                sp.dma_start(out_v[:, t:t + 1, :], X[:, t:t + 1, :]).then_inc(out_sem, 16)
            sp.wait_ge(out_sem, 16 * T)

        @block.gpsimd
        def _(pool):
            nc.gpsimd.memset(ident[:, :], 0.0).then_inc(pool_step, 1)
            nc.gpsimd.memset(earlier[:, :], 1.0).then_inc(pool_step, 1)
            nc.gpsimd.memset(causal[:, :], BIG).then_inc(pool_step, 1)
            nc.gpsimd.memset(causal_b[:, :], BIG).then_inc(pool_step, 1)
            nc.gpsimd.memset(ones[:, :], 1.0).then_inc(consts_ready, 1)
            pool.wait_ge(pool_step, 4)
            nc.gpsimd.affine_select(out=ident[:, :], in_=ident[:, :], compare_op=ALU.not_equal, fill=1.0, base=0,
                                    pattern=[[-1, P]], channel_multiplier=1).then_inc(consts_ready, 1)
            nc.gpsimd.affine_select(out=earlier[:, :], in_=earlier[:, :], compare_op=ALU.is_gt, fill=0.0, base=0,
                                    pattern=[[1, P]], channel_multiplier=-1).then_inc(consts_ready, 1)
            nc.gpsimd.affine_select(out=causal[:, :], in_=causal[:, :], compare_op=ALU.is_ge, fill=MASKED, base=0,
                                    pattern=[[-1, S]], channel_multiplier=1).then_inc(consts_ready, 1)
            nc.gpsimd.affine_select(out=causal_b[:, :], in_=causal_b[:, :], compare_op=ALU.is_ge, fill=MASKED,
                                    base=-S, pattern=[[-1, S]], channel_multiplier=1).then_inc(consts_ready, 1)

            def copies(t, first):
                pool.wait_ge(hc_ready, t + 1)
                if not first:
                    pool.wait_ge(hb_done, t)
                xt = X[:, bass.ds(t, 1), :].rearrange("p o d -> p (o d)")
                nc.gpsimd.tensor_tensor(xt, xt, row_b[:, :], ALU.add).then_inc(xb_ready, 1)
                nc.gpsimd.tensor_copy(hc2, hc).then_inc(hc2_ready, 1)

            pool.wait_ge(rows_in, 48)
            copies(0, True)
            with pool.Fori(1, T) as t:
                copies(t, False)
            pool.wait_ge(pv_done, NP * (T))
            for i in range(2):
                nc.gpsimd.memset(Kbd[i], 0.0).then_inc(kbd_zero, 1)
            pool.wait_ge(feats_done, T)
            for i in range(2):
                nc.gpsimd.memset(Vbd[i], 0.0).then_inc(vbd_zero, 1)
            nc.gpsimd.memset(zero, 0.0).then_inc(zero_ready, 1)
            pool.wait_ge(rows_in, 80)

            def add_bm(t):
                pool.wait_ge(h1_ready, t + 1)
                xt = X[:, bass.ds(t, 1), :].rearrange("p o d -> p (o d)")
                nc.gpsimd.tensor_tensor(xt, xt, row_b[:, :], ALU.add).then_inc(xb2_ready, 1)

            def split_weights(lo, hi, raw, loaded, done):
                pool.wait_ge(loaded, 16)
                nc.gpsimd.tensor_copy(hi, raw).then_inc(done, 1)
                pool.wait_ge(done, 1)
                nc.gpsimd.tensor_tensor(lo, raw, hi.bitcast(F32), ALU.subtract).then_inc(done, 1)

            with pool.Fori(0, T // 4) as t:
                add_bm(t)
            split_weights(ws2_p[1], ws2_p[0], raw_ws2[:, :, :], ws2_in, ws2_split)
            with pool.Fori(T // 4, T) as t:
                add_bm(t)
            split_weights(ws1_lo, ws1_hi, raw_ws1, ws1_in, ws1_split)
            pool.wait_ge(out_done, T)
            nc.gpsimd.iota(iota_m8, pattern=[[1, E]], base=-E, channel_multiplier=0,
                           allow_small_or_imprecise_dtypes=True).then_inc(iota_ready, 1)
            nc.gpsimd.iota(iota_k, pattern=[[P, T]], base=0, channel_multiplier=0,
                           allow_small_or_imprecise_dtypes=True).then_inc(iota_ready, 1)
            nc.gpsimd.iota(iota_g, pattern=[[1, GT]], base=0, channel_multiplier=0,
                           allow_small_or_imprecise_dtypes=True).then_inc(iota_ready, 1)
            with pool.Fori(0, T // 2) as n:
                for i in range(2):
                    pool.wait_ge(hs_ready, 2 * n + i + 1)
                    pool.wait_ge(idx_ready, 4 * n + 2 * i + 2)
                    pool.wait_ge(slots_zeroed, 48)
                    pool.sem_inc(pool_go, 1)
                    for k in range(2):
                        nc.gpsimd.indirect_dma_start(
                            moe_in, bass.IndirectOffsetOnAxis(ap=idx[k][i][:, :], axis=0), hs[i], None
                        ).then_inc(scat[i], 16)
            pool.wait_ge(y_out[0], 16 * (GP + 1))
            pool.wait_ge(y_out[1], 16 * GP)

            def gather(n, i, first):
                if not first:
                    pool.wait_ge(mix_ready, 4 * (n - 1) + i + 1)
                    pool.sem_inc(pool_go, 1)
                for k in range(2):
                    nc.gpsimd.tensor_copy(idx[k][i][:, :], slot_i[k][:, bass.ds(4 * n + i, 1)]).then_inc(gidx_ready, 1)
                pool.wait_ge(gidx_ready, 8 * n + 2 * i + 2)
                pool.sem_inc(pool_go, 1)
                for k in range(2):
                    nc.gpsimd.indirect_dma_start(
                        y01[k][i], None, moe_out, bass.IndirectOffsetOnAxis(ap=idx[k][i][:, :], axis=0)
                    ).then_inc(y01_in[i], 16)

            for i in range(4):
                gather(0, i, True)
            with pool.Fori(1, T // 4) as n:
                for i in range(4):
                    gather(n, i, False)

        @block.scalar
        def _(act):
            def copy(o, i):
                return nc.scalar.activation(o, i, ACT.Copy)

            def sqrt_of_var(s, lo=0, hi=T):
                act.wait_ge(var_ready, s + 1)
                nc.scalar.activation(var[:, lo:hi], var[:, lo:hi], ACT.Sqrt).then_inc(std_ready, 1)

            def exp_scores(t, first):
                act.wait_ge(nmax_ready, t + 1)
                if not first:
                    act.wait_ge(et_done, 4 * t)
                    act.wait_ge(rs_ready, t)
                nc.scalar.activation(expS, ps[:, 0:4, :].rearrange("p a b -> p (a b)")[:, 0:J], ACT.Exp,
                                     bias=nsmax, accum_out=erow).then_inc(exp_done, 1)

            def after_scores(t, first, tail=True):
                if not first:
                    act.wait_ge(feats_done, t)
                act.wait_ge(hcT_done, t + 1)
                copy(F1.rearrange("p a b -> p (a b)"), bank(4)).then_inc(F1_ready, 1)
                for g in (0, 2):
                    act.wait_ge(et_done, 4 * t + g + 1)
                    if not first and g == 0:
                        act.wait_ge(pv_done, NP * (t))
                    copy(ET[:, 4 * g:4 * g + 4, :].rearrange("p a b -> p (a b)"), bank(g)).then_inc(et_act, 1)
                if first:
                    sqrt_of_var(1, 1, TX)
                act.wait_ge(nbmax_ready, t + 1)
                if not first:
                    act.wait_ge(bmat_ready, t)
                for h in range(2):
                    r = slice(S * h, S * (h + 1))
                    nc.scalar.activation(bexp[r, :],
                                         bank(6)[r, S * h:S * (h + 1)], ACT.Exp, bias=nbmax[r, :],
                                         accum_out=bsum[r, :]).then_inc(bexp_ready, 1)
                nc.scalar.activation(ecol, smx, ACT.Exp, bias=nbmax).then_inc(bexp_ready, 1)
                if tail:
                    attended_copy(t)

            def attended_copy(t):
                act.wait_ge(hqT_done, t + 1)
                copy(F2.rearrange("p a b -> p (a b)"), bank(5)).then_inc(F2_ready, 1)

            sqrt_of_var(0, 0, 1)
            exp_scores(0, True)
            after_scores(0, True)
            with act.Fori(1, TX - 2) as t:
                exp_scores(t, False)
                after_scores(t, False)
            exp_scores(TX - 2, False)
            after_scores(TX - 2, False, tail=False)
            sqrt_of_var(2, TX, T)
            attended_copy(TX - 2)
            with act.Fori(TX - 1, T - 1) as t:
                exp_scores(t, False)
                after_scores(t, False)
            exp_scores(T - 1, False)
            after_scores(T - 1, False, tail=False)

            def round_weights(i):
                act.wait_ge(attnw_in, 64)
                nc.scalar.activation(w_hi[i], w_raw[i], ACT.Copy).then_inc(w_hi_ready, 1)

            sqrt_of_var(3, 0, T - 1)
            attended_copy(T - 1)
            round_weights(0)
            act.wait_ge(pv_done, NP * T)

            def h1_high(t, i, n):
                act.wait_ge(h1T_done, t + 1)
                if n is not None:
                    act.wait_ge(v_done, 2 * n)
                nc.scalar.activation(h1T[0][:, :, P * i:P * (i + 1)],
                                     bank(i).rearrange("p (k n) -> p k n", n=P), ACT.Copy).then_inc(h1hi_ready, 1)

            def attn_high(t, i, first):
                act.wait_ge(attnT_done, t + 1)
                if not first:
                    act.wait_ge(out_done, t - 1)
                nc.scalar.activation(attnT[i][0], bank(0).rearrange("p (k n) -> p k n", n=P),
                                     ACT.Copy).then_inc(ahi_ready, 1)

            def keys(t, i, n, first):
                act.wait_ge(k_ready, 2 * (n + 1))
                if not first:
                    act.wait_ge(s_done, t - 1)
                for h in range(HG):
                    r = slice(HD * h, HD * (h + 1))
                    copy(Kbd[i][r, :, :, S * h:S * (h + 1)],
                         khT[r, :, P * i:P * (i + 1)].rearrange("p m (b j) -> p m b j", b=2)).then_inc(kbd_ready, 1)

            def pt_copy(t, first):
                for g in range(2):
                    act.wait_ge(pt_done, 2 * t + g + 1)
                    if not first and g == 0:
                        act.wait_ge(av_done, t)
                    copy(PT[:, 4 * g:4 * g + 4, :].rearrange("p a b -> p (a b)"), bank(6 + g)).then_inc(pt_ready, 1)

            def exp_probs(t, first):
                act.wait_ge(ssub_ready, t + 1)
                if not first:
                    act.wait_ge(pt_done, 2 * t)
                    act.wait_ge(ssum_ready, t)
                nc.scalar.activation(prob.rearrange("p a b -> p (a b)"), sm.rearrange("p a b -> p (a b)"),
                                     ACT.Exp).then_inc(p_ready, 1)

            def stage_b(n, now, last, first=False, second=False, more=True):
                a = 2 * n
                if last:
                    pt_copy(a - 2, second)
                    exp_probs(a - 1, False)
                    attn_high(a - 2, 0, second)
                    pt_copy(a - 1, False)
                if now:
                    keys(a, 0, n, first)
                    keys(a + 1, 1, n, first)
                if now and not more:
                    sqrt_of_var(5, 0, TR)
                if last:
                    attn_high(a - 1, 1, second)
                if more:
                    h1_high(a + 2, 0, n + 1)
                    h1_high(a + 3, 1, n + 1)
                if now:
                    exp_probs(a, first)

            h1_high(0, 0, None)
            h1_high(1, 1, None)
            for i in range(1, 4):
                round_weights(i)
            act.wait_ge(kbd_zero, 2)
            stage_b(0, True, False, first=True)
            sqrt_of_var(4, T - 1, T)
            stage_b(1, True, True, second=True)
            with act.Fori(2, T // 2 - 1) as n:
                stage_b(n, True, True)
            def router(t, i, first, source=None):
                act.wait_ge(r_h2T_done, t + 1)
                if not first:
                    act.wait_ge(lg_done, t - 1)
                copy(h2Tr[i].rearrange("p a b -> p (a b)"), source or bank(1 + i)).then_inc(r_h2T_ready, 1)

            stage_b(T // 2 - 1, True, True, more=False)
            for i in range(2):
                router(i, i, True)
            pt_copy(T - 2, False)
            exp_probs(T - 1, False)
            for i in range(2):
                router(2 + i, i, False)
            attn_high(T - 2, 0, False)
            pt_copy(T - 1, False)
            for i in range(2):
                router(4 + i, i, False)
            attn_high(T - 1, 1, False)

            def h2_high(p, i, first):
                act.wait_ge(h2T_done, 2 * p + i + 1)
                if not first:
                    act.wait_ge(sh_done, 4 * p)
                nc.scalar.activation(h2T_p[0][:, :, P * i:P * (i + 1)],
                                     bank(7 * i).rearrange("p (k n) -> p k n", n=P), ACT.Copy).then_inc(h2hi_ready, 1)

            def relu_of(p, g, first=False):
                act.wait_ge(sh_done, 4 * p + g + 1)
                if not first:
                    act.wait_ge(shlo_ready, 4 * p + g - 1)
                nc.scalar.activation(relu[g % 2], group_bank(p, g), ACT.Relu).then_inc(relu_ready, 1)

            def shared_high(p, g, first):
                act.wait_ge(sq_ready, 4 * p + g + 1)
                if not first and g == 0:
                    act.wait_ge(shared_done, 2 * p)
                nc.scalar.activation(shT_p[0][:, 2 * g:2 * g + 2, :].rearrange("p a b -> p (a b)"), relu[g % 2],
                                     ACT.Copy).then_inc(shhi_ready, 1)

            def shared(p, more=True):
                relu_of(p, 0)
                relu_of(p, 1)
                if more:
                    for i in range(2):
                        h2_high(p + 1, i, False)
                shared_high(p, 0, False)
                relu_of(p, 2)
                shared_high(p, 1, False)
                relu_of(p, 3)
                shared_high(p, 2, False)
                shared_high(p, 3, False)

            with act.Fori(3, TR // 2 - 1) as n:
                for i in range(2):
                    router(2 * n + i, i, False)
            for i in range(2):
                h2_high(0, i, True)
            for i in range(2):
                router(TR - 2 + i, i, False)
            sqrt_of_var(6, TR, T)
            relu_of(0, 0, True)
            relu_of(0, 1, True)
            shared_high(0, 0, True)
            relu_of(0, 2)
            shared_high(0, 1, True)
            for i in range(2):
                h2_high(1, i, False)
            for t in range(TR, T):
                router(t, t % 2, False, late_bank[t % 2])
            relu_of(0, 3)
            shared_high(0, 2, True)
            shared_high(0, 3, True)
            act.wait_ge(rexp_in, 1)
            nc.scalar.activation(pr.rearrange("p a b -> p (a b)"), pr2.rearrange("p a b -> p (a b)"),
                                 ACT.Exp).then_inc(rexp_ready, 1)
            with act.Fori(1, TA // 2 - 1) as p:
                shared(p)
            shared(TA // 2 - 1, more=False)

            def experts(g, now, last):
                if last:
                    act.wait_ge(iT_done, g)
                    copy(interT.rearrange("p a b -> p (a b)"), bank(1)).then_inc(iT_ready, 1)
                if now:
                    act.wait_ge(in_done, g + 1)
                    if not last:
                        act.wait_ge(shlo_ready, 4 * (TA // 2) - 1)
                    nc.scalar.activation(inter, bank(2), ACT.Relu).then_inc(irelu_ready, 1)

            experts(0, True, False)
            with act.Fori(1, GT) as g:
                experts(g, True, True)

            def last_T(u):
                act.wait_ge(lT_done, u + 1)
                if u >= 2:
                    act.wait_ge(lsh_done, 2 * (u - 1))
                copy(h2T_l[u % 2].rearrange("p a b -> p (a b)"), bank(4)).then_inc(lT_ready, 1)

            last_T(0)
            experts(GT, False, True)
            for u in range(T - TA):
                for g in range(2):
                    act.wait_ge(lsh_done, 2 * u + g + 1)
                    if u == 1 and g == 0:
                        act.wait_ge(y_out[0], 16 * (GP + 1))
                        act.wait_ge(y_out[1], 16 * GP)
                    if u >= 2 and g == 0:
                        act.wait_ge(shared_done, TA + u - 1)
                    nc.scalar.activation(shT_l[u % 2][:, 4 * g:4 * g + 4, :].rearrange("p a b -> p (a b)"),
                                         bank(5 + g), ACT.Relu).then_inc(lrelu_ready, 1)
                    if g == 0 and u < T - TA - 1:
                        last_T(u + 1)

        @block.vector
        def _(dve):
            v = nc.vector
            chain = [0]

            def step(ins):
                chain[0] += 1
                ins.then_inc(dve_step, 1)
                dve.wait_ge(dve_step, chain[0])

            def finish_norm(s, count, lo=0, hi=T):
                r = slice(lo, hi)
                dve.wait_ge(stats_ready, count)
                step(v.tensor_tensor(mean[:, r], stats[:, r, 1], stats[:, r, 4], ALU.add))
                step(v.tensor_scalar(mean[:, r], mean[:, r], 0.5, None, ALU.mult))
                step(v.tensor_tensor(dmean[:, r], stats[:, r, 1], stats[:, r, 4], ALU.subtract))
                step(v.tensor_tensor(dmean[:, r], dmean[:, r], dmean[:, r], ALU.mult))
                step(v.tensor_tensor(var[:, r], stats[:, r, 2], stats[:, r, 5], ALU.add))
                step(v.scalar_tensor_tensor(var[:, r], dmean[:, r], D / 4.0, var[:, r], ALU.mult, ALU.add))
                v.tensor_scalar(var[:, r], var[:, r], 1.0 / D, EPS, ALU.mult, ALU.add).then_inc(var_ready, 1)
                dve.wait_ge(std_ready, s + 1)
                step(v.reciprocal(rstd[:, r], var[:, r]))
                v.scalar_tensor_tensor(nmr[:, r], mean[:, r], -1.0, rstd[:, r], ALU.mult, ALU.mult
                                       ).then_inc(ln_ready, 1)
                dve.wait_ge(ln_ready, s + 1)

            def x_tile(t):
                return X[:, bass.ds(t, 1), :].rearrange("p o d -> p (o d)")

            def normed(o, t):
                return v.tensor_scalar(o, x_tile(t), rstd[:, bass.ds(t, 1)], nmr[:, bass.ds(t, 1)], ALU.mult, ALU.add)

            def row_stats(t):
                return v.bn_stats(stats[:, bass.ds(t, 1), :].rearrange("p o s -> p (o s)"), x_tile(t))

            dve.wait_ge(x_in[0], 16)
            row_stats(0).then_inc(stats_ready, 1)
            finish_norm(0, 1, 0, 1)
            dve.wait_ge(const_in, 48)
            dve.wait_ge(consts_ready, 5)

            step(v.memset(same_batch[:, :], 0.0))
            for h in range(2):
                r = slice(S * h, S * (h + 1))
                step(v.memset(same_batch[r, r], 1.0))
            step(v.tensor_copy(causal[S:P, :], causal_b[S:P, :]))

            def norm_a(t, first, second=False):
                if not first:
                    dve.wait_ge(hcT_done, t)
                    dve.wait_ge(hc2_ready, t)
                normed(hc, t).then_inc(hc_ready, 1)
                if not first and not second:
                    dve.wait_ge(et_done, 4 * (t - 1))
                dve.wait_ge(hc_ready, t + 1)
                v.scalar_tensor_tensor(expS[:, 0:D], hc, 1.0, row_a[:, :], ALU.mult, ALU.mult,
                                       accum_out=cdot).then_inc(c_ready, 1)

            def keep_c(t):
                dve.wait_ge(c_ready, t + 1)
                v.tensor_copy(cnow, cdot).then_inc(cnow_ready, 1)
                dve.wait_ge(cnow_ready, t + 1)

            def queries(t, first):
                dve.wait_ge(hcT_done, t + 1)
                if not first:
                    dve.wait_ge(sim_done, KD * (t))
                for k in range(KD):
                    v.tensor_scalar(qT[:, k, :], bank(4)[:, P * k:P * (k + 1)], w23c[:, 1, k:k + 1],
                                    w23c[:, 0, k:k + 1], ALU.mult, ALU.add).then_inc(qT_ready, 1)

            def maxima(t, first):
                dve.wait_ge(sim_done, KD * (t + 1))
                if not first:
                    dve.wait_ge(exp_done, t)
                    dve.wait_ge(bexp_ready, 3 * t)
                    dve.wait_ge(mxb_done, t)
                v.reduce_max(smax, ps[:, 0:4, :].rearrange("p a b -> p (a b)")[:, 0:J], AX).then_inc(max_ready, 1)
                dve.wait_ge(max_ready, t + 1)
                v.tensor_scalar(nsmax, smax, -1.0, None, ALU.mult).then_inc(nmax_ready, 1)
                v.scalar_tensor_tensor(smx, smax, cnow, bsim[:, :], ALU.add, ALU.add).then_inc(smx_ready, 1)
                dve.wait_ge(smx_ready, t + 1)
                v.tensor_scalar(diag, ident[:, :], smx, None, ALU.mult).then_inc(diag_ready, 1)

            def batch_weights(t, first):
                dve.wait_ge(mxb_done, t + 1)
                if not first:
                    dve.wait_ge(bexp_ready, 3 * t)
                for h in range(2):
                    r = slice(S * h, S * (h + 1))
                    v.reduce_max(bmax[r, :], bank(6)[r, S * h:S * (h + 1)], AX).then_inc(bmax_ready, 1)
                dve.wait_ge(bmax_ready, 2 * (t + 1))
                v.tensor_scalar(nbmax, bmax, -1.0, None, ALU.mult).then_inc(nbmax_ready, 1)
                dve.wait_ge(bexp_ready, 3 * (t + 1))
                if not first:
                    dve.wait_ge(hb_done, t)
                v.reciprocal(brec, bsum).then_inc(brec_ready, 1)
                dve.wait_ge(brec_ready, t + 1)
                v.tensor_scalar(bmat, same_batch[:, :], ecol, brec, ALU.mult, ALU.mult).then_inc(bmat_ready, 1)

            def exp_copies(t, first):
                for g in (1, 3):
                    dve.wait_ge(et_done, 4 * t + g + 1)
                    if not first and g == 1:
                        dve.wait_ge(pv_done, NP * (t))
                    if g == 1:
                        v.tensor_copy(ET[:, 4:8, :].rearrange("p a b -> p (a b)"), bank(1)).then_inc(et_dve, 1)
                    else:
                        v.tensor_copy(ET[0:JT, JM, :], bank(3)[0:JT, 0:P]).then_inc(et_dve, 1)

            def attended(t, first):
                dve.wait_ge(exp_done, t + 1)
                v.reciprocal(rs, erow).then_inc(rs_ready, 1)
                dve.wait_ge(pv_done, NP * (t + 1))
                dve.wait_ge(rs_ready, t + 1)
                if not first:
                    dve.wait_ge(hqT_done, t)
                v.tensor_scalar(hq, bank(7), rs, None, ALU.mult).then_inc(hq_ready, 1)

            def features(t, first):
                dve.wait_ge(hb_done, t + 1)
                v.tensor_copy(hbar[:, :, :], bank(6).rearrange("p (k b s) -> p k b s", k=KD, b=2)[:, :, :, 0]
                              ).then_inc(hbar_ready, 1)
                dve.wait_ge(F1_ready, t + 1)
                dve.wait_ge(F2_ready, t + 1)
                if not first:
                    dve.wait_ge(feats_done, t)
                v.tensor_tensor(F3.rearrange("p a b -> p (a b)"), F1.rearrange("p a b -> p (a b)"),
                                F2.rearrange("p a b -> p (a b)"), ALU.mult).then_inc(F3_ready, 1)
                dve.wait_ge(hbar_ready, t + 1)
                if first:
                    dve.wait_ge(wqv_in, 16)
                combined(t, 0)

            def combined(t, k):
                if k > 0:
                    dve.wait_ge(wc_used, (KD - 1) * t + k)
                for h in range(2):
                    v.scalar_tensor_tensor(Wc[:, h, :], w_qv_sb[:, 3 * KD + k, :], hbar[:, k, h:h + 1],
                                           w_qv_sb[:, k, :], ALU.mult, ALU.add).then_inc(wc_ready, 1)

            def other_chunks(t, lo=1, hi=KD):
                for k in range(lo, hi):
                    combined(t, k)

            def residual_a(t):
                dve.wait_ge(feats_done, t + 1)
                dve.wait_ge(xb_ready, t + 1)
                v.tensor_tensor(x_tile(t), x_tile(t), bank(5), ALU.add).then_inc(x1_ready, 1)
                dve.wait_ge(x1_ready, t + 1)
                row_stats(t).then_inc(stats_ready, 1)

            def stage_a(t, first=False, more=True, after=False):
                if not first:
                    attended(t - 1, after)
                    features(t - 1, after)
                keep_c(t)
                if more:
                    norm_a(t + 1, False, first)
                if not first:
                    other_chunks(t - 1, 1, KD - 1)
                maxima(t, first)
                if not first:
                    other_chunks(t - 1, KD - 1)
                if not first:
                    residual_a(t - 1)
                exp_copies(t, first)
                if more:
                    queries(t + 1, False)
                batch_weights(t, first)

            norm_a(0, True)
            queries(0, True)
            keep_c(0)
            maxima(0, True)
            dve.wait_ge(rows_in, 48)
            for t in range(1, TX):
                row_stats(t).then_inc(stats_ready, 1)
            exp_copies(0, True)
            finish_norm(1, TX, 1, TX)
            dve.wait_ge(et_done, 4)
            norm_a(1, False, True)
            queries(1, False)
            batch_weights(0, True)
            stage_a(1, after=True)
            with dve.Fori(2, TX - 2) as t:
                stage_a(t)
            dve.wait_ge(x_in[0], 32)
            with dve.Fori(TX, TY) as t:
                row_stats(t).then_inc(stats_ready, 1)
            stage_a(TX - 2)
            dve.wait_ge(x_in[1], 16)
            with dve.Fori(TY, T) as t:
                row_stats(t).then_inc(stats_ready, 1)
            finish_norm(2, T + TX - 2, TX, T)
            with dve.Fori(TX - 1, T - 1) as t:
                stage_a(t)
            stage_a(T - 1, more=False)

            def norm_b(t, i, first=False):
                if not first:
                    dve.wait_ge(h1T_done, t - 1)
                normed(h1[i], t).then_inc(h1_ready, 1)

            def low_part(o, src, high):
                return v.tensor_tensor(o, src.rearrange("p (k n) -> p k n", n=P), high.bitcast(F32), ALU.subtract)

            def h1_low(t, i):
                dve.wait_ge(h1hi_ready, t + 1)
                c = slice(P * i, P * (i + 1))
                low_part(h1T[1][:, :, c], bank(i), h1T[0][:, :, c]).then_inc(h1lo_ready, 1)

            def attn_low(t, i):
                dve.wait_ge(ahi_ready, t + 1)
                low_part(attnT[i][1], bank(0), attnT[i][0]).then_inc(alo_ready, 1)

            def biased(o, src, row, j):
                w = 2 * P
                return v.tensor_tensor(o[:, 2 * j:2 * j + 2, :], src.rearrange("p (m n) -> p m n", n=w),
                                       bqkc[:, row, 2 * j:2 * j + 2].unsqueeze(2).to_broadcast([P, 2, w]), ALU.add)

            def low_weights(i):
                dve.wait_ge(w_hi_ready, i + 1)
                v.tensor_tensor(w_lo[i], w_raw[i], w_hi[i].bitcast(F32), ALU.subtract).then_inc(w_lo_ready, 1)

            finish_norm(3, 2 * T - 1, 0, T - 1)
            for i in range(2):
                norm_b(i, i, True)
            attended(T - 1, False)
            features(T - 1, False)
            low_weights(0)
            other_chunks(T - 1)
            for i in range(2):
                h1_low(i, i)
            low_weights(1)
            residual_a(T - 1)

            dve.wait_ge(rows_in, 80)
            dve.wait_ge(vbd_zero, 2)

            def queries_b(n, j, first):
                dve.wait_ge(q_done, 2 * n + j + 1)
                if not first:
                    dve.wait_ge(s_done, 2 * n)
                biased(qhT, bank(1 + j), 0, j).then_inc(q_ready, 1)

            def keys_b(n, j, first):
                dve.wait_ge(k_done, 2 * n + j + 1)
                if not first:
                    dve.wait_ge(kbd_ready, HG * 2 * n)
                biased(khT, bank(1 + j), 1, j).then_inc(k_ready, 1)

            def values(t, i, first):
                dve.wait_ge(v_done, t + 1)
                if not first:
                    dve.wait_ge(av_done, t - 1)
                for b in range(2):
                    rb = slice(S * b, S * (b + 1))
                    for e in range(2):
                        src = bank(3)[rb].rearrange("p (g e d) -> p g e d", e=2, d=HD)[:, :, e, :]
                        bias = row_a[rb].rearrange("p (g e d) -> p g e d", e=2, d=HD)[:, :, e, :]
                        v.tensor_tensor(Vbd[i][S * e:S * (e + 1), b, :, HD * e:HD * (e + 1)], src, bias,
                                        ALU.add).then_inc(vbd_ready, 1)

            def masked_scores(t, first):
                dve.wait_ge(s_done, t + 1)
                if not first:
                    dve.wait_ge(p_ready, t)
                v.scalar_tensor_tensor(sm, ps[:, 4:6, :].rearrange("p a (h j) -> p (a h) j", j=S), 1.0 / SCALE,
                                       causal[:, :].unsqueeze(1).to_broadcast([P, H, S]), ALU.mult, ALU.min
                                       ).then_inc(smask_ready, 1)
                dve.wait_ge(smask_ready, t + 1)
                v.tensor_reduce(rmax[:, :], sm, AX, ALU.max).then_inc(smax_ready, 1)
                dve.wait_ge(smax_ready, t + 1)
                v.tensor_tensor(sm, sm, rmax[:, :].unsqueeze(2).to_broadcast([P, H, S]), ALU.subtract
                                ).then_inc(ssub_ready, 1)

            def prob_sums(t):
                dve.wait_ge(p_ready, t + 1)
                v.tensor_reduce(rsum[:, :], prob, AX, ALU.add).then_inc(ssum_ready, 1)
                dve.wait_ge(ssum_ready, t + 1)
                v.reciprocal(rinv[:, :], rsum[:, :]).then_inc(rinv_ready, 1)

            def attended_b(t, first):
                dve.wait_ge(av_done, t + 1)
                dve.wait_ge(rinv_ready, t + 1)
                if not first:
                    dve.wait_ge(attnT_done, t)
                v.tensor_tensor(attn, bank(6).rearrange("p (h d) -> p h d", d=HD),
                                rinv[:, :].unsqueeze(2).to_broadcast([P, H, HD]), ALU.mult).then_inc(attn_ready, 1)

            def residual_b(t):
                dve.wait_ge(out_done, t + 1)
                dve.wait_ge(xb2_ready, t + 1)
                v.tensor_tensor(x_tile(t), x_tile(t), bank(7), ALU.add).then_inc(x2_ready, 1)
                dve.wait_ge(x2_ready, t + 1)
                row_stats(t).then_inc(stats_ready, 1)

            def stage_b(n, now, last, first=False, second=False, more=True):
                a = 2 * n
                if last:
                    masked_scores(a - 1, False)
                if now:
                    queries_b(n, 0, first)
                if last:
                    prob_sums(a - 2)
                if now:
                    queries_b(n, 1, first)
                if first:
                    low_weights(2)
                if last:
                    attended_b(a - 2, second)
                if now:
                    keys_b(n, 0, first)
                if last:
                    prob_sums(a - 1)
                    attn_low(a - 2, 0)
                if now:
                    keys_b(n, 1, first)
                if second:
                    low_weights(3)
                if last:
                    attended_b(a - 1, False)
                if more:
                    norm_b(a + 2, 0)
                    norm_b(a + 3, 1)
                elif now:
                    finish_norm(5, 2 * T + TR, 0, TR)
                if now:
                    values(a, 0, first)
                if last:
                    attn_low(a - 1, 1)
                    residual_b(a - 2)
                if now:
                    masked_scores(a, first)
                    values(a + 1, 1, first)
                if more:
                    h1_low(a + 2, 0)
                    h1_low(a + 3, 1)
                elif now:
                    for i in range(2):
                        router(i, i, True)
                if last:
                    residual_b(a - 1)

            def router(t, i, first):
                if not first:
                    dve.wait_ge(r_h2T_done, t - 1)
                normed(hs[i], t).then_inc(r_h2_ready, 1)

            def copy_logits(g):
                dve.wait_ge(lg_done, KD * (g + 1))
                v.tensor_copy(lg[:, KD * g:KD * (g + 1), :],
                              logits(g).rearrange("p (t e) -> p t e", e=P)[:, :, 0:E]).then_inc(lg_read, 1)

            def norm_c(t, i, first=False):
                if not first:
                    dve.wait_ge(h2T_done, t - 1)
                normed(h2[i], t).then_inc(h2_ready, 1)

            stage_b(0, True, False, first=True)
            finish_norm(4, 2 * T, T - 1, T)
            stage_b(1, True, True, second=True)
            with dve.Fori(2, T // 2 - 1) as n:
                stage_b(n, True, True)
            stage_b(T // 2 - 1, True, True, more=False)
            masked_scores(T - 1, False)
            for i in range(2):
                router(2 + i, i, False)
            prob_sums(T - 2)
            attended_b(T - 2, False)
            for i in range(2):
                router(4 + i, i, False)
            prob_sums(T - 1)
            attn_low(T - 2, 0)
            attended_b(T - 1, False)
            attn_low(T - 1, 1)
            for i in range(2):
                norm_c(i, i, True)
            for i in range(2):
                router(6 + i, i, False)
            residual_b(T - 2)
            router(8, 0, False)
            copy_logits(0)
            residual_b(T - 1)
            router(9, 1, False)
            for i in range(2):
                router(TR - 2 + i, i, False)
            assert TR == 12


            def to_scatter(i, t):
                def blocks(a, order):
                    return a.rearrange(f"p ({order} j) -> p c b j", j=Q, **{order[0]: NQ})

                return v.tensor_scalar(blocks(hs[i], "b c"), blocks(x_tile(t), "c b"), rstd[:, bass.ds(t, 1)],
                                       nmr[:, bass.ds(t, 1)], ALU.mult, ALU.add)

            def h2_low(p, i):
                dve.wait_ge(h2hi_ready, 2 * p + i + 1)
                c = slice(P * i, P * (i + 1))
                low_part(h2T_p[1][:, :, c], bank(7 * i), h2T_p[0][:, :, c]).then_inc(h2lo_ready, 1)

            def square(p, g):
                dve.wait_ge(relu_ready, 4 * p + g + 1)
                v.tensor_tensor(relu[g % 2], relu[g % 2], relu[g % 2], ALU.mult).then_inc(sq_ready, 1)

            def shared_low(p, g):
                dve.wait_ge(shhi_ready, 4 * p + g + 1)
                part = slice(2 * g, 2 * g + 2)
                dve.wait_ge(sq_ready, 4 * p + g + 1)
                v.tensor_tensor(shT_p[1][:, part, :].rearrange("p a b -> p (a b)"), relu[g % 2],
                                shT_p[0][:, part, :].rearrange("p a b -> p (a b)").bitcast(F32), ALU.subtract
                                ).then_inc(shlo_ready, 1)

            def residual_c(t, i):
                dve.wait_ge(shared_done, t + 1)
                v.tensor_tensor(x_tile(t), x_tile(t), bank(5 + i), ALU.add).then_inc(x3_ready, 1)

            copy_logits(1)
            for i in range(2):
                h2_low(0, i)
            finish_norm(6, 3 * T, TR, T)
            for i in range(2):
                router(TR + i, i, False)
            copy_logits(2)
            for i in range(2):
                norm_c(2 + i, i)
            square(0, 0)
            square(0, 1)
            shared_low(0, 0)
            square(0, 2)
            shared_low(0, 1)
            for i in range(2):
                h2_low(1, i)
            for i in range(2):
                router(TR + 2 + i, i, False)
            square(0, 3)
            shared_low(0, 2)
            shared_low(0, 3)
            for i in range(2):
                norm_c(4 + i, i)
            dve.wait_ge(iota_ready, 3)
            copy_logits(3)
            dve.wait_ge(lg_read, T // KD)

            def shared(p, more=True, norms=True, scatter=None):
                shared_start(p, more, norms)
                if scatter is not None:
                    scattered_norm(scatter)
                shared_rest(p)
                if scatter is not None:
                    scattered_norm(scatter + 1)

            def shared_start(p, more=True, norms=True):
                square(p, 0)
                square(p, 1)
                if more:
                    for i in range(2):
                        h2_low(p + 1, i)
                if norms:
                    for i in range(2):
                        norm_c(2 * p + 4 + i, i)

            def shared_rest(p):
                residual_c(2 * p - 2, 0)
                residual_c(2 * p - 1, 1)
                shared_low(p, 0)
                square(p, 2)
                shared_low(p, 1)
                square(p, 3)
                shared_low(p, 2)
                shared_low(p, 3)

            def tokens_T(i, n):
                dve.wait_ge(xg_in[i], 16 * NQ * (n + 1))
                v.transpose(xgT.bitcast(U32).rearrange("p c (a q) -> p a c q", q=Q),
                            xg[i].bitcast(U32).rearrange("p (a c j) -> p a c j", a=NQ, j=Q)).then_inc(xgT_ready, 1)

            def over_e(a):
                return a.unsqueeze(2).to_broadcast([P, T, E])

            def over_t(a):
                return a.unsqueeze(1).to_broadcast([P, T, E])

            step(v.tensor_reduce(v0, lg[:, :, :], AX, ALU.max))
            v.tensor_tensor(pr2, lg[:, :, :], over_e(v0), ALU.subtract).then_inc(rexp_in, 1)
            dve.wait_ge(rexp_ready, 1)
            step(v.tensor_reduce(vs, pr, AX, ALU.add))
            step(v.reciprocal(vs, vs))
            step(v.tensor_tensor(pr, pr, over_e(vs), ALU.mult))
            for probs, val, arg, onehot in ((pr, v0, e0, oh0), (pr2, v1, e1, oh1)):
                if probs is pr2:
                    step(v.scalar_tensor_tensor(pr2, oh0, -2.0, pr, ALU.mult, ALU.add))
                step(v.tensor_reduce(val, probs, AX, ALU.max))
                step(v.tensor_tensor(eq, probs, over_e(val), ALU.is_equal))
                step(v.tensor_tensor(cand, eq, over_t(iota_m8), ALU.mult))
                step(v.tensor_reduce(arg, cand, AX, ALU.min))
                step(v.tensor_tensor(onehot, over_t(iota_m8), over_e(arg), ALU.is_equal))
            step(v.tensor_tensor(vs, v0, v1, ALU.add))
            step(v.reciprocal(vs, vs))
            step(v.tensor_tensor(wt0[:, :], v0, vs, ALU.mult))
            step(v.tensor_tensor(wt1[:, :], v1, vs, ALU.mult))
            v.tensor_tensor(msk, oh0, oh1, ALU.add).then_inc(msk_ready, 1)
            for i in range(2):
                to_scatter(i, i).then_inc(hs_ready, 1)
            dve.wait_ge(prefix_done, 1)
            for i, dst in enumerate((slotm, tot)):
                v.tensor_copy(dst.rearrange("p a b -> p (a b)"), bank(6)[:, i * T * E:(i + 1) * T * E]
                              ).then_inc(prefix_read, 1)
            shared_start(1)
            dve.wait_ge(prefix_read, 2)
            src, d = tot, 1
            k = 0
            while d < T:
                dst = inc[k % 2]
                step(v.tensor_copy(dst[:, 0:d, :], src[:, 0:d, :]))
                step(v.tensor_tensor(dst[:, d:T, :], src[:, d:T, :], src[:, 0:T - d, :], ALU.add))
                src, d, k = dst, 2 * d, k + 1
            step(v.tensor_copy(cnt, src[:, T - 1, :]))
            step(v.tensor_tensor(cntcmp, cnt.unsqueeze(2).to_broadcast([P, E, T]),
                                 iota_k.unsqueeze(1).to_broadcast([P, E, T]), ALU.is_gt))
            step(v.tensor_reduce(nt, cntcmp, AX, ALU.add))
            a, b, d = nt, st0, 1
            while d < E:
                step(v.tensor_copy(b[:, 0:d], a[:, 0:d]))
                step(v.tensor_tensor(b[:, d:E], a[:, d:E], a[:, 0:E - d], ALU.add))
                a, b, d = b, (st1 if b is st0 else st0), 2 * d
            ends, first_tile = a, b
            step(v.tensor_tensor(first_tile, ends, nt, ALU.subtract))
            step(v.tensor_tensor(slotm, slotm, src, ALU.add))
            step(v.tensor_tensor(slotm, slotm, tot, ALU.subtract))
            step(v.scalar_tensor_tensor(slotm, over_t(first_tile), float(P), slotm, ALU.mult, ALU.add))
            for onehot, sf, si in ((oh0, s0f, slot_i[0]), (oh1, s1f, slot_i[1])):
                step(v.tensor_tensor(cand, slotm, onehot, ALU.mult))
                step(v.tensor_reduce(sf, cand, AX, ALU.add))
                step(v.tensor_copy(si[:, :], sf))
            step(v.tensor_tensor(gcmp, ends.unsqueeze(1).to_broadcast([P, GT, E]),
                                 iota_g.unsqueeze(2).to_broadcast([P, GT, E]), ALU.is_le))
            step(v.tensor_reduce(eg_f, gcmp, AX, ALU.add))
            step(v.tensor_scalar(eg_f, eg_f, float(E - 1), None, ALU.min))
            v.tensor_copy(eg_i[:, :], eg_f).then_inc(eg_ready, 1)

            def scattered_norm(n):
                for i in range(2):
                    t = 2 * n + i
                    if not (isinstance(n, int) and n == 0):
                        dve.wait_ge(scat[i], 32 * n)
                        to_scatter(i, t).then_inc(hs_ready, 1)
                    for k in range(2):
                        v.tensor_copy(idx[k][i][:, :], slot_i[k][:, bass.ds(t, 1)]).then_inc(idx_ready, 1)

            scattered_norm(0)
            shared_rest(1)
            scattered_norm(1)
            with dve.Fori(2, 4) as p:
                shared(p, scatter=2 * p - 2)
            shared(4, norms=False, scatter=6)
            shared_start(TA // 2 - 1, more=False, norms=False)
            dve.wait_ge(slots_zeroed, 48)
            tokens_T(0, 0)
            shared_rest(TA // 2 - 1)
            dve.wait_ge(shlo_ready, 4 * (TA // 2))
            normed(h2_l, TA).then_inc(h2_ready, 1)

            def experts(g, i, now, last, following=None):
                if following is not None:
                    dve.wait_ge(in_done, g + 1)
                    tokens_T(*following)
                if now:
                    dve.wait_ge(irelu_ready, g + 1)
                    v.tensor_tensor(inter, inter, inter, ALU.mult).then_inc(inter_ready, 1)
                if last:
                    dve.wait_ge(y_done, g)
                    v.tensor_copy(yg[1 - i], bank(3)).then_inc(y_ready, 1)

            experts(0, 0, True, False, (1, 0))
            for i in range(2):
                residual_c(TA - 2 + i, i)
            experts(1, 1, True, True, (0, 1))
            experts(2, 0, True, True, (1, 1))
            with dve.Fori(1, GP - 1) as n:
                dve.wait_ge(y_out[0], 16 * n)
                experts(2 * n + 1, 1, True, True, (0, n + 1))
                dve.wait_ge(y_out[1], 16 * n)
                experts(2 * n + 2, 0, True, True, (1, n + 1))
            dve.wait_ge(y_out[0], 16 * (GP - 1))
            experts(GT - 2, 1, True, True, (0, GP))
            dve.wait_ge(y_out[1], 16 * (GP - 1))
            experts(GT - 1, 0, True, True)
            def last_norm(u):
                dve.wait_ge(lT_done, u)
                normed(h2_l, TA + u).then_inc(h2_ready, 1)

            last_norm(1)
            dve.wait_ge(y_out[0], 16 * GP)
            experts(GT, 1, False, True)

            def mix(t, n, i):
                dve.wait_ge(y01_in[i], 32 * (n + 1))
                for k, weight, mixed in ((0, wt0, mix0_ready), (1, wt1, mix_ready)):
                    v.scalar_tensor_tensor(x_tile(t), y01[k][i], weight[:, bass.ds(t, 1)], x_tile(t), ALU.mult, ALU.add
                                           ).then_inc(mixed, 1)
                    if k == 0:
                        dve.wait_ge(mix0_ready, t + 1)

            def last_residual(u):
                dve.wait_ge(shared_done, TA + u + 1)
                v.tensor_tensor(x_tile(TA + u), x_tile(TA + u), last_bank[u % 2], ALU.add).then_inc(x3_ready, 1)

            for q in range(T - TA):
                if q >= 2:
                    last_residual(q - 2)
                if q >= 1:
                    for i in (2, 3):
                        mix(4 * (q - 1) + i, q - 1, i)
                for g in range(2):
                    dve.wait_ge(lrelu_ready, 2 * q + g + 1)
                    part = shT_l[q % 2][:, 4 * g:4 * g + 4, :].rearrange("p a b -> p (a b)")
                    v.tensor_tensor(part, part, part, ALU.mult).then_inc(lsh_ready, 1)
                if q < T - TA - 2:
                    last_norm(q + 2)
                if q == 0:
                    dve.wait_ge(x3_back, 16)
                if q == T - TA - 1:
                    dve.wait_ge(x3_ready, T - 2)
                for i in (0, 1):
                    mix(4 * q + i, q, i)
            for i in (2, 3):
                mix(T - 4 + i, T // 4 - 1, i)
            dve.wait_ge(mix_ready, T)
            for u in (T - TA - 2, T - TA - 1):
                last_residual(u)
            assert T - TA == 4 and T == 16

        @block.tensor
        def _(pe):
            mm = nc.tensor.matmul

            def transposes(dst, src):
                for k in range(KD):
                    last = nc.tensor.transpose(dst[:, P * k:P * (k + 1)], src[:, P * k:P * (k + 1)], ident[:, :])
                return last

            def rows(dst, lhsT, rhs):
                n = lhsT.shape[1]
                for k in range(n):
                    last = mm(dst, lhsT[:, k, :], rhs[:, k, :], start=(k == 0), stop=(k == n - 1))
                return last

            def normed_T(t, first):
                pe.wait_ge(hc_ready, t + 1)
                if not first:
                    pe.wait_ge(F1_ready, t)
                transposes(bank(4), hc).then_inc(hcT_done, 1)

            def batch_means(t):
                pe.wait_ge(bmat_ready, t + 1)
                pe.wait_ge(hc2_ready, t + 1)
                for k in range(KD):
                    last = mm(bank(6)[:, P * k:P * (k + 1)], hc2[:, P * k:P * (k + 1)], bmat, start=True, stop=True)
                last.then_inc(hb_done, 1)

            def attended_T(t, first):
                pe.wait_ge(hq_ready, t + 1)
                if not first:
                    pe.wait_ge(x1_ready, t)
                transposes(bank(5), hq).then_inc(hqT_done, 1)

            def similarities(t, first, lo=0, hi=KD):
                if lo > 0:
                    return similarity_chunks(t, lo, hi)
                pe.wait_ge(qT_ready, KD * (t + 1))
                if not first:
                    pe.wait_ge(et_act, 2 * t)
                    pe.wait_ge(et_dve, 2 * t)
                similarity_chunks(t, lo, hi)

            def similarity_chunks(t, lo, hi):
                for k in range(lo, hi):
                    pe.wait_ge(ctxT_in[k], 32 * (t + 1))
                    for n, (at_j, w) in enumerate(JB):
                        for h in range(2):
                            last = mm(bank(n)[S * h:S * (h + 1), 0:w], qT[:, k, S * h:S * (h + 1)],
                                      ctxT[h][:, k, at_j:at_j + w], start=(k == 0), stop=(k == KD - 1))
                    last.then_inc(sim_done, 1)

            def features(t, lo=0, hi=KD):
                if lo == 0:
                    pe.wait_ge(F1_ready, t + 1)
                    pe.wait_ge(F2_ready, t + 1)
                    pe.wait_ge(F3_ready, t + 1)
                for k in range(lo, hi):
                    mm(bank(5), F2[:, k, :], w_qv_sb[:, KD + k, :], start=(k == 0), stop=False)
                    mm(bank(5), F3[:, k, :], w_qv_sb[:, 2 * KD + k, :], start=False, stop=False)
                    pe.wait_ge(wc_ready, 2 * (KD * t + k + 1))
                    for h in range(2):
                        r = slice(S * h, S * (h + 1))
                        last = mm(bank(5)[r, :], F1[:, k, r], Wc[:, h, :], start=False, stop=(k == KD - 1))
                    if k < KD - 1:
                        last.then_inc(wc_used, 1)
                    else:
                        last.then_inc(feats_done, 1)

            def spread_max(t):
                pe.wait_ge(diag_ready, t + 1)
                mm(bank(6)[:, 0:P], ones[:, :], diag, start=True, stop=True).then_inc(mxb_done, 1)

            def exp_T(t):
                pe.wait_ge(exp_done, t + 1)
                for c in range(JC):
                    w = P if c < JM else JT
                    last = nc.tensor.transpose(bank(c // 4)[0:w, P * (c % 4):P * (c % 4 + 1)],
                                               expS[:, P * c:P * c + w], ident[:, :])
                    if c % 4 == 3 or c == JC - 1:
                        last.then_inc(et_done, 1)

            def attend(t, first):
                if not first:
                    pe.wait_ge(hq_ready, t)
                for c in range(JC):
                    w = P if c < JM else JT
                    if c == 0:
                        pe.wait_ge(et_act, 2 * t + 1)
                    if c == 4:
                        pe.wait_ge(et_dve, 2 * t + 1)
                    if c == 8:
                        pe.wait_ge(et_act, 2 * t + 2)
                    if c == 12:
                        pe.wait_ge(et_dve, 2 * t + 2)
                    if c % 3 == 0:
                        pe.wait_ge(ctxN_in[c // 3], 32 * (t + 1))
                    for h in range(2):
                        last = mm(bank(7)[S * h:S * (h + 1), :], ET[0:w, c, S * h:S * (h + 1)], ctxN[h][0:w, c, :],
                                  start=(c == 0), stop=(c == JC - 1))
                    if c % 3 == 2 or c == JC - 1:
                        last.then_inc(pv_done, 1)

            pe.wait_ge(consts_ready, 5)

            def normed_T_b(t, i):
                pe.wait_ge(h1_ready, t + 1)
                transposes(bank(i), h1[i]).then_inc(h1T_done, 1)

            def stage_a(t, now, last, first=False, second=False, more=True):
                if last:
                    batch_means(t - 1)
                    attended_T(t - 1, second)
                if not now:
                    for i in range(2):
                        normed_T_b(i, i)
                if second:
                    pe.wait_ge(wqv_in, 16)
                    features(t - 1, 0, 1)
                    similarities(t, first, 0, 1)
                    features(t - 1, 1, 2)
                    similarities(t, first, 1, KD)
                    features(t - 1, 2, KD)
                elif now and last:
                    similarities(t, first, 0, 1)
                    features(t - 1, 0, 1)
                    similarities(t, first, 1, 2)
                    features(t - 1, 1, 2)
                    similarities(t, first, 2, KD)
                    features(t - 1, 2, KD)
                elif now:
                    similarities(t, first)
                else:
                    features(t - 1)
                if now:
                    spread_max(t)
                    exp_T(t)
                    if more and not first:
                        normed_T(t + 1, False)
                    attend(t, first)
                    if first:
                        normed_T(t + 1, False)

            normed_T(0, True)
            stage_a(0, True, False, first=True)
            stage_a(1, True, True, second=True)
            with pe.Fori(2, T - 1) as t:
                stage_a(t, True, True)
            stage_a(T - 1, True, True, more=False)
            stage_a(T, False, True)

            PASSES = ((0, 0), (0, 1), (1, 0))

            def split_rows(dst, lhs, rhs, arrived=None):
                n = lhs[0].shape[1]
                for k in range(n):
                    if arrived is not None:
                        arrived(k)
                    for i, (a, b) in enumerate(PASSES):
                        last = mm(dst, lhs[a][:, k, :], rhs[b][:, k, :],
                                  start=(k + i == 0), stop=(k == n - 1 and i == 2))
                return last

            def project(dst, w, j, tokens):
                for m in range(2):
                    c = slice(P * (2 * j + m), P * (2 * j + m + 1))
                    for k in range(KD):
                        for i, (a, b) in enumerate(PASSES):
                            last = mm(dst[:, 2 * P * m:2 * P * (m + 1)], w[a][:, k, c],
                                      tokens[b][:, k, :], start=(k + i == 0), stop=(k == KD - 1 and i == 2))
                return last

            wq_p, wk_p, wv_p, wm_p = zip(w_hi, w_lo)

            def probs_T(t):
                for g in range(H // 2):
                    mt = nc.tensor.transpose(bank(6 + g // 4)[:, P * (g % 4):P * (g % 4 + 1)],
                                             prob[:, 2 * g:2 * g + 2, :].rearrange("p a b -> p (a b)"), ident[:, :])
                    if g % 4 == 3:
                        mt.then_inc(pt_done, 1)

            def attend_b(t, i):
                pe.wait_ge(pt_ready, 2 * (t + 1))
                pe.wait_ge(vbd_ready, 4 * (t + 1))
                for g in range(H // 2):
                    for b in range(2):
                        ma = mm(bank(6)[S * b:S * (b + 1), 2 * HD * g:2 * HD * (g + 1)], PT[:, g, S * b:S * (b + 1)],
                                Vbd[i][:, b, g, :], start=True, stop=True)
                ma.then_inc(av_done, 1)

            def attended_T_b(t):
                pe.wait_ge(attn_ready, t + 1)
                transposes(bank(0), attn.rearrange("p h d -> p (h d)")).then_inc(attnT_done, 1)

            def project_out(t, i):
                pe.wait_ge(ahi_ready, t + 1)
                pe.wait_ge(alo_ready, t + 1)
                split_rows(bank(7), attnT[i], wm_p).then_inc(out_done, 1)

            def scores(t, i):
                pe.wait_ge(kbd_ready, HG * (t + 1))
                for m in range(KD):
                    for b in range(2):
                        ms = mm(bank(4 + m // 2)[S * b:S * (b + 1), HG * S * (m % 2):HG * S * (m % 2 + 1)],
                                qhT[:, m, P * i + S * b:P * i + S * (b + 1)], Kbd[i][:, m, b, :], start=True, stop=True)
                ms.then_inc(s_done, 1)

            def project_v(i):
                split_rows(bank(3), [p[:, :, P * i:P * (i + 1)] for p in h1T], wv_p).then_inc(v_done, 1)

            def stage_b(n, now, last, first=False, second=False, more=True):
                a = 2 * n
                if now:
                    pe.wait_ge(h1hi_ready, a + 2)
                    pe.wait_ge(h1lo_ready, a + 2)
                    if first:
                        pe.wait_ge(w_lo_ready, 1)
                    project(bank(1), wq_p, 0, h1T).then_inc(q_done, 1)
                if last:
                    pe.wait_ge(p_ready, a - 1)
                    if not second:
                        pe.wait_ge(attn_ready, a - 2)
                        pe.wait_ge(x2_ready, a - 2)
                    probs_T(a - 2)
                if now:
                    if not first:
                        pe.wait_ge(k_ready, 2 * n)
                    project(bank(2), wq_p, 1, h1T).then_inc(q_done, 1)
                if last:
                    attend_b(a - 2, 0)
                if now:
                    pe.wait_ge(q_ready, 2 * n + 1)
                    if first:
                        pe.wait_ge(w_lo_ready, 2)
                    project(bank(1), wk_p, 0, h1T).then_inc(k_done, 1)
                if last:
                    attended_T_b(a - 2)
                    pe.wait_ge(p_ready, a)
                    probs_T(a - 1)
                if now:
                    pe.wait_ge(q_ready, 2 * n + 2)
                    project(bank(2), wk_p, 1, h1T).then_inc(k_done, 1)
                if last:
                    attend_b(a - 1, 1)
                if now:
                    if not first:
                        pe.wait_ge(vbd_ready, 4 * a)
                    else:
                        pe.wait_ge(w_lo_ready, 3)
                    project_v(0)
                if last:
                    pe.wait_ge(ahi_ready, a - 1)
                    pe.wait_ge(alo_ready, a - 1)
                    attended_T_b(a - 1)
                    if second:
                        pe.wait_ge(w_lo_ready, 4)
                    project_out(a - 2, 0)
                if now:
                    if not first:
                        pe.wait_ge(smask_ready, a)
                    scores(a, 0)
                    pe.wait_ge(vbd_ready, 4 * (a + 1))
                    project_v(1)
                if more:
                    if last:
                        pe.wait_ge(ahi_ready, a)
                        pe.wait_ge(alo_ready, a)
                    normed_T_b(a + 2, 0)
                    pe.wait_ge(k_ready, 2 * n + 1)
                    normed_T_b(a + 3, 1)
                if last:
                    pe.wait_ge(x2_ready, a - 1)
                    project_out(a - 1, 1)
                if now:
                    pe.wait_ge(smask_ready, a + 1)
                    scores(a + 1, 1)

            stage_b(0, True, False, first=True)
            stage_b(1, True, True, second=True)
            with pe.Fori(2, T // 2 - 1) as n:
                stage_b(n, True, True)
            stage_b(T // 2 - 1, True, True, more=False)

            def router_T(t, i, first, to=None):
                pe.wait_ge(r_h2_ready, t + 1)
                if not first:
                    pe.wait_ge(r_h2T_ready, t - 1)
                transposes(to or bank(1 + i), hs[i]).then_inc(r_h2T_done, 1)

            def router(t, i):
                pe.wait_ge(r_h2T_ready, t + 1)
                for k in range(KD):
                    last = mm(logits(t // KD)[:, P * (t % KD):P * (t % KD + 1)], h2Tr[i][:, k, :], wr_sb[:, k, :],
                              start=(k == 0), stop=(k == KD - 1))
                last.then_inc(lg_done, 1)

            def tokens_T_c(p, i, first=False):
                pe.wait_ge(h2_ready, 2 * p + i + 1)
                if not first:
                    pe.wait_ge(h2hi_ready, 2 * p + i - 1)
                    pe.wait_ge(h2lo_ready, 2 * p + i - 1)
                transposes(bank(7 * i), h2[i]).then_inc(h2T_done, 1)

            pe.wait_ge(k_ready, T)
            router_T(0, 0, True)
            router_T(1, 1, True)
            pe.wait_ge(p_ready, T - 1)
            pe.wait_ge(attn_ready, T - 2)
            pe.wait_ge(x2_ready, T - 2)
            probs_T(T - 2)
            pe.wait_ge(wr_in, 16)
            pe.wait_ge(vbd_ready, 4 * T)
            router(0, 0)
            router(1, 1)
            attend_b(T - 2, 0)
            router_T(2, 0, False)
            router_T(3, 1, False)
            attended_T_b(T - 2)
            pe.wait_ge(p_ready, T)
            probs_T(T - 1)
            router(2, 0)
            router(3, 1)
            attend_b(T - 1, 1)
            router_T(4, 0, False)
            router_T(5, 1, False)
            pe.wait_ge(ahi_ready, T - 1)
            pe.wait_ge(alo_ready, T - 1)
            attended_T_b(T - 1)
            project_out(T - 2, 0)
            pe.wait_ge(smask_ready, T)
            router(4, 0)
            router_T(6, 0, False)
            router(5, 1)
            pe.wait_ge(x2_ready, T - 1)
            project_out(T - 1, 1)
            router_T(7, 1, False)
            router(6, 0)
            router_T(8, 0, False)
            router(7, 1)
            router_T(9, 1, False)
            pe.wait_ge(lg_read, 1)
            router(8, 0)
            pe.wait_ge(x2_ready, T)
            for i in range(2):
                tokens_T_c(0, i, first=True)
            for i in range(2):
                router_T(TR - 2 + i, i, False)
                router(TR - 3 + i, 1 - i)
            router(TR - 1, 1)

            def shared_first(p, first=False, second=False):
                pe.wait_ge(h2hi_ready, 2 * (p + 1))
                pe.wait_ge(h2lo_ready, 2 * (p + 1))
                for g in range(KF // 2):
                    if not first:
                        pe.wait_ge(relu_ready, 4 * p + g - 3)
                    if (first or second) and g == 2:
                        pe.wait_ge(lg_read, 3 if second else 2)
                    project(group_bank(p, g), ws1_p, g, h2T_p).then_inc(sh_done, 1)

            def shared_second(p, i, first=False):
                if not first:
                    pe.wait_ge(x3_ready, 2 * p + i - 1)

                def arrived(k):
                    if k % 2 == 0:
                        pe.wait_ge(shlo_ready, 4 * p + k // 2 + 1)

                split_rows(bank(5 + i), [a[:, :, P * i:P * (i + 1)] for a in shT_p], ws2_p,
                           arrived if i == 0 else None).then_inc(shared_done, 1)

            def shared(p, second=False, more=True):
                shared_first(p)
                for i in range(2):
                    if more:
                        tokens_T_c(p + 1, i)
                for i in range(2):
                    shared_second(p - 1, i, second)

            pe.wait_ge(ws1_split, 2)
            shared_first(0, first=True)
            for i in range(2):
                tokens_T_c(1, i)
            for t in range(TR, T):
                if t == TR + 1:
                    pe.wait_ge(relu_ready, 1)
                router_T(t, t % 2, False, late_bank[t % 2])
                if t == TR + 1:
                    pe.wait_ge(relu_ready, 3)
                if t > TR:
                    router(t - 1, 1 - t % 2)
            router(T - 1, 1)
            shared_first(1, second=True)
            pe.wait_ge(msk_ready, 1)
            flat = msk.rearrange("p a b -> p (a b)")
            mm(bank(6)[:, 0:T * E], earlier[:, :], flat, start=True, stop=True)
            mm(bank(6)[:, T * E:2 * T * E], ones[:, :], flat, start=True, stop=True).then_inc(prefix_done, 1)
            for i in range(2):
                tokens_T_c(2, i)
            pe.wait_ge(ws2_split, 2)
            pe.wait_ge(lg_read, T // KD)
            shared_second(0, 0, first=True)
            pe.wait_ge(prefix_read, 2)
            shared_second(0, 1, first=True)
            with pe.Fori(2, TA // 2 - 1) as p:
                shared(p)
            shared(TA // 2 - 1, more=False)


            def expert(g):
                return pe.value_load(eg_i[0:1, bass.ds(g, 1)], min_val=0, max_val=E - 1)

            def experts(g, now, last, second=False, between=None):
                if last:
                    pe.wait_ge(inter_ready, g)
                    if not second:
                        pe.wait_ge(iT_ready, g - 1)
                    transposes(bank(1), inter).then_inc(iT_done, 1)
                if now:
                    e = expert(g)
                    pe.wait_ge(xgT_ready, g + 1)
                    for k in range(KD):
                        m1 = mm(bank(2), xgT[:, k, :], w1_sb[:, bass.ds(e, 1), k, :].rearrange("p o f -> p (o f)"),
                                start=(k == 0), stop=(k == KD - 1))
                    m1.then_inc(in_done, 1)
                if between is not None:
                    between()
                if last:
                    e = expert(g - 1)
                    if second:
                        pe.wait_ge(w2_in, 96)
                    pe.wait_ge(iT_ready, g)
                    if not second:
                        pe.wait_ge(y_ready, g - 1)
                    for k in range(KD):
                        m2 = mm(bank(3), interT[:, k, :], w2_of(e, k), start=(k == 0), stop=(k == KD - 1))
                    m2.then_inc(y_done, 1)

            def w2_of(e, k):
                at_e = e * (KD * D) + (e >= 6) * (ARENA - 6 * KD * D) + k * D
                return arena[:, bass.ds(at_e, D)]

            pe.wait_ge(w1_in, 32)
            pe.wait_ge(relu_ready, 4 * (TA // 2) - 2)
            experts(0, True, False)
            for i in range(2):
                shared_second(TA // 2 - 1, i)
            experts(1, True, True, second=True)
            with pe.Fori(2, GT - 1) as g:
                experts(g, True, True)

            def last_T(u):
                pe.wait_ge(h2_ready, TA + u + 1)
                if u > 0:
                    pe.wait_ge(lT_ready, u)
                transposes(bank(4), h2_l).then_inc(lT_done, 1)

            def last_first(u, g):
                if u > 0:
                    pe.wait_ge(lrelu_ready, 2 * u - 1 + g)
                for m in range(4 * g, 4 * g + 4):
                    for k in range(KD):
                        ms = mm(bank(5 + g)[:, P * (m % 4):P * (m % 4 + 1)], ws1_sb[:, k, P * m:P * (m + 1)],
                                h2T_l[u % 2][:, k, :], start=(k == 0), stop=(k == KD - 1))
                ms.then_inc(lsh_done, 1)

            def last_second(u):
                pe.wait_ge(lsh_ready, 2 * (u + 1))
                if u > 1:
                    pe.wait_ge(x3_ready, TA + u - 1)
                rows(last_bank[u % 2], shT_l[u % 2], ws2_sb).then_inc(shared_done, 1)

            def first_of_last():
                pe.wait_ge(wsl_in, 16 * (KD + KF))
                pe.wait_ge(x3_ready, TA)
                pe.wait_ge(lT_ready, 1)
                last_first(0, 0)

            experts(GT - 1, True, True, between=lambda: last_T(0))
            experts(GT, False, True, between=first_of_last)
            for u in range(T - TA):
                if u > 0:
                    pe.wait_ge(lT_ready, u + 1)
                    last_first(u, 0)
                if u < T - TA - 1:
                    last_T(u + 1)
                last_first(u, 1)
                if u > 0:
                    last_second(u - 1)
            last_second(T - TA - 1)


_OUT = "out"


def kernel(x, ctx_1024, L0_xattn_w_sim, L0_xattn_b_sim, L0_xattn_W_qv, L0_xattn_b_qv, L0_attn_Wq, L0_attn_bq,
           L0_attn_Wk, L0_attn_bk, L0_attn_Wv, L0_attn_bv, L0_attn_Wm, L0_attn_bm, L0_ffn_w_router,
           L0_ffn_w1_stack, L0_ffn_w2_stack, L0_ffn_ws1, L0_ffn_ws2):
    import numpy as np
    from concourse import bacc
    from concourse.bass_utils import run_bass_kernel_spmd

    def cols(v):
        return np.asarray(v).reshape(KD, P).T

    ctx = np.asarray(ctx_1024)
    main = ctx[:, :JM * P].reshape(B, P, JM, KD, P).transpose(0, 3, 4, 2, 1).reshape(B, KD, P, JM * P)
    tail = ctx[:, JM * P:].reshape(B, JT, KD, P).transpose(0, 2, 3, 1)
    w_sim = np.asarray(L0_xattn_w_sim)
    w_r = np.zeros((D, P), np.float32)
    w_r[:, :E] = np.asarray(L0_ffn_w_router).T
    ins = {
        "x": np.asarray(x).reshape(B * S, D),
        "ctx_n": ctx,
        "ctx_t": np.concatenate([main, tail], axis=-1),
        "w1": w_sim[0:D],
        "w23": np.stack([cols(w_sim[D:2 * D]), cols(w_sim[2 * D:])], axis=1),
        "b_sim": np.asarray(L0_xattn_b_sim),
        "w_qv": np.asarray(L0_xattn_W_qv),
        "b_qv": np.asarray(L0_xattn_b_qv),
        "wq": np.asarray(L0_attn_Wq), "wk": np.asarray(L0_attn_Wk),
        "wv": np.asarray(L0_attn_Wv), "wm": np.asarray(L0_attn_Wm),
        "b_qk": np.stack([cols(L0_attn_bq), cols(L0_attn_bk)], axis=1),
        "bv": np.asarray(L0_attn_bv), "bm": np.asarray(L0_attn_bm),
        "w_router": w_r,
        "w1t": np.asarray(L0_ffn_w1_stack).transpose(0, 2, 1),
        "w2t": np.asarray(L0_ffn_w2_stack).transpose(0, 2, 1),
        "ws1t": np.asarray(L0_ffn_ws1).T,
        "ws2t": np.asarray(L0_ffn_ws2).T,
    }
    ins = {n: np.ascontiguousarray(a) for n, a in ins.items()}
    nc = bacc.Bacc("TRN2", target_bir_lowering=False, num_devices=1)
    aps = [nc.dram_tensor(n, a.shape, mybir.dt.from_np(a.dtype), kind="ExternalInput").ap() for n, a in ins.items()]
    out = nc.dram_tensor(_OUT, (B * S, D), F32, kind="ExternalOutput").ap()
    perceiver_layer(nc, *aps, out)
    r = run_bass_kernel_spmd(nc, [ins], core_ids=[0])
    return r.results[0][_OUT].reshape(B, S, D)
```
